# Optimizing a Trainium2 kernel written in Bass

```python
import numpy as np
import jax
import jax.numpy as jnp

def _softmax(x, axis=-1):
    return jax.nn.softmax(x, axis=axis)

def _gelu(x):
    return jax.nn.gelu(x, approximate=True)

def _silu(x):
    return jax.nn.silu(x)

def _sigmoid(x):
    return jax.nn.sigmoid(x)

def _layernorm(x, axis=-1, eps=1e-05):
    m = jnp.mean(x, axis=axis, keepdims=True)
    v = jnp.var(x, axis=axis, keepdims=True)
    return (x - m) / jnp.sqrt(v + eps)

def _scatter_add(tgt, idx, src, axis=0):
    return tgt.at[idx].add(src)

def _segment_sum(src, seg, n):
    return jax.ops.segment_sum(src, seg, n)
kernel_name = 'mk_vit_tower_d1_tok_img768_r4_37714f'

def setup_inputs(seed: int=0):
    np.random.seed(seed)
    _w = jnp.asarray

    def _rec_inputs():
        import jax
        import jax.numpy as jnp
        _rk = jax.random.key(seed)
        x = 7.57192e-06 + 1.00007 * jax.random.normal(jax.random.fold_in(_rk, 1), (64, 3, 112, 112), jnp.float32)
        return x
    x = _rec_inputs()

    def _L0_tok_setup():
        import jax, jax.numpy as jnp
        import numpy as np
        B, C, H, W = (64, 3, 224, 224)
        P = 16
        SHIFT = P // 2
        DIM = 192
        PATCH_DIM = C * 5 * P * P
        WAVE_PATCH_DIM = PATCH_DIM // 4

        def _patch_shift(x, shift):
            xp = jnp.pad(x, ((0, 0), (0, 0), (shift, shift), (shift, shift)))
            s2 = 2 * shift
            x_lu = xp[:, :, :-s2, :-s2]
            x_ru = xp[:, :, :-s2, s2:]
            x_lb = xp[:, :, s2:, :-s2]
            x_rb = xp[:, :, s2:, s2:]
            return jnp.concatenate([x, x_lu, x_ru, x_lb, x_rb], axis=1)

        def _haar_detail_mean(x):
            b_, c_, h, w = x.shape
            r = x.reshape(b_, c_, h // 2, 2, w // 2, 2)
            a = r[:, :, :, 0, :, 0]
            bb = r[:, :, :, 0, :, 1]
            cc = r[:, :, :, 1, :, 0]
            dd = r[:, :, :, 1, :, 1]
            return (3.0 * a - bb - cc - dd) / 6.0

        def _patchify(x, p):
            b_, c_, hh, ww = x.shape
            h, w = (hh // p, ww // p)
            x = x.reshape(b_, c_, h, p, w, p)
            x = x.transpose(0, 2, 4, 3, 5, 1)
            return x.reshape(b_, h * w, p * p * c_)

        def _layernorm(x, g, b, eps=1e-05):
            m = jnp.mean(x, axis=-1, keepdims=True)
            v = jnp.mean(jnp.square(x - m), axis=-1, keepdims=True)
            return (x - m) * jax.lax.rsqrt(v + eps) * g + b
        key = jax.random.key(seed)
        ks = jax.random.split(key, 7)
        x = jax.random.normal(ks[0], (B, C, H, W), dtype=jnp.float32)
        ln1_g = jnp.ones((PATCH_DIM,), jnp.float32)
        ln1_b = jnp.zeros((PATCH_DIM,), jnp.float32)
        w1 = jax.random.normal(ks[1], (PATCH_DIM, DIM), jnp.float32) * 0.02
        b1 = jnp.zeros((DIM,), jnp.float32)
        ln2_g = jnp.ones((WAVE_PATCH_DIM,), jnp.float32)
        ln2_b = jnp.zeros((WAVE_PATCH_DIM,), jnp.float32)
        w2 = jax.random.normal(ks[2], (WAVE_PATCH_DIM, DIM), jnp.float32) * 0.02
        b2 = jnp.zeros((DIM,), jnp.float32)
        return {'x': x, 'ln1_g': ln1_g, 'ln1_b': ln1_b, 'w1': w1, 'b1': b1, 'ln2_g': ln2_g, 'ln2_b': ln2_b, 'w2': w2, 'b2': b2}
    _L0_tok_all = _L0_tok_setup()
    _L0_tok_in = {k: v for k, v in _L0_tok_all.items() if k in ('ln1_g', 'ln1_b', 'w1', 'b1', 'ln2_g', 'ln2_b', 'w2', 'b2')}
    del _L0_tok_all

    def _L0_attn_setup():
        import jax, jax.numpy as jnp
        import numpy as np
        P, L, H = (3, 4, 6)
        EPS = 1e-05

        def _layernorm(x, g, b):
            mu = jnp.mean(x, -1, keepdims=True)
            var = jnp.mean((x - mu) ** 2, -1, keepdims=True)
            return (x - mu) * jax.lax.rsqrt(var + EPS) * g + b

        def _mha_windows(q, k, v, inw, inb, mow, mob):
            B, W, Pw, D = q.shape
            hd = D // H
            wq, wk, wv = (inw[:D], inw[D:2 * D], inw[2 * D:])
            bq, bk, bv = (inb[:D], inb[D:2 * D], inb[2 * D:])
            qp = (q @ wq.T + bq).reshape(B, W, Pw, H, hd)
            kp = (k @ wk.T + bk).reshape(B, W, Pw, H, hd)
            vp = (v @ wv.T + bv).reshape(B, W, Pw, H, hd)
            scores = jnp.einsum('bwqhd,bwkhd->bwhqk', qp, kp) / jnp.sqrt(jnp.float32(hd))
            attn = jax.nn.softmax(scores, axis=-1)
            o = jnp.einsum('bwhqk,bwkhd->bwqhd', attn, vp).reshape(B, W, Pw, D)
            return o @ mow.T + mob
        key = jax.random.key(seed)
        B, T, D = (8, 1024, 192)
        ks = jax.random.split(key, 12)
        s = 0.02
        w = lambda k, shape: jax.random.normal(k, shape, jnp.float32) * s
        z = lambda n: jnp.zeros((n,), jnp.float32)
        return {'x': jax.random.normal(ks[0], (B, T, D), jnp.float32), 'ln_g': jnp.ones((D,), jnp.float32), 'ln_b': z(D), 'qw': w(ks[1], (D, D)), 'qb': z(D), 'kw': w(ks[2], (D, D)), 'kb': z(D), 'vw': w(ks[3], (D, D)), 'vb': z(D), 'inw': w(ks[4], (3 * D, D)), 'inb': z(3 * D), 'mow': w(ks[5], (D, D)), 'mob': z(D), 'ow': w(ks[6], (D, D)), 'ob': z(D)}
    _L0_attn_all = _L0_attn_setup()
    _L0_attn_in = {k: v for k, v in _L0_attn_all.items() if k in ('ln_g', 'ln_b', 'qw', 'qb', 'kw', 'kb', 'vw', 'vb', 'inw', 'inb', 'mow', 'mob', 'ow', 'ob')}
    del _L0_attn_all

    def _L0_ffn_setup():
        import jax, jax.numpy as jnp
        import numpy as np
        B, N, D, H, E, HID, TOPK = (8, 197, 192, 12, 8, 768, 2)

        def _layernorm(x, w, b, eps=1e-05):
            mu = jnp.mean(x, axis=-1, keepdims=True)
            var = jnp.mean((x - mu) ** 2, axis=-1, keepdims=True)
            return (x - mu) * jax.lax.rsqrt(var + eps) * w + b
        key = jax.random.key(seed)
        ks = jax.random.split(key, 8)
        s = 0.02
        return {'x': jax.random.normal(ks[0], (B, N, D), jnp.float32), 'norm1_w': jnp.ones((D,), jnp.float32), 'norm1_b': jnp.zeros((D,), jnp.float32), 'qkv_w': jax.random.normal(ks[1], (3 * D, D), jnp.float32) * s, 'qkv_b': jnp.zeros((3 * D,), jnp.float32), 'proj_w': jax.random.normal(ks[2], (D, D), jnp.float32) * s, 'proj_b': jnp.zeros((D,), jnp.float32), 'norm2_w': jnp.ones((D,), jnp.float32), 'norm2_b': jnp.zeros((D,), jnp.float32), 'w_gate': jax.random.normal(ks[3], (D, E), jnp.float32) * s, 'W1': jax.random.normal(ks[4], (E, D, HID), jnp.float32) * s, 'b1': jnp.zeros((E, HID), jnp.float32), 'W2': jax.random.normal(ks[5], (E, HID, D), jnp.float32) * s, 'b2': jnp.zeros((E, D), jnp.float32)}
    _L0_ffn_all = _L0_ffn_setup()
    _L0_ffn_in = {k: v for k, v in _L0_ffn_all.items() if k in ('norm1_w', 'norm1_b', 'qkv_w', 'qkv_b', 'proj_w', 'proj_b', 'norm2_w', 'norm2_b', 'w_gate', 'W1', 'b1', 'W2', 'b2')}
    del _L0_ffn_all
    return {'x': x, 'L0_tok_ln1_g': _L0_tok_in['ln1_g'], 'L0_tok_ln1_b': _L0_tok_in['ln1_b'], 'L0_tok_w1': _L0_tok_in['w1'], 'L0_tok_b1': _L0_tok_in['b1'], 'L0_tok_ln2_g': _L0_tok_in['ln2_g'], 'L0_tok_ln2_b': _L0_tok_in['ln2_b'], 'L0_tok_w2': _L0_tok_in['w2'], 'L0_tok_b2': _L0_tok_in['b2'], 'L0_attn_ln_g': _L0_attn_in['ln_g'], 'L0_attn_ln_b': _L0_attn_in['ln_b'], 'L0_attn_qw': _L0_attn_in['qw'], 'L0_attn_qb': _L0_attn_in['qb'], 'L0_attn_kw': _L0_attn_in['kw'], 'L0_attn_kb': _L0_attn_in['kb'], 'L0_attn_vw': _L0_attn_in['vw'], 'L0_attn_vb': _L0_attn_in['vb'], 'L0_attn_inw': _L0_attn_in['inw'], 'L0_attn_inb': _L0_attn_in['inb'], 'L0_attn_mow': _L0_attn_in['mow'], 'L0_attn_mob': _L0_attn_in['mob'], 'L0_attn_ow': _L0_attn_in['ow'], 'L0_attn_ob': _L0_attn_in['ob'], 'L0_ffn_norm1_w': _L0_ffn_in['norm1_w'], 'L0_ffn_norm1_b': _L0_ffn_in['norm1_b'], 'L0_ffn_qkv_w': _L0_ffn_in['qkv_w'], 'L0_ffn_qkv_b': _L0_ffn_in['qkv_b'], 'L0_ffn_proj_w': _L0_ffn_in['proj_w'], 'L0_ffn_proj_b': _L0_ffn_in['proj_b'], 'L0_ffn_norm2_w': _L0_ffn_in['norm2_w'], 'L0_ffn_norm2_b': _L0_ffn_in['norm2_b'], 'L0_ffn_w_gate': _L0_ffn_in['w_gate'], 'L0_ffn_W1': _L0_ffn_in['W1'], 'L0_ffn_b1': _L0_ffn_in['b1'], 'L0_ffn_W2': _L0_ffn_in['W2'], 'L0_ffn_b2': _L0_ffn_in['b2']}

def reference(x, L0_tok_ln1_g, L0_tok_ln1_b, L0_tok_w1, L0_tok_b1, L0_tok_ln2_g, L0_tok_ln2_b, L0_tok_w2, L0_tok_b2, L0_attn_ln_g, L0_attn_ln_b, L0_attn_qw, L0_attn_qb, L0_attn_kw, L0_attn_kb, L0_attn_vw, L0_attn_vb, L0_attn_inw, L0_attn_inb, L0_attn_mow, L0_attn_mob, L0_attn_ow, L0_attn_ob, L0_ffn_norm1_w, L0_ffn_norm1_b, L0_ffn_qkv_w, L0_ffn_qkv_b, L0_ffn_proj_w, L0_ffn_proj_b, L0_ffn_norm2_w, L0_ffn_norm2_b, L0_ffn_w_gate, L0_ffn_W1, L0_ffn_b1, L0_ffn_W2, L0_ffn_b2):
    import jax
    import jax.numpy as jnp

    def _L0_tok_ref(x, ln1_g, ln1_b, w1, b1, ln2_g, ln2_b, w2, b2):
        import jax, jax.numpy as jnp
        import numpy as np
        B, C, H, W = (64, 3, 224, 224)
        P = 16
        SHIFT = P // 2
        DIM = 192
        PATCH_DIM = C * 5 * P * P
        WAVE_PATCH_DIM = PATCH_DIM // 4

        def _patch_shift(x, shift):
            xp = jnp.pad(x, ((0, 0), (0, 0), (shift, shift), (shift, shift)))
            s2 = 2 * shift
            x_lu = xp[:, :, :-s2, :-s2]
            x_ru = xp[:, :, :-s2, s2:]
            x_lb = xp[:, :, s2:, :-s2]
            x_rb = xp[:, :, s2:, s2:]
            return jnp.concatenate([x, x_lu, x_ru, x_lb, x_rb], axis=1)

        def _haar_detail_mean(x):
            b_, c_, h, w = x.shape
            r = x.reshape(b_, c_, h // 2, 2, w // 2, 2)
            a = r[:, :, :, 0, :, 0]
            bb = r[:, :, :, 0, :, 1]
            cc = r[:, :, :, 1, :, 0]
            dd = r[:, :, :, 1, :, 1]
            return (3.0 * a - bb - cc - dd) / 6.0

        def _patchify(x, p):
            b_, c_, hh, ww = x.shape
            h, w = (hh // p, ww // p)
            x = x.reshape(b_, c_, h, p, w, p)
            x = x.transpose(0, 2, 4, 3, 5, 1)
            return x.reshape(b_, h * w, p * p * c_)

        def _layernorm(x, g, b, eps=1e-05):
            m = jnp.mean(x, axis=-1, keepdims=True)
            v = jnp.mean(jnp.square(x - m), axis=-1, keepdims=True)
            return (x - m) * jax.lax.rsqrt(v + eps) * g + b
        out5 = _patch_shift(x, SHIFT)
        waves = _haar_detail_mean(out5)
        tok = _layernorm(_patchify(out5, P), ln1_g, ln1_b) @ w1 + b1
        wtok = _layernorm(_patchify(waves, P // 2), ln2_g, ln2_b) @ w2 + b2
        return tok + wtok

    def _L0_attn_ref(x, ln_g, ln_b, qw, qb, kw, kb, vw, vb, inw, inb, mow, mob, ow, ob):
        import jax, jax.numpy as jnp
        import numpy as np
        P, L, H = (3, 4, 6)
        EPS = 1e-05

        def _layernorm(x, g, b):
            mu = jnp.mean(x, -1, keepdims=True)
            var = jnp.mean((x - mu) ** 2, -1, keepdims=True)
            return (x - mu) * jax.lax.rsqrt(var + EPS) * g + b

        def _mha_windows(q, k, v, inw, inb, mow, mob):
            B, W, Pw, D = q.shape
            hd = D // H
            wq, wk, wv = (inw[:D], inw[D:2 * D], inw[2 * D:])
            bq, bk, bv = (inb[:D], inb[D:2 * D], inb[2 * D:])
            qp = (q @ wq.T + bq).reshape(B, W, Pw, H, hd)
            kp = (k @ wk.T + bk).reshape(B, W, Pw, H, hd)
            vp = (v @ wv.T + bv).reshape(B, W, Pw, H, hd)
            scores = jnp.einsum('bwqhd,bwkhd->bwhqk', qp, kp) / jnp.sqrt(jnp.float32(hd))
            attn = jax.nn.softmax(scores, axis=-1)
            o = jnp.einsum('bwhqk,bwkhd->bwqhd', attn, vp).reshape(B, W, Pw, D)
            return o @ mow.T + mob
        B, T, D = x.shape
        xn = _layernorm(x, ln_g, ln_b)
        Q = xn @ qw.T + qb
        K = xn @ kw.T + kb
        V = xn @ vw.T + vb
        acc = jnp.zeros_like(x)
        for kk in range(L):
            scale = P ** kk
            if T < scale:
                continue
            Lp = T // scale
            pool = lambda z: z[:, :Lp * scale].reshape(B, Lp, scale, D).mean(axis=2)
            pQ, pK, pV = (pool(Q), pool(K), pool(V))
            W = Lp // P
            if W == 0:
                continue
            win = lambda z: z[:, :W * P].reshape(B, W, P, D)
            o = _mha_windows(win(pQ), win(pK), win(pV), inw, inb, mow, mob)
            so = o.reshape(B, W * P, D)
            idx = jnp.arange(T) * (W * P) // T
            up = so[:, idx]
            acc = acc + jax.nn.gelu(up, approximate=False)
        out = acc @ ow.T + ob
        return x + out

    def _L0_ffn_ref(x, norm1_w, norm1_b, qkv_w, qkv_b, proj_w, proj_b, norm2_w, norm2_b, w_gate, W1, b1, W2, b2):
        import jax, jax.numpy as jnp
        import numpy as np
        B, N, D, H, E, HID, TOPK = (8, 197, 192, 12, 8, 768, 2)

        def _layernorm(x, w, b, eps=1e-05):
            mu = jnp.mean(x, axis=-1, keepdims=True)
            var = jnp.mean((x - mu) ** 2, axis=-1, keepdims=True)
            return (x - mu) * jax.lax.rsqrt(var + eps) * w + b
        Bx, Nx, C = x.shape
        hd = C // H
        scale = hd ** (-0.5)
        xn = _layernorm(x, norm1_w, norm1_b)
        qkv = (xn @ qkv_w.T + qkv_b).reshape(Bx, Nx, 3, H, hd).transpose(2, 0, 3, 1, 4)
        q, k, v = (qkv[0], qkv[1], qkv[2])
        attn = jax.nn.softmax(jnp.einsum('bhqd,bhkd->bhqk', q, k) * scale, axis=-1)
        o = jnp.einsum('bhqk,bhkd->bqhd', attn, v).reshape(Bx, Nx, C)
        x = x + (o @ proj_w.T + proj_b)
        xn2 = _layernorm(x, norm2_w, norm2_b).reshape(-1, C)
        T = xn2.shape[0]
        logits = xn2 @ w_gate
        top_vals, top_idx = jax.lax.top_k(logits, TOPK)
        gates = jax.nn.softmax(top_vals, axis=-1)
        gates_full = jnp.zeros((T, E), xn2.dtype).at[jnp.arange(T)[:, None], top_idx].add(gates)

        def body(acc, p):
            w1, bb1, w2, bb2, g = p
            h = jax.nn.gelu(xn2 @ w1 + bb1, approximate=False)
            return (acc + g[:, None] * (h @ w2 + bb2), None)
        moe_out, _ = jax.lax.scan(body, jnp.zeros_like(xn2), (W1, b1, W2, b2, gates_full.T))
        return x + moe_out.reshape(Bx, Nx, C)
    h = _L0_tok_ref(x, L0_tok_ln1_g, L0_tok_ln1_b, L0_tok_w1, L0_tok_b1, L0_tok_ln2_g, L0_tok_ln2_b, L0_tok_w2, L0_tok_b2)
    h = h + _L0_attn_ref(_layernorm(h, axis=-1), L0_attn_ln_g, L0_attn_ln_b, L0_attn_qw, L0_attn_qb, L0_attn_kw, L0_attn_kb, L0_attn_vw, L0_attn_vb, L0_attn_inw, L0_attn_inb, L0_attn_mow, L0_attn_mob, L0_attn_ow, L0_attn_ob)
    h = h + _L0_ffn_ref(_layernorm(h, axis=-1), L0_ffn_norm1_w, L0_ffn_norm1_b, L0_ffn_qkv_w, L0_ffn_qkv_b, L0_ffn_proj_w, L0_ffn_proj_b, L0_ffn_norm2_w, L0_ffn_norm2_b, L0_ffn_w_gate, L0_ffn_W1, L0_ffn_b1, L0_ffn_W2, L0_ffn_b2)
    return h

_drawn_inputs = setup_inputs


def setup_inputs(seed=0):
    import zlib

    import numpy as np

    out = dict(_drawn_inputs(seed))
    spreads = {'L0_tok_ln1_g': (1.0, 0.2),
     'L0_tok_ln1_b': (0.0, 0.1),
     'L0_tok_b1': (0.0, 0.1),
     'L0_tok_ln2_g': (1.0, 0.2),
     'L0_tok_ln2_b': (0.0, 0.1),
     'L0_tok_b2': (0.0, 0.1),
     'L0_attn_ln_g': (1.0, 0.6),
     'L0_attn_ln_b': (0.0, 0.8),
     'L0_attn_qb': (0.0, 0.8),
     'L0_attn_kb': (0.0, 2.0),
     'L0_attn_vb': (0.0, 0.8),
     'L0_attn_inb': (0.0, 0.8),
     'L0_attn_mob': (0.0, 0.442),
     'L0_attn_ob': (0.0, 0.8),
     'L0_ffn_norm1_w': (1.0, 0.6),
     'L0_ffn_norm1_b': (0.0, 0.8),
     'L0_ffn_qkv_b': (0.0, 0.8),
     'L0_ffn_proj_b': (0.0, 0.8),
     'L0_ffn_norm2_w': (1.0, 0.6),
     'L0_ffn_norm2_b': (0.0, 0.8),
     'L0_ffn_b1': (0.0, 2.0),
     'L0_ffn_b2': (0.0, 2.0)}
    factors = {'L0_attn_qw': 8.0,
     'L0_attn_kw': 8.0,
     'L0_attn_vw': 8.0,
     'L0_attn_inw': 8.0,
     'L0_attn_mow': 8.0,
     'L0_attn_ow': 2.881,
     'L0_ffn_qkv_w': 8.0,
     'L0_ffn_proj_w': 5.343,
     'L0_ffn_W1': 3.191,
     'L0_ffn_W2': 2.947}
    for name, (base, spread) in spreads.items():
        noise = np.random.default_rng([zlib.crc32(name.encode()), seed]).standard_normal(out[name].shape)
        drawn = base * np.exp(spread * noise) if base else spread * noise
        out[name] = jnp.asarray(drawn.astype(out[name].dtype))
    for name, factor in factors.items():
        out[name] = (out[name] * factor).astype(out[name].dtype)
    return out
```

```python
from contextlib import ExitStack

import concourse.bass as bass
from concourse import mybir

F32 = mybir.dt.float32
BF16 = mybir.dt.bfloat16
I32 = mybir.dt.int32
U32 = mybir.dt.uint32
ALU = mybir.AluOpType
ACT = mybir.ActivationFunctionType
X = mybir.AxisListType.X

P = 128
B = 64
G = 7
T = G * G
D = 192
H2 = D // 2
EPS = 1e-5
CELL = 16
NC = 8
CH = 3
KC = CELL * CELL * CH // P
PATCH = 5 * CELL * CELL * CH
WAVE = PATCH // 4
NA = 7 * B
NB = 6 * B
WH = 6
WHD = D // WH
NWT = 11
POS = 66
FRONT = 3
AH = 12
AHD = D // AH
NP = B // 2
E = 8
HID = 768
HC = HID // P
ROWS = 256
NT = (2 * B * T + E * (ROWS - 1)) // ROWS
R = B * T + ROWS
NROW = E * R + ROWS
FAR = 1 << 20
TT = (T + 1) // 2
UNIT_AT = [(1, 2, 16), (2, 1, 16), (3, 0, 32)]

C_ID = 0
C_MK = C_ID + P
C_INV = C_MK + 10
C_SIX = C_INV + 4
C_KM = C_SIX + 2
C_NH = C_KM + 6
C_EPS = C_NH + 2
C_EI = C_EPS + 2
C_VAL = C_EI + E
C_ER = C_VAL + 2
C_J = C_ER + E
C_L8 = C_J + NT
C_TRI = C_L8 + E * E
NCONST = C_TRI + P


def run_slots(eng, n, depth, slot, unroll=2):
    def at(t, k, u, full):
        def item(lag):
            if not full and not 0 <= t - lag < n:
                return None
            return (t - lag, (u - lag) % unroll, k + (u - lag) // unroll)
        return item

    first = -(-(depth - 1) // unroll)
    last = n // unroll
    for t in range(first * unroll):
        slot(at(t, t // unroll, t % unroll, False))
    with eng.Fori(first, last) as k:
        for u in range(unroll):
            slot(at(unroll * k + u, k, u, True))
    for t in range(last * unroll, n + depth - 1):
        slot(at(t, t // unroll, t % unroll, False))


class Windows:

    def __init__(self, nc, ctx, sb, sem, A, const, ones, xnT, wqkv, colg, mowT, owT, hall, base_d, h2_d, pe1, pt1, pp, s):
        self.nc, self.const, self.xnT, self.wqkv, self.colg, self.mowT, self.owT = nc, const, xnT, wqkv, colg, mowT, owT
        self.hall, self.base_d, self.h2_d, self.pe1, self.pt1, self.pp, self.s = hall, base_d, h2_d, pe1, pt1, pp, s
        own = ExitStack()
        self.stg = sb("stg", [H2 + 1, 2, 2, 3, P], to=own)
        self.qkv = sb("qkv", [P, 2, 3, 3 * D], to=own)
        self.prod = sb("prod", [P, 3, 3, D], to=own)
        self.sc = sb("sc", [P, 3, 3, WH], to=own)
        self.ex = sb("ex", [P, 3, 3, WH], to=own)
        self.mx = sb("mx", [P, 3, WH], to=own)
        self.ob = sb("ob", [P, 3, D], to=own)
        self.oT = sb("oT", [H2, 2, 3 * P], to=own)
        self.gall = sb("gall", [H2, 2, POS, B], to=own)
        self.g12 = sb("g12", [H2, 2, 15, B], to=own)
        self.accT = sb("accT", [H2, 2, 2 * TT, B], to=own)
        self.st3 = sb("st3", [H2 + 1, 2, 2, P], to=own)
        own.close()
        self.stg_set, self.stg_used, self.qkv_mm, self.qkv_out, self.qkv_free = sem("stg_set"), sem("stg_used"), sem("qkv_mm"), sem("qkv_out"), sem("qkv_free")
        self.w_sc, self.w_ex, self.w_o, self.o_T, self.o_out = sem("w_sc"), sem("w_ex"), sem("w_o"), sem("o_T"), sem("o_out")
        self.so_mm, self.so_out, self.pooled, self.gelu_set, self.acc_set = sem("so_mm"), sem("so_out"), sem("pooled"), sem("gelu_set"), sem("acc_set")
        self.st3_set, self.st3_used, self.mix_mm, self.h2_set = sem("st3_set"), sem("st3_used"), sem("mix_mm"), sem("h2_set")

    def gpsimd(self, pool):
        nc, xnT, stg = self.nc, self.xnT, self.stg
        pool.wait_ge(self.s["xh_out"], 25)
        pool.wait_ge(self.pooled, 1)

        def slot(item):
            if (it := item(0)):
                i, u, _ = it
                pool.wait_ge(self.stg_used, i + 1)
                for h in range(2):
                    src = xnT[:, h, bass.ds(FRONT + 6 * i, 6), :].rearrange("p (w s) b -> p s w b", s=3)
                    last = nc.gpsimd.tensor_copy(stg[0:H2, u, h].rearrange("p s (w b) -> p s w b", w=2), src)
                last.then_inc(self.stg_set, 1)
        run_slots(pool, NWT, 1, slot)

        def mix(item):
            i, u, _ = item(0)
            pool.wait_ge(self.st3_used, i)
            nc.gpsimd.tensor_copy(self.st3[0:H2, u], self.accT[:, :, bass.ds(2 * i, 2), :].rearrange("p h t b -> p h (t b)")).then_inc(self.st3_set, 1)
        pool.wait_ge(self.acc_set, 1)
        run_slots(pool, TT, 1, mix)

    def tensor(self, pe):
        nc, mm = self.nc, self.nc.tensor.matmul
        pe1, pt1, pp, stg = self.pe1, self.pt1, self.pp, self.stg
        ident = self.const[:, C_ID:C_ID + P]
        pe.wait_ge(self.s["tok_free"], 28)
        pe.wait_ge(self.s["xh_out"], 25)

        def qkv(i, u, s):
            pe.wait_ge(self.qkv_out, 3 * i + s + 1)
            b = 2 * ((u + s) % 2)
            for n in range(2):
                mm(pe1[:, b + n, 0:288], stg[0:H2, u, 0, s], self.wqkv[0:H2, 0, n * 288:(n + 1) * 288], start=True, stop=False)
                last = mm(pe1[:, b + n, 0:288], stg[:, u, 1, s], self.wqkv[:, 1, n * 288:(n + 1) * 288], start=False, stop=True)
            last.then_inc(self.qkv_mm, 1)
            if s == 2:
                pe.drain().then_inc(self.stg_used, 1)

        def slot(item):
            a, c = item(0), item(2)
            if c:
                i, u, _ = c
                pe.wait_ge(self.w_o, i + 1)
                pe.wait_ge(self.o_out, i)
                for h in range(2):
                    for s in range(3):
                        last = nc.tensor.transpose(pt1[0:H2, h, s * P:(s + 1) * P], self.ob[:, s, h * H2:(h + 1) * H2], ident)
                last.then_inc(self.o_T, 1)
            if a:
                i, u, _ = a
                pe.wait_ge(self.stg_set, i + 1)
                qkv(i, u, 0)
            if c:
                i, u, _ = c
                pe.wait_ge(self.o_out, i + 1)
                pe.wait_ge(self.so_out, i)
                for m in range(2):
                    for h in range(2):
                        last = mm(pp[0:H2, m, 0:3 * P], self.mowT[:, h, m * H2:(m + 1) * H2], self.oT[:, h], start=(h == 0), stop=(h == 1))
                last.then_inc(self.so_mm, 1)
            if a:
                i, u, _ = a
                qkv(i, u, 1)
                qkv(i, u, 2)
        run_slots(pe, NWT, 3, slot)

        pe.wait_ge(self.so_out, NWT)

        def mix(item):
            i, u, _ = item(0)
            pe.wait_ge(self.st3_set, i + 1)
            pe.wait_ge(self.h2_set, i)
            mm(pp[:, u, 0:D], self.st3[0:H2, u, 0], self.owT[0:H2, 0], start=True, stop=False)
            mm(pp[:, u, 0:D], self.st3[:, u, 1], self.owT[:, 1], start=False, stop=True).then_inc(self.mix_mm, 1)
            pe.drain().then_inc(self.st3_used, 1)
        run_slots(pe, TT, 1, mix)

    def scalar(self, act):
        nc = self.nc
        pe1, pt1, pp, gall, colg = self.pe1, self.pt1, self.pp, self.gall, self.colg

        def qkv(i, u, s):
            if s == 0:
                act.wait_ge(self.qkv_free, i + 1)
            act.wait_ge(self.qkv_mm, 3 * i + s + 1)
            b = 2 * ((u + s) % 2)
            nc.scalar.activation(self.qkv[:, u, s].rearrange("p (n f) -> p n f", n=2), pe1[:, b:b + 2, 0:288], ACT.Copy).then_inc(self.qkv_out, 1)

        def slot(item):
            a, b, c = item(0), item(1), item(2)
            if c:
                i, u, _ = c
                act.wait_ge(self.o_T, i + 1)
                nc.scalar.activation(self.oT[:], pt1[0:H2, :, 0:3 * P], ACT.Copy).then_inc(self.o_out, 1)
            if a:
                qkv(*a[:2], 0)
            if c:
                i, u, _ = c
                act.wait_ge(self.so_mm, i + 1)
                for m in range(2):
                    dst = gall[:, m, bass.ds(6 * i, 6), :].rearrange("p (w s) b -> p s w b", s=3)
                    last = nc.scalar.activation(dst, pp[0:H2, m, 0:3 * P].rearrange("p (s w b) -> p s w b", s=3, w=2),
                                                ACT.Identity, bias=colg[:, m, 2:3])
                last.then_inc(self.so_out, 1)
            if a:
                qkv(*a[:2], 1)
            if b:
                i, u, _ = b
                act.wait_ge(self.w_sc, i + 1)
                nc.scalar.activation(self.ex[:], self.sc[:], ACT.Exp, scale=WHD ** -0.5).then_inc(self.w_ex, 1)
            if a:
                qkv(*a[:2], 2)
        run_slots(act, NWT, 3, slot)
        act.drain()
        for a, b in ((48, 66), (0, 16), (16, 32), (32, 48)):
            nc.scalar.activation(gall[:, :, a:b].rearrange("p h t b -> p h (t b)"), gall[:, :, a:b].rearrange("p h t b -> p h (t b)"), ACT.Gelu).then_inc(self.gelu_set, 1)

    def vector(self, dve):
        nc, v, xnT, qkv, prod = self.nc, self.nc.vector, self.xnT, self.qkv, self.prod
        dve.wait_ge(self.s["xh_out"], 25)
        for src, dst, n in ((FRONT, FRONT + 48, 15), (FRONT + 48, FRONT + 63, 3)):
            out = xnT[:, :, dst:dst + n, :]
            x = [xnT[:, :, src + q:src + q + 3 * n - 2:3, :] for q in range(3)]
            v.tensor_tensor(out, x[0], x[1], ALU.add)
            dve.drain()
            v.tensor_tensor(out, out, x[2], ALU.add)
            dve.drain()
            v.tensor_scalar(out, out, 1 / 3, None, ALU.mult)
            dve.drain()
        v.memset(self.stg[H2:H2 + 1].rearrange("p u h s n -> p (u h s n)"), 1.0).then_inc(self.stg_used, 2)
        v.memset(self.st3[H2:H2 + 1].rearrange("p u h n -> p (u h n)"), 1.0).then_inc(self.st3_used, 1)
        v.memset(self.mx[0:1, 0, 0:1], 0.0).then_inc(self.qkv_free, 2)
        v.memset(self.mx[0:1, 0, 1:2], 0.0).then_inc(self.qkv_out, 2)
        dve.drain().then_inc(self.pooled, 1)

        def slot(item):
            if not (it := item(1)):
                return
            i, u, _ = it
            dve.drain()
            dve.wait_ge(self.qkv_out, 3 * i + 5)
            for a in range(3):
                v.tensor_tensor(prod[:, a], qkv[:, u, a:a + 1, 0:D].to_broadcast([P, 3, D]), qkv[:, u, :, D:2 * D], ALU.mult)
            dve.drain()
            sc, ex, mx = self.sc, self.ex, self.mx
            v.tensor_reduce(sc[:].rearrange("p a b h -> p (a b h)"), prod[:].rearrange("p a b (h d) -> p (a b h) d", h=WH), X, ALU.add)
            dve.drain()
            v.tensor_reduce(mx[:], sc[:].rearrange("p a b h -> p a h b"), X, ALU.max)
            dve.drain()
            v.tensor_tensor(sc[:], sc[:], mx[:].unsqueeze(2).to_broadcast([P, 3, 3, WH]), ALU.subtract).then_inc(self.w_sc, 1)
            dve.wait_ge(self.w_ex, i + 1)
            v.tensor_reduce(mx[:], ex[:].rearrange("p a b h -> p a h b"), X, ALU.add)
            dve.drain()
            v.reciprocal(mx[:], mx[:])
            dve.drain()
            v.tensor_tensor(ex[:], ex[:], mx[:].unsqueeze(2).to_broadcast([P, 3, 3, WH]), ALU.mult)
            dve.drain()
            for a in range(3):
                v.tensor_tensor(prod[:, a].rearrange("p b (h d) -> p b h d", h=WH),
                                qkv[:, u, :, 2 * D:3 * D].rearrange("p b (h d) -> p b h d", h=WH),
                                ex[:, a].unsqueeze(3).to_broadcast([P, 3, WH, WHD]), ALU.mult)
            dve.drain().then_inc(self.qkv_free, 1)
            dve.wait_ge(self.o_T, i)
            v.tensor_tensor(self.ob[:], prod[:, :, 0], prod[:, :, 1], ALU.add)
            dve.drain()
            v.tensor_tensor(self.ob[:], self.ob[:], prod[:, :, 2], ALU.add).then_inc(self.w_o, 1)
        run_slots(dve, NWT, 3, slot)

        gall, g12, acc = self.gall, self.g12, self.accT
        dve.wait_ge(self.s["base_ld"], 16)
        dve.wait_ge(self.gelu_set, 1)
        for h in range(2):
            v.tensor_tensor(g12[:, h].rearrange("p (v u) b -> p v u b", u=5), gall[:, h, 48:63].rearrange("p (v u) b -> p v u b", u=5),
                            gall[:, h, 63:66].unsqueeze(2).to_broadcast([H2, 3, 5, B]), ALU.add)
        dve.drain()
        starts = [next(t for t in range(T) if t * 15 // T == u) for u in range(15)] + [2 * TT]
        for u in range(15):
            a, b = starts[u], starts[u + 1]
            dve.wait_ge(self.gelu_set, 2 + min((b - 2) // 16, 2))
            for lo, hi, src in (((0, 1, 0), (1, b, 0)) if u == 0 else ((a, b, a - 1),)):
                n = hi - lo
                v.tensor_tensor(acc[:, :, lo:hi], gall[:, :, src:src + n], g12[:, :, u:u + 1].to_broadcast([H2, 2, n, B]), ALU.add)
        dve.drain().then_inc(self.acc_set, 1)

        def mix(item):
            i, u, _ = item(0)
            dve.wait_ge(self.mix_mm, i + 1)
            row = self.hall[:, bass.ds(i, 1), :].rearrange("p o d -> p (o d)")
            v.tensor_tensor(row, row, self.pp[:, u, 0:D], ALU.add).then_inc(self.h2_set, 1)
        run_slots(dve, TT, 1, mix)

    def sync(self, sp, bs_st, last):
        for n in range(4):
            sp.wait_ge(bs_st[n], 112)
        sp.dma_start(self.hall[:, 0:TT], self.base_d.rearrange("(i t) b d -> (t b) i d", t=2)).then_inc(self.s["base_ld"], 16)
        for g in range(5):
            sp.wait_ge(self.h2_set, 5 * g + 5)
            for q in range(2):
                dst = self.h2_d.rearrange("b (i t) d -> t b i d", t=2)[q, :, 5 * g:5 * g + 5, :]
                sp.dma_start(dst, self.hall[q * B:(q + 1) * B, 5 * g:5 * g + 5]).then_inc(self.s["h2_st"], 16)
        sp.wait_ge(self.s["h2_st"], 160)


class Heads:

    def __init__(self, nc, ctx, sb, sem, A, const, ones, colg, hall, h2_d, xs_d, ys_d, out, pe1, pt1, pp, s):
        self.nc, self.A, self.const, self.ones, self.colg, self.hall = nc, A, const, ones, colg, hall
        self.h2_d, self.xs_d, self.ys_d, self.out = h2_d, xs_d, ys_d, out
        self.pe1, self.pt1, self.pp, self.s = pe1, pt1, pp, s
        self.wqk = sb("wqk", [H2 + 1, 2, 3 * D])
        self.wproj = sb("wproj", [H2 + 1, 2, D])
        self.wgate = sb("wgate", [H2, 2, E])
        self.n2 = sb("n2", [P, 2, D])
        self.gates = sb("gates", [P, NP, 2])
        self.dest = sb("dest", [P, NP, 2], I32)
        self.meta = sb("meta", [1, 3, NT], I32)
        own = ExitStack()
        self.x2 = sb("x2", [P, NP, D], to=own)
        self.st = sb("st", [P, 32], to=own)
        self.bn = sb("bn", [P, 2, 6], to=own)
        self.xh2 = sb("xh2", [P, D], to=own)
        self.xT2 = sb("xT2", [H2 + 1, 2, P], to=own)
        self.qT = sb("qT", [H2, 2, P], to=own)
        self.kbd = sb("kbd", [H2, 2, 2, 6, T], to=own)
        self.vbd = sb("vbd", [P, 2, 6, 2 * (AHD + 1)], to=own)
        self.pm = sb("pm", [P, AH, B], to=own)
        self.mx2 = sb("mx2", [P, AH], to=own)
        self.pT = sb("pT", [P, 6, P], to=own)
        self.on = sb("on", [P, D], to=own)
        self.onT = sb("onT", [H2 + 1, 2, P], to=own)
        self.xn = sb("xn", [P, D], to=own)
        self.xsrc = sb("xsrc", [P, D], to=own)
        self.xnT2 = sb("xnT2", [H2, 2, P], to=own)
        self.lg = sb("lg", [P, E], to=own)
        self.m8 = sb("m8", [P, E], to=own)
        self.i8 = sb("i8", [P, E], U32, to=own)
        self.idx = sb("idx", [P, 2], to=own)
        self.oh = sb("oh", [P, 2, E], to=own)
        self.ohs = sb("ohs", [P, E], to=own)
        self.acc = sb("acc", [P, E], to=own)
        self.eg = sb("eg", [P, 1], to=own)
        self.t8 = sb("t8", [P, 3, E], to=own)
        self.df = sb("df", [P, 2], to=own)
        self.dst = sb("dst", [P, 2], I32, to=own)
        self.zero = sb("zero", [P, 2, D], to=own)
        self.mf = sb("mf", [P, 6, NT * E], to=own)
        self.nf = sb("nf", [P, 5, E], to=own)
        self.idxs = sb("idxs", [P, NP, 2], to=own)
        self.offs = sb("offs", [P, NP * 2, E], to=own)
        own.close()
        ex = ExitStack()
        self.w1 = sb("ew1", [H2, 2, 2, HID], to=ex)
        self.b1 = sb("eb1", [P, 2, HC], to=ex)
        self.w2 = sb("ew2", [P, 2, HC, D], to=ex)
        self.b2 = sb("eb2", [P, 2, D], to=ex)
        self.xs = sb("xs", [P, 2, 2, D], to=ex)
        self.xsT = sb("xsT", [H2, 2, ROWS], to=ex)
        self.hT = sb("hT", [P, 2, HC, ROWS], to=ex)
        self.ys = sb("ys", [P, 2, 2, D], to=ex)
        ex.close()
        self.yg = sb("yg", [P, 4, 2, D], to=ctx)
        self.di = sb("di", [P, 4, 2], I32)
        self.a_var, self.a_r, self.a_x, self.a_T, self.a_xT = sem("a_var"), sem("a_r"), sem("a_x"), sem("a_T"), sem("a_xT")
        self.a_qkv, self.a_qv, self.a_k, self.b_s, self.b_sub = sem("a_qkv"), sem("a_qv"), sem("a_k"), sem("b_s"), sem("b_sub")
        self.b_ex, self.b_pT, self.b_pTo, self.b_pv, self.b_on = sem("b_ex"), sem("b_pT"), sem("b_pTo"), sem("b_pv"), sem("b_on")
        self.c_T, self.c_out, self.c_proj, self.c_var, self.c_r = sem("c_T"), sem("c_out"), sem("c_proj"), sem("c_var"), sem("c_r")
        self.c_xn, self.c_nT, self.d_out, self.d_lg, self.d_oh = sem("c_xn"), sem("c_nT"), sem("d_out"), sem("d_lg"), sem("d_oh")
        self.d_rank, self.d_eg, self.d_dst, self.scat, self.d_src = sem("d_rank"), sem("d_eg"), sem("d_dst"), sem("scat"), sem("d_src")
        self.h_ld, self.hw_ld, self.init, self.tot, self.meta_set = sem("h_ld"), sem("hw_ld"), sem("init"), sem("tot"), sem("meta_set")
        self.zero_st, self.e_T, self.e_xT, self.e_h, self.e_g = sem("zero_st"), sem("e_T"), sem("e_xT"), sem("e_h"), sem("e_g")
        self.e_y, self.e_out, self.e_free, self.y_free, self.g_free = sem("e_y"), sem("e_out"), sem("e_free"), sem("y_free"), sem("g_free")
        self.o_st = sem("o_st")
        self.e_w = [sem("e_w0"), sem("e_w1")]
        self.e_w2 = [sem("e_w20"), sem("e_w21")]
        self.e_st = [sem("e_st0"), sem("e_st1")]
        self.gat = [sem(f"gat{n}") for n in range(4)]

    def gpsimd(self, pool):
        nc, st, g = self.nc, self.st, self.nc.gpsimd
        pool.wait_ge(self.init, 2)
        eps, mhalf = self.const[:, C_EPS:C_EPS + 1], self.const[:, C_NH:C_NH + 1]

        def slot(item):
            a, c, d = item(0), item(2), item(3)
            if a:
                i = a[0]
                pool.wait_ge(self.a_var, i + 1)
                g.tensor_tensor(st[:, 2:3], st[:, 1:2], eps, ALU.add)
                pool.drain()
                g.tensor_tensor(st[:, 2:3], st[:, 2:3], mhalf, ALU.pow)
                pool.drain()
                g.tensor_tensor(st[:, 3:4], st[:, 1:2], st[:, 2:3], ALU.mult)
                pool.drain()
                g.tensor_tensor(st[:, 3:4], st[:, 3:4], st[:, 2:3], ALU.mult)
                pool.drain()
                g.tensor_tensor(st[:, 3:4], st[:, 3:4], eps, ALU.add)
                pool.drain()
                g.tensor_tensor(st[:, 3:4], st[:, 3:4], mhalf, ALU.pow).then_inc(self.a_r, 1)
            if c:
                i = c[0]
                pool.wait_ge(self.c_var, i + 1)
                g.tensor_tensor(st[:, 8:9], st[:, 7:8], eps, ALU.add)
                pool.drain()
                g.tensor_tensor(st[:, 8:9], st[:, 8:9], mhalf, ALU.pow).then_inc(self.c_r, 1)
            if d:
                i = d[0]
                pool.wait_ge(self.d_src, i + 1)
                pool.wait_ge(self.d_dst, i + 1)
                at = self.dest[:, bass.ds(i, 1), :].rearrange("p o k -> p (o k)")
                g.tensor_copy(self.dst[:], at)
                pool.drain()
                for k in range(2):
                    g.indirect_dma_start(self.xs_d[:, :], bass.IndirectOffsetOnAxis(ap=self.dst[:, k:k + 1], axis=0),
                                         self.xsrc[:], None, bounds_check=E * R - 1, oob_is_err=False).then_inc(self.scat, 16)
        run_slots(pool, NP, 4, slot, unroll=1)

        pool.wait_ge(self.meta_set, 1)
        pool.wait_ge(self.e_st[0], NT // 2 * 16)
        pool.wait_ge(self.e_st[1], NT // 2 * 16)

        def gather(item):
            i, u, _ = item(0)
            pool.wait_ge(self.g_free, i + 1)
            at = self.dest[:, bass.ds(i, 1), :].rearrange("p o k -> p (o k)")
            g.tensor_copy(self.di[:, u], at)
            pool.drain()
            for k in range(2):
                g.indirect_dma_start(self.yg[:, u, k], None, self.ys_d[:, :],
                                     bass.IndirectOffsetOnAxis(ap=self.di[:, u, k:k + 1], axis=0),
                                     bounds_check=NT * ROWS - 1, oob_is_err=False).then_inc(self.gat[u], 16)
        run_slots(pool, NP, 1, gather, unroll=4)

    def vector(self, dve):
        nc, v, st, const, hall, x2 = self.nc, self.nc.vector, self.st, self.const, self.hall, self.x2
        pe1, pp = self.pe1, self.pp
        dve.wait_ge(self.s["h2_st"], 160)
        dve.drain()
        v.memset(self.pm[:], 0.0)
        v.memset(self.vbd[:], 0.0)
        dve.drain()
        v.memset(self.vbd[0:T, :, :, AHD:AHD + 1], 1.0)
        v.memset(self.vbd[B:B + T, :, :, 2 * AHD + 1:2 * AHD + 2], 1.0)
        v.memset(self.acc[:], 0.0)
        v.memset(self.xT2[H2:H2 + 1, 1], 1.0)
        v.memset(self.onT[H2:H2 + 1, 1], 1.0)
        v.memset(self.zero[:], 0.0)
        v.memset(hall[:], 0.0)
        dve.drain().then_inc(self.init, 2)
        dve.drain().then_inc(self.e_free, 2)
        dve.drain().then_inc(self.y_free, 2)
        dve.drain().then_inc(self.e_g, 3)
        dve.wait_ge(self.h_ld, 64)
        dve.wait_ge(self.hw_ld, 16 * 7)

        def row(t, i):
            return t[:, bass.ds(i, 1), :].rearrange("p o d -> p (o d)")

        def stats(src, k, bnk):
            v.bn_stats(self.bn[:, bnk], src)
            dve.drain()
            v.bn_aggr(st[:, k:k + 2], self.bn[:, bnk])

        def slot(item):
            a, b, c, d = (item(k) for k in range(4))
            dve.drain()
            if a:
                i = a[0]
                stats(row(hall, i), 0, 0)
                dve.drain().then_inc(self.a_var, 1)
            if b:
                i = b[0]
                dve.wait_ge(self.b_s, i + 1)
                sc = pe1[:, 0:2, 0:6 * T].rearrange("p n (h k) -> p n h k", h=6)
                v.tensor_reduce(self.mx2[:].rearrange("p (n h) -> p n h", n=2), sc, X, ALU.max)
                dve.drain()
                v.tensor_tensor(self.pm[:].rearrange("p (n h) k -> p n h k", n=2)[:, :, :, 0:T], sc,
                                self.mx2[:].rearrange("p (n h) -> p n h", n=2).unsqueeze(3).to_broadcast([P, 2, 6, T]),
                                ALU.subtract).then_inc(self.b_sub, 1)
            if a:
                i = a[0]
                dve.wait_ge(self.a_r, i + 1)
                v.tensor_scalar(row(x2, i), row(hall, i), st[:, 0:1], st[:, 2:3], ALU.subtract, ALU.mult)
                dve.drain()
                v.tensor_scalar(self.xh2[:], row(x2, i), st[:, 3:4], None, ALU.mult).then_inc(self.a_x, 1)
            if d:
                i = d[0]
                dve.wait_ge(self.d_lg, i + 1)
                v.tensor_copy(self.lg[:], pe1[:, 3, 256:256 + E])
                dve.drain()
                v.max(self.m8[:], self.lg[:])
                dve.drain()
                v.max_index(self.i8[:], self.m8[:], self.lg[:])
                v.tensor_tensor(st[:, 12:13], self.m8[:, 1:2], self.m8[:, 0:1], ALU.subtract)
                dve.drain()
                v.tensor_copy(self.idx[:], self.i8[:, 0:2])
                v.tensor_copy(row(self.idxs, i), self.i8[:, 0:2])
                dve.drain()
                for k in range(2):
                    v.tensor_scalar(self.oh[:, k], const[:, C_EI:C_EI + E], self.idx[:, k:k + 1], const[:, C_VAL:C_VAL + 1],
                                    ALU.is_equal, ALU.mult)
                dve.drain()
                v.tensor_tensor(self.ohs[:], self.oh[:, 0], self.oh[:, 1], ALU.add)
                dve.drain().then_inc(self.d_oh, 1)
            if c:
                i = c[0]
                dve.wait_ge(self.c_proj, i + 1)
                v.tensor_tensor(row(x2, i), row(x2, i), pe1[:, 2, 256:256 + D], ALU.add)
                dve.drain()
                stats(row(x2, i), 6, 1)
                dve.drain().then_inc(self.c_var, 1)
                v.tensor_tensor(row(hall, i), row(hall, i), row(x2, i), ALU.add)
            if d:
                i = d[0]
                dve.wait_ge(self.d_rank, i + 1)
                t = self.t8
                v.tensor_tensor(t[:, 0], pe1[:, 3, 256:256 + E], const[:, C_ER:C_ER + E], ALU.add)
                v.tensor_tensor(self.acc[:], self.acc[:], self.ohs[:], ALU.add)
                dve.drain()
                v.tensor_tensor(t[:, 1:3], self.oh[:], t[:, 0:1].to_broadcast([P, 2, E]), ALU.mult)
                dve.drain()
                v.tensor_reduce(self.df[:], t[:, 1:3], X, ALU.add)
                dve.drain()
                v.tensor_scalar(self.df[:], self.df[:], const[:, C_VAL + 1:C_VAL + 2], None, ALU.add)
                dve.drain()
                v.tensor_copy(row(self.dest, i), self.df[:]).then_inc(self.d_dst, 1)
                dve.wait_ge(self.d_eg, i + 1)
                v.tensor_scalar(st[:, 13:14], self.eg[:], 1.0, None, ALU.add)
                dve.drain()
                gt = self.gates
                v.reciprocal(gt[:, bass.ds(i, 1), 0:1].rearrange("p o k -> p (o k)"), st[:, 13:14])
                dve.drain()
                v.tensor_tensor(gt[:, bass.ds(i, 1), 1:2].rearrange("p o k -> p (o k)"), gt[:, bass.ds(i, 1), 0:1].rearrange("p o k -> p (o k)"), self.eg[:], ALU.mult)
            if c:
                i = c[0]
                dve.wait_ge(self.c_r, i + 1)
                dve.wait_ge(self.d_src, i)
                v.tensor_scalar(self.xn[:], row(x2, i), st[:, 6:7], st[:, 8:9], ALU.subtract, ALU.mult)
                dve.drain()
                v.tensor_tensor(self.xn[:], self.xn[:], self.n2[:, 0], ALU.mult)
                dve.drain()
                v.tensor_tensor(self.xn[:], self.xn[:], self.n2[:, 1], ALU.add).then_inc(self.c_xn, 1)
            if b:
                i = b[0]
                dve.wait_ge(self.b_pv, i + 1)
                o = pe1[:, 1, 0:AH * (AHD + 1)].rearrange("p (h d) -> p h d", h=AH)
                v.reciprocal(self.mx2[:], o[:, :, AHD:AHD + 1].rearrange("p h o -> p (h o)"))
                dve.drain()
                dve.wait_ge(self.c_T, i)
                v.tensor_tensor(self.on[:].rearrange("p (h d) -> p h d", h=AH), o[:, :, 0:AHD],
                                self.mx2[:].unsqueeze(2).to_broadcast([P, AH, AHD]), ALU.mult).then_inc(self.b_on, 1)
            if a:
                i = a[0]
                dve.wait_ge(self.a_qkv, i + 1)
                for m in range(2):
                    for h in range(2):
                        k = pp[0:H2, 1, h * P + m * B:h * P + m * B + T].unsqueeze(1).to_broadcast([H2, 6, T])
                        last = v.tensor_tensor(self.kbd[:, m, h], k, const[0:H2, C_KM:C_KM + 6].unsqueeze(2).to_broadcast([H2, 6, T]), ALU.mult)
                last.then_inc(self.a_k, 1)
        run_slots(dve, NP, 4, slot, unroll=1)

        dve.drain().then_inc(self.tot, 1)
        dve.wait_ge(self.tot, 2)
        nf, mf = self.nf, self.mf
        cnt, cnt256, nt, cum, off = (nf[:, n] for n in range(5))
        ge = mf[:, 0].rearrange("p (j e) -> p j e", e=E)
        js, ers = const[:, C_J:C_J + NT], const[:, C_ER:C_ER + E]
        v.tensor_copy(cnt, pe1[:, 3, 0:E])
        dve.drain()
        v.tensor_scalar(cnt256, cnt, 1 / ROWS, None, ALU.mult)
        dve.drain()
        ng = NT // 2
        gt = mf[:, 1, 0:E * ng].rearrange("p (e m) -> p e m", e=E)
        v.tensor_tensor(gt, cnt256.unsqueeze(2).to_broadcast([P, E, ng]), js[:, 0:ng].unsqueeze(1).to_broadcast([P, E, ng]), ALU.is_gt)
        dve.drain()
        v.tensor_reduce(nt, gt, X, ALU.add)
        dve.drain()
        pr = mf[:, 2, 0:E * E].rearrange("p (e f) -> p e f", e=E)
        v.tensor_tensor(pr, const[:, C_L8:C_L8 + E * E].rearrange("p (e f) -> p e f", e=E), nt.unsqueeze(1).to_broadcast([P, E, E]), ALU.mult)
        dve.drain()
        v.tensor_reduce(cum, pr, X, ALU.add)
        dve.drain()
        v.tensor_tensor(ge, js.unsqueeze(2).to_broadcast([P, NT, E]), cum.unsqueeze(1).to_broadcast([P, NT, E]), ALU.is_ge)
        dve.drain()
        te, tl = mf[:, 3, 0:NT], mf[:, 4, 0:NT]
        v.tensor_reduce(te, ge, X, ALU.add)
        v.tensor_tensor(mf[:, 5].rearrange("p (j e) -> p j e", e=E), ge, nt.unsqueeze(1).to_broadcast([P, NT, E]), ALU.mult)
        v.tensor_tensor(off, cum, nt, ALU.subtract)
        dve.drain()
        v.tensor_reduce(tl, mf[:, 5].rearrange("p (j e) -> p j e", e=E), X, ALU.add)
        v.scalar_tensor_tensor(off, off, float(ROWS), ers, ALU.mult, ALU.subtract)
        v.tensor_tensor(self.offs[:], self.idxs[:].rearrange("p i k -> p (i k)").unsqueeze(2).to_broadcast([P, 2 * NP, E]),
                        const[:, C_EI:C_EI + E].unsqueeze(1).to_broadcast([P, 2 * NP, E]), ALU.is_equal)
        dve.drain()
        v.tensor_tensor(tl, js, tl, ALU.subtract)
        v.tensor_tensor(self.offs[:], self.offs[:], off.unsqueeze(1).to_broadcast([P, 2 * NP, E]), ALU.mult)
        dve.drain()
        v.tensor_scalar(tl, tl, float(ROWS), None, ALU.mult)
        v.tensor_reduce(self.idxs[:].rearrange("p i k -> p (i k)"), self.offs[:], X, ALU.add)
        dve.drain()
        v.scalar_tensor_tensor(tl, te, float(R), tl, ALU.mult, ALU.add)
        dve.drain()
        v.tensor_scalar(self.meta[:, 0], te[0:1], float(E - 1), None, ALU.min)
        v.tensor_scalar(self.meta[:, 1], tl[0:1], float(E * R), None, ALU.min)
        v.tensor_tensor(self.meta[:, 2, 0:E], cnt[0:1], ers[0:1], ALU.add)
        dve.wait_ge(self.scat, 32 * NP)
        v.tensor_tensor(self.dest[:], self.dest[:], self.idxs[:], ALU.add)
        dve.drain().then_inc(self.meta_set, 1)

        def expert(item):
            if not (c := item(3)):
                return
            i, u, h = c
            dve.wait_ge(self.e_y, i + 1)
            dve.wait_ge(self.e_w2[u], 32 * h + 32)
            dve.wait_ge(self.e_st[u], 16 * h)
            v.tensor_tensor(self.ys[:, u], pp[:, u, 0:2 * D].rearrange("p (k d) -> p k d", k=2),
                            self.b2[:, u:u + 1, :].to_broadcast([P, 2, D]), ALU.add).then_inc(self.e_out, 1)
            dve.drain().then_inc(self.y_free, 1)
        run_slots(dve, NT, 5, expert)

        v.memset(self.yg[:], 0.0).then_inc(self.g_free, 4)

        def combine(item):
            i, u, h = item(0)
            dve.wait_ge(self.gat[u], 32 * h + 32)
            for k in range(2):
                v.scalar_tensor_tensor(row(hall, i), self.yg[:, u, k], self.gates[:, bass.ds(i, 1), k:k + 1].rearrange("p o k -> p (o k)"),
                                       row(hall, i), ALU.mult, ALU.add)
                dve.drain()
            dve.drain().then_inc(self.g_free, 1)
        run_slots(dve, NP, 1, combine, unroll=4)

    def scalar(self, act):
        nc, f, pe1, pt1, pp, colg = self.nc, self.nc.scalar.activation, self.pe1, self.pt1, self.pp, self.colg
        act.wait_ge(self.init, 2)

        def slot(item):
            a, b, c, d = (item(k) for k in range(4))
            if d:
                i = d[0]
                act.wait_ge(self.c_nT, i + 1)
                f(self.xnT2[:], pe1[0:H2, 3, 0:2 * P].rearrange("p (h n) -> p h n", h=2), ACT.Copy).then_inc(self.d_out, 1)
            if c:
                i = c[0]
                act.wait_ge(self.c_T, i + 1)
                f(self.onT[0:H2], pe1[0:H2, 2, 0:2 * P].rearrange("p (h n) -> p h n", h=2), ACT.Copy).then_inc(self.c_out, 1)
            if b:
                i = b[0]
                act.wait_ge(self.b_sub, i + 1)
                f(self.pm[:, :, 0:T], self.pm[:, :, 0:T], ACT.Exp, scale=AHD ** -0.5).then_inc(self.b_ex, 1)
            if d:
                i = d[0]
                act.wait_ge(self.scat, 32 * i)
                f(self.xsrc[:], self.xn[:], ACT.Copy).then_inc(self.d_src, 1)
                act.wait_ge(self.d_oh, i + 1)
                f(self.eg[:], self.st[:, 12:13], ACT.Exp).then_inc(self.d_eg, 1)
            if a:
                i = a[0]
                act.wait_ge(self.a_T, i + 1)
                for h in range(2):
                    last = f(self.xT2[0:H2, h], pt1[0:H2, 0, h * P:(h + 1) * P], ACT.Identity, bias=colg[:, h, 4:5], scale=colg[:, h, 3:4])
                last.then_inc(self.a_xT, 1)
            if b:
                i = b[0]
                act.wait_ge(self.b_pT, i + 1)
                f(self.pT[:, 0:4].rearrange("p h n -> p (h n)"), pe1[:, 0], ACT.Copy)
                f(self.pT[:, 4:6].rearrange("p h n -> p (h n)"), pe1[:, 1, 0:2 * P], ACT.Copy).then_inc(self.b_pTo, 1)
            if a:
                i = a[0]
                act.wait_ge(self.a_qkv, i + 1)
                act.wait_ge(self.b_pv, i)
                f(self.qT[:], pp[0:H2, 0, 0:2 * P].rearrange("p (h n) -> p h n", h=2), ACT.Copy)
                for m in range(2):
                    for e in range(2):
                        src = pp[m * B:m * B + T, 0, 256:256 + D].rearrange("p (h e d) -> p h e d", e=2, d=AHD)[:, :, e]
                        last = f(self.vbd[e * B:e * B + T, m, :, e * (AHD + 1):e * (AHD + 1) + AHD], src, ACT.Copy)
                last.then_inc(self.a_qv, 1)
        run_slots(act, NP, 4, slot, unroll=1)

        def expert(item):
            if not (b := item(1)):
                return
            i, u, h = b
            act.wait_ge(self.e_T, i + 1)
            f(self.xsT[:].rearrange("p h n -> p (h n)"), pt1[0:H2, 0, :], ACT.Copy).then_inc(self.e_xT, 1)

        def hidden(item):
            if not (b := item(2)):
                return
            i, u, h = b
            act.wait_ge(self.y_free, i + 1)
            for c in range(HC):
                if c % 2 == 0:
                    act.wait_ge(self.e_h, 3 * i + c // 2 + 1)
                last = f(self.hT[:, u, c], pe1[:, c // 2, (c % 2) * ROWS:(c % 2 + 1) * ROWS], ACT.Gelu, bias=self.b1[:, u, c:c + 1])
                if c % 2:
                    last.then_inc(self.e_g, 1)
            act.drain().then_inc(self.e_free, 1)

        def both(item):
            hidden(item)
            expert(item)
        run_slots(act, NT, 5, both)

    def tensor(self, pe):
        nc, mm, T_, pe1, pt1, pp = self.nc, self.nc.tensor.matmul, self.nc.tensor.transpose, self.pe1, self.pt1, self.pp
        ident, const = self.const[:, C_ID:C_ID + P], self.const
        pe.wait_ge(self.init, 2)
        pe.wait_ge(self.hw_ld, 16 * 7)

        def slot(item):
            a, b, c, d = (item(k) for k in range(4))
            if b:
                i = b[0]
                pe.wait_ge(self.a_qv, i + 1)
                pe.wait_ge(self.a_k, i + 1)
                pe.wait_ge(self.b_on, i)
                for m in range(2):
                    for h in range(2):
                        last = mm(pe1[m * B:(m + 1) * B, h, 0:6 * T], self.qT[:, h, m * B:(m + 1) * B],
                                  self.kbd[:, m, h].rearrange("p h k -> p (h k)"), start=True, stop=True)
                last.then_inc(self.b_s, 1)
            if c:
                i = c[0]
                pe.wait_ge(self.b_on, i + 1)
                pe.wait_ge(self.c_var, i)
                for h in range(2):
                    last = T_(pe1[0:H2, 2, h * P:(h + 1) * P], self.on[:, h * H2:(h + 1) * H2], ident)
                last.then_inc(self.c_T, 1)
            if d:
                i = d[0]
                pe.wait_ge(self.d_out, i + 1)
                for h in range(2):
                    last = mm(pe1[:, 3, 256:256 + E], self.xnT2[:, h], self.wgate[:, h], start=(h == 0), stop=(h == 1))
                last.then_inc(self.d_lg, 1)
            if c:
                i = c[0]
                pe.wait_ge(self.c_out, i + 1)
                mm(pe1[:, 2, 256:256 + D], self.onT[0:H2, 0], self.wproj[0:H2, 0], start=True, stop=False)
                mm(pe1[:, 2, 256:256 + D], self.onT[:, 1], self.wproj[:, 1], start=False, stop=True).then_inc(self.c_proj, 1)
            if a:
                i = a[0]
                pe.wait_ge(self.a_x, i + 1)
                pe.wait_ge(self.a_xT, i)
                for h in range(2):
                    last = T_(pt1[0:H2, 0, h * P:(h + 1) * P], self.xh2[:, h * H2:(h + 1) * H2], ident)
                last.then_inc(self.a_T, 1)
            if b:
                i = b[0]
                pe.wait_ge(self.b_ex, i + 1)
                for n in range(6):
                    last = T_(pe1[:, n // 4, (n % 4) * P:(n % 4 + 1) * P], self.pm[:, 2 * n:2 * n + 2].rearrange("p h k -> p (h k)"), ident)
                last.then_inc(self.b_pT, 1)
            if d:
                i = d[0]
                pe.wait_ge(self.d_oh, i + 1)
                mm(pe1[:, 3, 256:256 + E], self.ones[:], self.acc[:], start=True, stop=False)
                mm(pe1[:, 3, 256:256 + E], const[:, C_TRI:C_TRI + P], self.ohs[:], start=False, stop=True).then_inc(self.d_rank, 1)
            if a:
                i = a[0]
                pe.wait_ge(self.a_xT, i + 1)
                pe.wait_ge(self.a_qv, i)
                pe.wait_ge(self.a_k, i)
                for g, bank, c0 in ((0, 0, 0), (1, 1, 0)):
                    for m in range(2):
                        for h in range(2):
                            rows = H2 + h
                            mm(pp[0:H2, bank, m * P:(m + 1) * P], self.wqk[0:rows, h, g * D + m * H2:g * D + (m + 1) * H2],
                               self.xT2[0:rows, h], start=(h == 0), stop=(h == 1))
                for h in range(2):
                    last = mm(pp[:, 0, 256:256 + D], self.xT2[0:H2 + h, h], self.wqk[0:H2 + h, h, 2 * D:3 * D], start=(h == 0), stop=(h == 1))
                last.then_inc(self.a_qkv, 1)
            if b:
                i = b[0]
                pe.wait_ge(self.b_pTo, i + 1)
                w = 2 * (AHD + 1)
                for m in range(2):
                    for n in range(6):
                        last = mm(pe1[m * B:(m + 1) * B, 1, n * w:(n + 1) * w], self.pT[:, n, m * B:(m + 1) * B], self.vbd[:, m, n], start=True, stop=True)
                last.then_inc(self.b_pv, 1)
            if c:
                i = c[0]
                pe.wait_ge(self.c_xn, i + 1)
                pe.wait_ge(self.d_dst, i)
                for h in range(2):
                    last = T_(pe1[0:H2, 3, h * P:(h + 1) * P], self.xn[:, h * H2:(h + 1) * H2], ident)
                last.then_inc(self.c_nT, 1)
        run_slots(pe, NP, 4, slot, unroll=1)
        pe.wait_ge(self.tot, 1)
        mm(pe1[:, 3, 0:E], self.ones[:], self.acc[:], start=True, stop=True).then_inc(self.tot, 1)
        pe.wait_ge(self.meta_set, 1)

        def expert(item):
            if (b := item(2)):
                i, u, h = b
                pe.wait_ge(self.e_xT, i + 1)
                for n in range(HC):
                    if n % 2 == 0:
                        pe.wait_ge(self.e_g, 3 * i + n // 2 + 1)
                    for m in range(2):
                        last = mm(pe1[:, n // 2, (n % 2) * ROWS:(n % 2 + 1) * ROWS], self.w1[:, u, m, n * P:(n + 1) * P], self.xsT[:, m], start=(m == 0), stop=(m == 1))
                    if n % 2:
                        last.then_inc(self.e_h, 1)
            if (a := item(1)):
                i, u, h = a
                pe.wait_ge(self.e_w[u], 48 * h + 48)
                pe.wait_ge(self.e_xT, i)
                for k in range(2):
                    for n in range(2):
                        last = T_(pt1[0:H2, 0, n * ROWS + k * P:n * ROWS + (k + 1) * P], self.xs[:, u, k, n * H2:(n + 1) * H2], ident)
                last.then_inc(self.e_T, 1)
            if (c := item(3)):
                i, u, h = c
                pe.wait_ge(self.e_g, 3 * i + 6)
                pe.wait_ge(self.e_w2[u], 32 * h + 32)
                pe.wait_ge(self.y_free, i + 1)
                for k in range(2):
                    for n in range(HC):
                        last = mm(pp[:, u, k * D:(k + 1) * D], self.hT[:, u, n, k * P:(k + 1) * P], self.w2[:, u, n], start=(n == 0), stop=(n == HC - 1))
                last.then_inc(self.e_y, 1)
        run_slots(pe, NT, 5, expert)

    def sync(self, sp):
        A, hall = self.A, self.hall
        sp.wait_ge(self.init, 2)
        for dst, src in ((self.wqk[0:H2], A["qkvT"]), (self.wqk[H2:H2 + 1, 1], A["qkvb"]), (self.wproj[0:H2], A["projT"]),
                         (self.wproj[H2:H2 + 1, 1], A["projb"]), (self.wgate[:], A["wgate"]), (self.n2[:, 0], A["n2"][0:1].to_broadcast([P, D])),
                         (self.n2[:, 1], A["n2"][1:2].to_broadcast([P, D]))):
            sp.dma_start(dst, src).then_inc(self.hw_ld, 16)
        for q in range(2):
            src = self.h2_d.rearrange("(i q) t d -> q t i d", q=2)[q, 0:T]
            for g in range(2):
                sp.dma_start(hall[q * B:q * B + T, 16 * g:16 * g + 16], src[:, 16 * g:16 * g + 16]).then_inc(self.h_ld, 16)
        sp.dma_start(self.xs_d[E * R:E * R + ROWS].rearrange("(k p) d -> p k d", k=2), self.zero[:]).then_inc(self.zero_st, 16)
        sp.wait_ge(self.meta_set, 1)
        for e in range(E):
            at = sp.value_load(self.meta[0:1, 2, e:e + 1], min_val=0, max_val=E * R - ROWS)
            sp.dma_start(self.xs_d[bass.ds(at, ROWS)].rearrange("(k p) d -> p k d", k=2), self.zero[:]).then_inc(self.zero_st, 16)
        sp.wait_ge(self.scat, 32 * NP)
        sp.wait_ge(self.zero_st, 16 * (E + 1))

        def slot(item):
            a, b, c = item(0), item(1), item(4)
            if a:
                i, u, h = a
                e = sp.value_load(self.meta[0:1, 0, bass.ds(i, 1)], min_val=0, max_val=E - 1)
                at = sp.value_load(self.meta[0:1, 1, bass.ds(i, 1)], min_val=0, max_val=E * R)
                sp.wait_ge(self.e_free, i + 1)
                sp.dma_start(self.w1[:, u], A["W1"][bass.ds(e, 1)].rearrange("e p h f -> p (e h) f")).then_inc(self.e_w[u], 16)
                sp.dma_start(self.b1[:, u], A["b1"][bass.ds(e, 1)].rearrange("e p c -> p (e c)")).then_inc(self.e_w[u], 16)
                sp.dma_start(self.xs[:, u], self.xs_d[bass.ds(at, ROWS)].rearrange("(k p) d -> p k d", k=2)).then_inc(self.e_w[u], 16)
            if b:
                i, u, h = b
                e = sp.value_load(self.meta[0:1, 0, bass.ds(i, 1)], min_val=0, max_val=E - 1)
                sp.wait_ge(self.y_free, i + 1)
                sp.dma_start(self.w2[:, u], A["W2"][bass.ds(e, 1)].rearrange("e p c d -> p (e c) d")).then_inc(self.e_w2[u], 16)
                sp.dma_start(self.b2[:, u], A["b2"][bass.ds(e, 1)].to_broadcast([P, D])).then_inc(self.e_w2[u], 16)
            if c:
                i, u, h = c
                sp.wait_ge(self.e_out, i + 1)
                sp.dma_start(self.ys_d[bass.ds(i * ROWS, ROWS)].rearrange("(k p) d -> p k d", k=2), self.ys[:, u]).then_inc(self.e_st[u], 16)
        run_slots(sp, NT, 5, slot)

        for g in range(8):
            sp.wait_ge(self.g_free, 4 * g + 8)
            for q in range(2):
                dst = self.out.rearrange("(i q) t d -> q t i d", q=2)[q, :, 4 * g:4 * g + 4]
                sp.dma_start(dst, hall[q * B:q * B + T, 4 * g:4 * g + 4]).then_inc(self.o_st, 16)
        sp.wait_ge(self.o_st, 256)


def build(nc, A, out, stop=99):
    ctx = ExitStack()
    with ctx:
        def sem(name):
            return ctx.enter_context(nc.semaphore(name))

        def ps(name, shape):
            return ctx.enter_context(nc.psum_tensor(name, shape, F32))

        def sb(name, shape, dt=F32, to=None):
            return (to or ctx).enter_context(nc.sbuf_tensor(name, shape, dt))

        def dram(name, shape, dt=F32):
            return nc.dram_tensor(name, shape, dt, kind="Internal").ap()

        base_d = dram("base_d", [2 * TT, B, D])
        h2_d = dram("h2_d", [B, 2 * TT, D])
        xs_d = dram("xs_d", [NROW, D])
        ys_d = dram("ys_d", [NT * ROWS, D])

        const = sb("const", [P, NCONST])
        ones = sb("ones", [P, P])
        ident = const[:, C_ID:C_ID + P]
        xnT = sb("xnT", [H2, 2, FRONT + POS, B])
        wqkv = sb("wqkv", [H2 + 1, 2, 3 * D])
        colg = sb("colg", [H2, 2, 5])
        mowT = sb("mowT", [H2, 2, D])
        owT = sb("owT", [H2 + 1, 2, D])

        e1 = ExitStack()
        wm = sb("wm", [P, 4, KC, D + 1], to=e1)
        ww = sb("ww", [P, 6, D + 1], to=e1)
        s1b = sb("s1b", [P, D], to=e1)
        s2b = sb("s2b", [P, D], to=e1)
        cb = sb("cb", [P, D], to=e1)
        xm = sb("xm", [P, 2, 2, KC, NA], to=e1)
        x6 = sb("x6", [P, 4, KC, P], to=e1)
        raw = sb("raw", [P, 8 * NA + 8 * NB], to=e1)
        sqs = sb("sqs", [P, 2, 2, NA], to=e1)
        sq6 = sb("sq6", [P, 4, P], to=e1)
        xh = sb("xh", [P, 4, D], to=e1)
        bs = sb("bs", [P, 4, D], to=e1)
        hh = sb("hh", [P, D], to=e1)
        st1 = sb("st1", [P, 24], to=e1)
        bn1 = sb("bn1", [P, 6], to=e1)
        e0 = ExitStack()
        w1 = sb("w1", [P, 5, KC, D], to=e0)
        w2 = sb("w2", [P, 8, D], to=e0)
        gb = sb("gb", [P, 2, 38], to=e0)
        trow = sb("trow", [1, 2, D], to=e0)
        inw = sb("inw", [H2, 2, 3, D], to=e0)
        qkw = sb("qkw", [H2, 2, 3, D + 1], to=e0)
        inb = sb("inb", [H2 + 1, 3 * D], to=e0)
        e0.close()
        wv = sb("wv", [P, 2, 2 * NA + 2 * NB], to=e1)
        wsq = sb("wsq", [P, 2, 2 * NA + 2 * NB], to=e1)
        wv6 = sb("wv6", [P, 6 * P], to=e1)
        wsq6 = sb("wsq6", [P, 6 * P], to=e1)
        sqt = sb("sqt", [P, KC * NA], to=e1)
        e1.close()

        pe1 = ps("pe1", [P, 4, 512])
        pt1 = ps("pt1", [P, 2, 512])
        pp = ps("pp", [P, 2, 512])

        c_ld, w_ld, w_ld2 = sem("c_ld"), sem("w_ld"), sem("w_ld2")
        ones_set = sem("ones_set")
        bias_mm, bias_out = sem("bias_mm"), sem("bias_out")
        wm_set, sum_mm, sum_out = sem("wm_set"), sem("sum_mm"), sem("sum_out")
        fold_mm, fold_out = sem("fold_mm"), sem("fold_out")
        x_ld = [sem("x_ld0"), sem("x_ld1"), sem("x_ld6")]
        raw_ld = sem("raw_ld")
        wave_set, wsq_set, sq_half, sq_free, sqs_set = sem("wave_set"), sem("wsq_set"), sem("sq_half"), sem("sq_free"), sem("sqs_set")
        tok_mm, tok_free = sem("tok_mm"), sem("tok_free")
        xh_set, xh_T, xh_out = sem("xh_set"), sem("xh_T"), sem("xh_out")
        bs_set = sem("bs_set")
        var_set, var_r = sem("var_set"), sem("var_r")
        hvar_set, hvar_r = sem("hvar_set"), sem("hvar_r")
        bs_st = [sem(f"bs_st{n}") for n in range(4)]

        NTOK = 25
        s = {"xh_out": xh_out, "tok_free": tok_free, "base_ld": sem("base_ld"), "h2_st": sem("h2_st")}
        hall = sb("hall", [P, NP, D])
        wins = Windows(nc, ctx, sb, sem, A, const, ones, xnT, wqkv, colg, mowT, owT, hall, base_d, h2_d, pe1, pt1, pp, s) if stop >= 2 else None
        heads = Heads(nc, ctx, sb, sem, A, const, ones, colg, hall, h2_d, xs_d, ys_d, out, pe1, pt1, pp, s) if stop >= 4 else None
        block = ctx.enter_context(nc.Block())

        def tile_of(r, pos):
            if pos == 3:
                return "last", 6, 14 * r + 6, 7
            i, j = (0, pos) if pos < 3 else (1, pos - 4)
            return i, 2 * j, 14 * r + 7 * i + 2 * j, 1

        eps_col = const[:, C_EPS:C_EPS + 1]

        def minus_half(n):
            return const[:, C_NH:C_NH + n]

        def before(pos):
            return (pos - 1) % 4 if pos else 2

        @block.sync
        def _(sp):
            sp.dma_start(const[:], A["consts"]).then_inc(c_ld, 16)
            for dst, src in ((gb[:], A["gb"]), (trow[:], A["tok_b"]), (w2[:], A["w2"])):
                sp.dma_start(dst, src).then_inc(w_ld, 16)
            for s in range(5):
                sp.dma_start(w1[:, s], A["w1"][:, s]).then_inc(w_ld, 16)
            for dst, src in ((inw[:], A["inw"]), (qkw[:], A["qkw"]), (inb[H2:H2 + 1, :], A["inb"]),
                             (colg[:], A["cols"]), (mowT[:], A["mowT"]), (owT[0:H2], A["owT"]), (owT[H2:H2 + 1, 1, :], A["ob"])):
                sp.dma_start(dst, src).then_inc(w_ld2, 16)

            def load_x(i, b):
                if b < 2:
                    sp.dma_start(xm[:, b].rearrange("p a c n -> p a (c n)"), A["xm"][bass.ds(i, 2)].rearrange("a p f -> p a f")).then_inc(x_ld[b], 16)
                else:
                    sp.dma_start(x6[:].rearrange("p a c n -> p (a c n)"), A["x6"][bass.ds(i, 1)].rearrange("a p f -> p (a f)")).then_inc(x_ld[2], 16)

            def load_raw(i, b):
                if b < 2:
                    for src, f0, f1 in (("xwa", 0, 8 * NA), ("xwb", 8 * NA, 8 * NA + 8 * NB)):
                        sp.dma_start(raw[:, f0:f1].rearrange("p (a f) -> p a f", a=2), A[src][bass.ds(i, 2)].rearrange("a p f -> p a f")).then_inc(raw_ld, 16)
                else:
                    for f0, f1 in ((0, 2048), (2048, 3072)):
                        sp.dma_start(raw[:, f0:f1], A["xw6"][bass.ds(i, 1), :, f0:f1].rearrange("a p f -> p (a f)")).then_inc(raw_ld, 16)

            load_x(0, 0)
            load_raw(0, 0)
            sp.wait_ge(wave_set, 1)
            load_raw(0, 2)
            load_x(0, 2)

            def pair(r):
                sp.wait_ge(wave_set, 3 * r + 2)
                load_raw(2 * r + 1, 1)
                sp.wait_ge(tok_mm, 7 * r)
                load_x(2 * r + 1, 1)
                sp.wait_ge(wave_set, 3 * r + 3)
                load_raw(2 * r + 2, 0)
                sp.wait_ge(tok_mm, 7 * r + 3)
                load_x(2 * r + 2, 0)
                sp.wait_ge(tok_mm, 7 * r + 4)
                load_x(r + 1, 2)
                sp.wait_ge(wave_set, 3 * r + 4)
                load_raw(r + 1, 2)

            with sp.Fori(0, 3) as r:
                pair(r)
            if wins:
                wins.sync(sp, bs_st, not heads)
            else:
                for n in range(4):
                    sp.wait_ge(bs_st[n], 112)
            if heads:
                heads.sync(sp)

        @block.scalar
        def _(act):
            def squares(u, b, loads, a):
                act.wait_ge(x_ld[b], loads)
                act.wait_ge(sq_free, 2 * u + a + 1)
                src = xm[:, b, a].rearrange("p c n -> p (c n)") if b < 2 else x6[:, 2 * a:2 * a + 2].rearrange("p q c n -> p (q c n)")
                nc.scalar.activation(sqt[:, 0:src.shape[1]], src, ACT.Square).then_inc(sq_half, 1)
                if a == 1:
                    act.wait_ge(wave_set, u + 1)
                    nc.scalar.activation(wsq[:, b] if b < 2 else wsq6[:], wv[:, b] if b < 2 else wv6[:], ACT.Square).then_inc(wsq_set, 1)

            def store(n, pos, r):
                _, _, t0, dt = tile_of(r, pos)
                k = pos % 4
                act.wait_ge(bs_set, n + 1)
                if dt == 1:
                    act.dma_start(base_d[bass.ds(t0, 2)].rearrange("t b d -> (t b) d"), bs[:, k]).then_inc(bs_st[k], 16)
                else:
                    for q in range(2):
                        act.dma_start(base_d[bass.ds(t0 + q * dt, 1)].rearrange("t b d -> (t b) d"),
                                      bs[q * B:(q + 1) * B, k]).then_inc(bs_st[k], 16)

            def put_T(n, pos, r):
                _, _, t0, dt = tile_of(r - 1, 6) if pos == 0 else tile_of(r, pos - 1)
                act.wait_ge(xh_T, n + 1)
                for h in range(2):
                    src = pt1[0:H2, pos % 2, h * P:(h + 1) * P].rearrange("p (t b) -> p t b", t=2)
                    for q in range(1 if dt == 1 else 2):
                        dst = xnT[:, h, bass.ds(FRONT + t0 + q * dt, 3 - dt if dt == 1 else 1), :]
                        last = nc.scalar.activation(dst, src if dt == 1 else src[:, q:q + 1, :], ACT.Identity,
                                                    bias=colg[:, h, 1:2], scale=colg[:, h, 0:1])
                last.then_inc(xh_out, 1)

            act.wait_ge(wm_set, 1)
            act.wait_ge(fold_out, 1)
            squares(0, 0, 16, 0)
            squares(0, 0, 16, 1)
            with act.Fori(0, 3) as r:
                for pos in range(7):
                    u, b, loads = UNIT_AT[pos // 2] if pos < 6 else (0, 0, 0)
                    if pos < 6:
                        squares(3 * r + u, b, 16 * r + loads, pos % 2)
                    put_T(7 * r + pos, pos, r)
                    store(7 * r + pos, pos, r)
            squares(10, 2, 64, 0)
            squares(10, 2, 64, 1)
            for pos in range(4):
                put_T(21 + pos, pos, 3)
                if pos < 3:
                    store(21 + pos, pos, 3)
            act.wait_ge(bs_set, 25)
            act.dma_start(base_d[T - 1:T + 1].rearrange("t b d -> (t b) d"), bs[:, 3]).then_inc(bs_st[3], 16)
            if wins:
                wins.scalar(act)
            if heads:
                heads.scalar(act)

        @block.gpsimd
        def _(pool):
            nc.gpsimd.memset(ones[:], 1.0).then_inc(ones_set, 1)
            nc.gpsimd.memset(xh[:, 2], 0.0).then_inc(ones_set, 1)

            def add_squares(u, b, a):
                pool.wait_ge(sq_half, 2 * u + a + 1)
                if b < 2:
                    dst = sqs[:, b, a]
                    src = [sqt[:, c * NA:(c + 1) * NA] for c in range(KC)]
                else:
                    dst = sq6[:, 2 * a:2 * a + 2]
                    halves = sqt[:, 0:2 * KC * P].rearrange("p (q c n) -> p q c n", q=2, c=KC)
                    src = [halves[:, :, c] for c in range(KC)]
                nc.gpsimd.tensor_tensor(dst, src[0], src[1], ALU.add)
                for c in range(2, KC):
                    pool.drain()
                    last = nc.gpsimd.tensor_tensor(dst, dst, src[c], ALU.add)
                last.then_inc(sq_free, 1)
                if a == 1:
                    pool.drain().then_inc(sqs_set, 1)

            def roots(n):
                pool.wait_ge(var_set, n + 1)
                nc.gpsimd.tensor_tensor(st1[:, 12:14], st1[:, 4:6], minus_half(2), ALU.pow).then_inc(var_r, 1)
                pool.wait_ge(hvar_set, n + 1)
                nc.gpsimd.tensor_tensor(st1[:, 10:11], st1[:, 9:10], eps_col, ALU.add)
                pool.drain()
                nc.gpsimd.tensor_tensor(st1[:, 10:11], st1[:, 10:11], minus_half(1), ALU.pow)
                pool.drain()
                nc.gpsimd.tensor_tensor(st1[:, 11:12], st1[:, 9:10], st1[:, 10:11], ALU.mult)
                pool.drain()
                nc.gpsimd.tensor_tensor(st1[:, 11:12], st1[:, 11:12], st1[:, 10:11], ALU.mult)
                pool.drain()
                nc.gpsimd.tensor_tensor(st1[:, 11:12], st1[:, 11:12], eps_col, ALU.add)
                pool.drain()
                nc.gpsimd.tensor_tensor(st1[:, 11:12], st1[:, 11:12], minus_half(1), ALU.pow).then_inc(hvar_r, 1)

            pool.wait_ge(c_ld, 16)
            nc.gpsimd.memset(st1[0:1, 20:21], 0.0).then_inc(sq_free, 1)
            add_squares(0, 0, 0)
            add_squares(0, 0, 1)
            with pool.Fori(0, 3) as r:
                for pos in range(7):
                    if pos < 6:
                        u, b, _ = UNIT_AT[pos // 2]
                        pool.wait_ge(tok_mm, 7 * r + (0, 0, 3)[pos // 2])
                        add_squares(3 * r + u, b, pos % 2)
                    roots(7 * r + pos)
            pool.wait_ge(tok_mm, 18)
            add_squares(10, 2, 0)
            add_squares(10, 2, 1)
            for pos in range(4):
                roots(21 + pos)
            if wins:
                wins.gpsimd(pool)
            if heads:
                heads.gpsimd(pool)

        @block.vector
        def _(dve):
            v = nc.vector
            v.memset(st1[0:1, 21:22], 0.0).then_inc(tok_free, 3)
            dve.wait_ge(c_ld, 16)
            dve.wait_ge(bias_mm, 1)
            v.tensor_copy(cb[:], pp[:, 0, 0:D]).then_inc(bias_out, 1)
            gm = gb[:, 0, 0:30].rearrange("p (s c) -> p s c", s=5)
            for s in range(5):
                v.tensor_tensor(w1[:, s], w1[:, s], gm[:, s].unsqueeze(2).to_broadcast([P, KC, D]), ALU.mult)
            v.tensor_tensor(w2[:], w2[:], gb[:, 0, 30:38].unsqueeze(2).to_broadcast([P, 8, D]), ALU.mult)
            dve.drain()
            for q in range(4):
                v.scalar_tensor_tensor(wm[:, q, :, 0:D], w1[:, 4], const[:, C_MK + q:C_MK + q + 1], w1[:, q], ALU.mult, ALU.add)
                v.tensor_scalar(wm[:, q, :, D:D + 1], const[:, C_MK + q:C_MK + q + 1].unsqueeze(1).to_broadcast([P, KC, 1]), 1.0, None, ALU.add)
            for q in range(6):
                v.scalar_tensor_tensor(ww[:, q, 0:D], w2[:, 6 + q // 4], const[:, C_MK + 4 + q:C_MK + 5 + q], w2[:, q], ALU.mult, ALU.add)
            v.tensor_scalar(ww[:, :, D:D + 1], const[:, C_MK + 4:C_MK + 10].unsqueeze(2), 1.0, None, ALU.add)
            dve.drain().then_inc(wm_set, 1)
            dve.wait_ge(sum_mm, 1)
            v.tensor_copy(s1b[:], pp[:, 0, 0:D])
            v.tensor_copy(s2b[:], pp[:, 1, 0:D]).then_inc(sum_out, 1)
            dve.wait_ge(fold_mm, 1)
            dve.wait_ge(w_ld2, 16 * 7)
            for h in range(2):
                v.tensor_copy(wqkv[0:H2, h, 0:2 * D], pe1[0:H2, 2 * h, 0:2 * D])
                v.tensor_copy(wqkv[0:H2, h, 2 * D:3 * D], pe1[0:H2, 2 * h + 1, 0:D])
            v.tensor_tensor(wqkv[H2:H2 + 1, 1, 0:2 * D], pt1[H2:H2 + 1, 0, 0:2 * D], inb[H2:H2 + 1, 0:2 * D], ALU.add)
            v.tensor_tensor(wqkv[H2:H2 + 1, 1, 2 * D:3 * D], pt1[H2:H2 + 1, 1, 0:D], inb[H2:H2 + 1, 2 * D:3 * D], ALU.add)
            dve.drain().then_inc(fold_out, 1)

            def waves(u, b):
                dve.wait_ge(raw_ld, 32 * u + 32)
                parts = ((2, NA), (2, NB)) if b < 2 else ((4, P), (2, P))
                f0 = w0 = 0
                for rows, n in parts:
                    src = raw[:, f0:f0 + 4 * rows * n].rearrange("p (a k n) -> p a k n", a=rows, k=4)
                    w = (wv[:, b] if b < 2 else wv6[:])[:, w0:w0 + rows * n].rearrange("p (a n) -> p a n", a=rows)
                    v.tensor_tensor(w, src[:, :, 1], src[:, :, 2], ALU.add)
                    dve.drain()
                    v.tensor_tensor(w, w, src[:, :, 3], ALU.add)
                    dve.drain()
                    v.scalar_tensor_tensor(w, src[:, :, 0], 3.0, w, ALU.mult, ALU.subtract)
                    f0, w0 = f0 + 4 * rows * n, w0 + rows * n
                dve.drain().then_inc(wave_set, 1)

            def post(n, k, stored):
                dve.wait_ge(tok_mm, n + 1)
                y = pe1[:, k]
                stat = y.rearrange("p (a c) -> p a c", a=2)[:, :, D:D + 2]
                m = st1[:, 0:4].rearrange("p (a c) -> p a c", a=2)
                mean, e2 = m[:, :, 0], m[:, :, 1]
                v.tensor_tensor(m, stat, const[:, C_INV:C_INV + 4].rearrange("p (a c) -> p a c", a=2), ALU.mult)
                dve.drain()
                v.tensor_tensor(st1[:, 4:6], mean, mean, ALU.mult)
                dve.drain()
                v.tensor_tensor(st1[:, 4:6], e2, st1[:, 4:6], ALU.subtract)
                dve.drain()
                v.tensor_scalar(st1[:, 4:6], st1[:, 4:6], 0.0, EPS, ALU.max, ALU.add).then_inc(var_set, 1)
                dve.wait_ge(var_r, n + 1)
                v.scalar_tensor_tensor(st1[:, 6:8], mean, -1.0, st1[:, 12:14], ALU.mult, ALU.mult)
                v.tensor_tensor(st1[:, 4:6], st1[:, 12:14], const[:, C_SIX:C_SIX + 2], ALU.mult)
                dve.drain()
                v.scalar_tensor_tensor(hh[:], s1b[:], st1[:, 6:7], cb[:], ALU.mult, ALU.add)
                dve.drain()
                v.scalar_tensor_tensor(hh[:], s2b[:], st1[:, 7:8], hh[:], ALU.mult, ALU.add)
                dve.drain()
                v.scalar_tensor_tensor(hh[:], y[:, 0:D], st1[:, 4:5], hh[:], ALU.mult, ALU.add)
                dve.drain()
                v.scalar_tensor_tensor(hh[:], y[:, 256:256 + D], st1[:, 5:6], hh[:], ALU.mult, ALU.add).then_inc(tok_free, 1)
                dve.drain()
                v.bn_stats(bn1[:], hh[:])
                dve.drain()
                v.bn_aggr(st1[:, 8:10], bn1[:]).then_inc(hvar_set, 1)
                dve.wait_ge(hvar_r, n + 1)
                dve.wait_ge(xh_T, n)
                dve.wait_ge(bs_st[k], stored)
                v.tensor_scalar(xh[:, k], hh[:], st1[:, 8:9], st1[:, 10:11], ALU.subtract, ALU.mult)
                dve.drain()
                v.tensor_tensor(bs[:, k], hh[:], xh[:, k], ALU.add).then_inc(bs_set, 1)
                v.tensor_scalar(xh[:, k], xh[:, k], st1[:, 11:12], None, ALU.mult).then_inc(xh_set, 1)
                dve.drain()

            waves(0, 0)
            with dve.Fori(0, 3) as r:
                for pos in range(7):
                    if pos in (0, 2, 4):
                        u, b, _ = UNIT_AT[pos // 2]
                        dve.wait_ge(tok_mm, 7 * r + (0, 0, 3)[pos // 2])
                        waves(3 * r + u, b)
                    post(7 * r + pos, pos % 4, 32 * r + (16 if pos >= 4 else 0))
            waves(10, 2)
            for pos in range(4):
                post(21 + pos, pos, 96)
            if wins:
                wins.vector(dve)
            if heads:
                heads.vector(dve)

        @block.tensor
        def _(pe):
            mm = nc.tensor.matmul
            pe.wait_ge(ones_set, 2)
            pe.wait_ge(w_ld, 16 * 8)
            def bcol(n, k=P):
                return gb[0:k, 1, n:n + 1].to_broadcast([k, P])

            for n in range(30):
                mm(pp[:, 0, 0:D], bcol(n), w1[:, n // KC, n % KC], start=(n == 0), stop=False)
            for n in range(8):
                k = 64 if n == 7 else P
                mm(pp[:, 0, 0:D], bcol(30 + n, k), w2[0:k, n], start=False, stop=False)
            for n in range(2):
                last = mm(pp[:, 0, 0:D], ones[0:1, :], trow[0:1, n], start=False, stop=(n == 1))
            last.then_inc(bias_mm, 1)
            pe.wait_ge(w_ld2, 16 * 7)
            for h in range(2):
                for g in range(3):
                    dst = pe1[0:H2, 2 * h + g // 2, (g % 2) * D:(g % 2) * D + D]
                    for m in range(2):
                        mm(dst, qkw[:, m, g, h * H2:(h + 1) * H2], inw[:, m, g], start=(m == 0), stop=(m == 1))
            for g in range(3):
                for m in range(2):
                    dst = pt1[H2:H2 + 1, g // 2, (g % 2) * D:(g % 2) * D + D]
                    last = mm(dst, qkw[:, m, g, D:D + 1], inw[:, m, g], start=(m == 0), stop=(m == 1))
            last.then_inc(fold_mm, 1)
            pe.wait_ge(wm_set, 1)
            pe.wait_ge(bias_out, 1)
            for n in range(24):
                mm(pp[:, 0, 0:D], ones[:], wm[:, n // KC, n % KC, 0:D], start=(n == 0), stop=(n == 23))
            for n in range(6):
                last = mm(pp[:, 1, 0:D], ones[:], ww[:, n, 0:D], start=(n == 0), stop=(n == 5))
            last.then_inc(sum_mm, 1)
            pe.wait_ge(fold_out, 1)

            def tokens(n, b, j0, k):
                pe.wait_ge(tok_free, n + 1)
                y = pe1[:, k]

                def cell(q, c):
                    if b == 2:
                        return x6[:, q, c]
                    n0 = (j0 + q % 2) * B
                    return xm[:, b, q // 2, c, n0:n0 + P]

                def cell_squares(q):
                    if b == 2:
                        return sq6[:, q]
                    n0 = (j0 + q % 2) * B
                    return sqs[:, b, q // 2, n0:n0 + P]

                def wave(rows, col, q):
                    if b == 2:
                        return col[:, q * P:(q + 1) * P]
                    n0 = (q // 2) * NA + (j0 + q % 2) * B if q < 4 else 2 * NA + (q - 4) * NB + j0 * B
                    return rows[:, b, n0:n0 + P]

                for q in range(4):
                    for c in range(KC):
                        mm(y[:, 0:D + 1], cell(q, c), wm[:, q, c], start=(q + c == 0), stop=(q == 3 and c == KC - 1))
                for q in range(4):
                    mm(y[:, D + 1:D + 2], cell_squares(q), wm[:, q, 0, D:D + 1], start=(q == 0), stop=(q == 3))
                for q in range(6):
                    mm(y[:, 256:256 + D + 1], wave(wv, wv6, q), ww[:, q], start=(q == 0), stop=(q == 5))
                for q in range(6):
                    last = mm(y[:, 256 + D + 1:256 + D + 2], wave(wsq, wsq6, q), ww[:, q, D:D + 1], start=(q == 0), stop=(q == 5))
                last.then_inc(tok_mm, 1)

            def transpose(n, pos):
                pe.wait_ge(xh_set, n)
                pe.wait_ge(xh_out, n)
                for h in range(2):
                    last = nc.tensor.transpose(pt1[0:H2, pos % 2, h * P:(h + 1) * P],
                                               xh[:, before(pos), h * H2:(h + 1) * H2], ident)
                last.then_inc(xh_T, 1)

            def unit_ready(u, b, loads):
                pe.wait_ge(x_ld[b], loads)
                pe.wait_ge(wave_set, u + 1)
                pe.wait_ge(wsq_set, u + 1)
                pe.wait_ge(sqs_set, u + 1)

            with pe.Fori(0, 3) as r:
                for pos in range(7):
                    if pos == 0:
                        unit_ready(3 * r, 0, 16 * r + 16)
                    if pos == 3:
                        unit_ready(3 * r + 1, 2, 16 * r + 16)
                    if pos == 4:
                        unit_ready(3 * r + 2, 1, 16 * r + 16)
                    tokens(7 * r + pos, 0 if pos < 3 else 2 if pos == 3 else 1, tile_of(0, pos)[1], pos % 4)
                    transpose(7 * r + pos, pos)
            for pos in range(4):
                if pos == 0:
                    unit_ready(9, 0, 64)
                if pos == 3:
                    unit_ready(10, 2, 64)
                tokens(21 + pos, 0 if pos < 3 else 2, tile_of(3, pos)[1], pos)
                transpose(21 + pos, pos)
            if wins:
                wins.tensor(pe)
            if heads:
                heads.tensor(pe)


def lay_out(inputs):
    import numpy as np

    f = {k: np.asarray(v) for k, v in inputs.items()}
    g = {}
    x = f["x"]
    pad = np.zeros((B, CH, NC * CELL, NC * CELL), x.dtype)
    pad[:, :, CELL // 2:CELL // 2 + 112, CELL // 2:CELL // 2 + 112] = x
    m = pad.reshape(B, CH, NC, 2, 8, NC, 2, 4, 2)
    m = m.transpose(2, 5, 3, 6, 4, 7, 8, 1, 0).reshape(NC, NC, P, KC, B)
    rows = np.ascontiguousarray(m.transpose(0, 2, 3, 1, 4))
    g["xm"] = np.ascontiguousarray(rows[:, :, :, :7]).reshape(NC, P, KC * NA)
    w = pad.reshape(B, CH, NC, 2, 4, 2, NC, 2, 4, 2)
    w = w.transpose(2, 6, 3, 7, 4, 8, 1, 5, 9, 0).reshape(NC, NC, D, 4, B)
    w = np.ascontiguousarray(w.transpose(0, 2, 3, 1, 4))
    low = w[:, P:]
    both = np.concatenate([low[:, :, :, 0:NC - 1], low[:, :, :, 1:NC]], 1)
    g["xwa"] = np.ascontiguousarray(w[:, :P, :, :7]).reshape(NC, P, 4 * NA)
    g["xwb"] = np.ascontiguousarray(both[:, :, :, :6]).reshape(NC, P, 4 * NB)
    x6, xw6 = [], []
    for r in range(4):
        i = [2 * r, min(2 * r + 1, G - 1)]
        x6.append(np.stack([np.stack([rows[k + a, :, :, 6 + b] for k in i], 2) for a in range(2) for b in range(2)], 1).reshape(P, -1))
        wa = np.stack([np.stack([w[k + a, :P, :, 6 + b] for k in i], 2) for a in range(2) for b in range(2)], 1).reshape(P, -1)
        wb = np.stack([np.stack([both[k + a, :, :, 6] for k in i], 2) for a in range(2)], 1).reshape(P, -1)
        xw6.append(np.concatenate([wa, wb], 1))
    g["x6"], g["xw6"] = np.stack(x6), np.stack(xw6)

    def main_rows(a):
        n = a.shape[1]
        a = a.reshape(16, 16, 5, CH, n)
        out = []
        for s in (1, 2, 3, 4, 0):
            t = a[:, :, s]
            if s == 0:
                t = np.roll(t, (8, 8), (0, 1))
            t = t.reshape(2, 8, 2, 4, 2, CH, n).transpose(0, 2, 1, 3, 4, 5, 6)
            out.append(t.reshape(P, KC, n))
        return np.ascontiguousarray(np.stack(out, 1))

    def wave_rows(a):
        n = a.shape[1]
        a = a.reshape(8, 8, 5, CH, n)
        r = []
        for s in (1, 2, 3, 4, 0):
            t = a[:, :, s]
            if s == 0:
                t = np.roll(t, (4, 4), (0, 1))
            r.append(t.reshape(2, 4, 2, 4, CH, n).transpose(0, 2, 1, 3, 4, 5).reshape(D, n))
        out = [r[q][:P] for q in range(4)]
        out += [np.concatenate([r[0][P:], r[1][P:]]), np.concatenate([r[2][P:], r[3][P:]])]
        out += [r[4][:P], np.concatenate([r[4][P:], r[4][P:]])]
        return np.ascontiguousarray(np.stack(out, 1))

    g["w1"] = main_rows(f["L0_tok_w1"])
    g["w2"] = wave_rows(f["L0_tok_w2"])
    gb = np.zeros((P, 2, 38), np.float32)
    for n, (a, b) in enumerate((("L0_tok_ln1_g", "L0_tok_ln2_g"), ("L0_tok_ln1_b", "L0_tok_ln2_b"))):
        gb[:, n, 0:30] = main_rows(f[a][:, None]).reshape(P, 30)
        gb[:, n, 30:] = wave_rows(f[b][:, None]).reshape(P, 8)
    g["gb"] = gb
    g["tok_b"] = np.stack([f["L0_tok_b1"], f["L0_tok_b2"]])[None]

    def halves(a):
        return np.ascontiguousarray(a.reshape(2, H2, -1).transpose(1, 0, 2))

    g["inw"] = halves(f["L0_attn_inw"].T).reshape(H2, 2, 3, D)
    qk = [halves(np.concatenate([f[f"L0_attn_{c}w"], f[f"L0_attn_{c}b"][:, None]], 1)) for c in "qkv"]
    g["qkw"] = np.ascontiguousarray(np.stack(qk, 2))
    g["inb"] = f["L0_attn_inb"][None]
    cols = [f[n][:, None] for n in ("L0_attn_ln_g", "L0_attn_ln_b", "L0_attn_mob", "L0_ffn_norm1_w", "L0_ffn_norm1_b")]
    g["cols"] = halves(np.concatenate(cols, 1))
    g["mowT"] = halves(f["L0_attn_mow"].T)
    g["owT"] = halves(f["L0_attn_ow"].T)
    g["ob"] = f["L0_attn_ob"][None]
    g["qkvT"] = halves(f["L0_ffn_qkv_w"].T)
    g["qkvb"] = f["L0_ffn_qkv_b"][None]
    g["projT"] = halves(f["L0_ffn_proj_w"].T)
    g["projb"] = f["L0_ffn_proj_b"][None]
    g["n2"] = np.stack([f["L0_ffn_norm2_w"], f["L0_ffn_norm2_b"]])
    g["wgate"] = halves(f["L0_ffn_w_gate"])
    g["W1"] = np.ascontiguousarray(f["L0_ffn_W1"].reshape(E, 2, H2, HID).transpose(0, 2, 1, 3))
    g["b1"] = np.ascontiguousarray(f["L0_ffn_b1"].reshape(E, HC, P).transpose(0, 2, 1))
    g["W2"] = np.ascontiguousarray(f["L0_ffn_W2"].reshape(E, HC, P, D).transpose(0, 2, 1, 3))
    g["b2"] = f["L0_ffn_b2"]

    c = np.zeros((P, NCONST), np.float32)
    c[:, C_ID:C_ID + P] = np.eye(P)
    p = np.arange(P)
    for q in range(4):
        c[:, C_MK + q] = p // 32 == 3 - q
        c[:, C_MK + 4 + q] = p // 48 == 3 - q
    for a in range(2):
        quad = (P + p % 64) // 48
        c[:, C_MK + 8 + a] = quad == 3 - 2 * a - p // 64
    c[:, C_INV:C_INV + 4] = [1 / PATCH, 1 / PATCH, 1 / (6 * WAVE), 1 / (36 * WAVE)]
    c[:, C_SIX:C_SIX + 2] = [1, 1 / 6]
    for h in range(6):
        c[:, C_KM + h] = p // AHD == h
    c[:, C_NH:C_NH + 2] = -0.5
    c[:, C_EPS:C_EPS + 2] = EPS
    c[:, C_EI:C_EI + E] = np.arange(E)
    real = (p % B) < T
    c[:, C_VAL] = real
    c[:, C_VAL + 1] = np.where(real, 0, FAR)
    c[:, C_ER:C_ER + E] = np.arange(E) * R
    c[:, C_J:C_J + NT] = np.arange(NT)
    c[:, C_L8:C_L8 + E * E] = (np.arange(E)[:, None] >= np.arange(E)[None]).reshape(-1)
    c[:, C_TRI:C_TRI + P] = p[:, None] < p[None]
    g["consts"] = c
    return g


def kernel(**inputs):
    import numpy as np
    import concourse.bacc as bacc
    from concourse.bass_utils import run_bass_kernel_spmd

    nc = bacc.Bacc("TRN2", target_bir_lowering=False, num_devices=1)
    arrays = lay_out(inputs)
    aps = {n: nc.dram_tensor(f"in_{n}", a.shape, mybir.dt.from_np(a.dtype), kind="ExternalInput").ap() for n, a in arrays.items()}
    out = nc.dram_tensor("out", (B, T, D), F32, kind="ExternalOutput").ap()
    build(nc, aps, out)
    r = run_bass_kernel_spmd(nc, [{f"in_{n}": a for n, a in arrays.items()}], core_ids=[0])
    return r.results[0]["out"]
```

```python
from contextlib import ExitStack

import concourse.bass as bass
from concourse import mybir

F32 = mybir.dt.float32
BF16 = mybir.dt.bfloat16
I32 = mybir.dt.int32
U32 = mybir.dt.uint32
ALU = mybir.AluOpType
ACT = mybir.ActivationFunctionType
X = mybir.AxisListType.X

P = 128
B = 64
G = 7
T = G * G
D = 192
H2 = D // 2
EPS = 1e-5
CELL = 16
NC = 8
CH = 3
KC = CELL * CELL * CH // P
PATCH = 5 * CELL * CELL * CH
WAVE = PATCH // 4
NA = 7 * B
NB = 6 * B
WH = 6
WHD = D // WH
NWT = 11
POS = 66
FRONT = 3
AH = 12
AHD = D // AH
NP = B // 2
E = 8
HID = 768
HC = HID // P
ROWS = 128
NT = (2 * B * T + E * (ROWS - 1)) // ROWS
R = B * T + ROWS
DX = D + 1
NROW = E * R + ROWS
FAR = 1 << 20
TT = (T + 1) // 2
UNIT_AT = [(1, 2, 16), (2, 1, 16), (3, 0, 32)]

C_ID = 0
C_MK = C_ID + P
C_INV = C_MK + 10
C_SIX = C_INV + 4
C_KM = C_SIX + 2
C_NH = C_KM + 6
C_EPS = C_NH + 2
C_EI = C_EPS + 2
C_VAL = C_EI + E
C_ER = C_VAL + 2
C_J = C_ER + E
C_L8 = C_J + NT
C_TRI = C_L8 + E * E
C_ROW = C_TRI + P
NCONST = C_ROW + 2 * NP


def run_slots(eng, n, depth, slot, unroll=2):
    def at(t, k, u, full):
        def item(lag):
            if not full and not 0 <= t - lag < n:
                return None
            return (t - lag, (u - lag) % unroll, k + (u - lag) // unroll)
        return item

    first = -(-(depth - 1) // unroll)
    last = n // unroll
    for t in range(first * unroll):
        slot(at(t, t // unroll, t % unroll, False))
    with eng.Fori(first, last) as k:
        for u in range(unroll):
            slot(at(unroll * k + u, k, u, True))
    for t in range(last * unroll, n + depth - 1):
        slot(at(t, t // unroll, t % unroll, False))


class Windows:

    def __init__(self, nc, ctx, sb, sem, A, const, ones, xnT, wqkv, colg, mowT, owT, hall, base_d, h2_d, pe1, pt1, pp, s):
        self.nc, self.const, self.xnT, self.wqkv, self.colg, self.mowT, self.owT = nc, const, xnT, wqkv, colg, mowT, owT
        self.hall, self.base_d, self.h2_d, self.pe1, self.pt1, self.pp, self.s = hall, base_d, h2_d, pe1, pt1, pp, s
        own = ExitStack()
        self.stg = sb("stg", [H2 + 1, 2, 2, 3, P], to=own)
        self.qkv = sb("qkv", [P, 2, 3, 3 * D], to=own)
        self.prod = sb("prod", [P, 3, 3, D], to=own)
        self.sc = sb("sc", [P, 3, 3, WH], to=own)
        self.ex = sb("ex", [P, 3, 3, WH], to=own)
        self.mx = sb("mx", [P, 3, WH], to=own)
        self.ob = sb("ob", [P, 3, D], to=own)
        self.oT = sb("oT", [H2, 2, 3 * P], to=own)
        self.gall = sb("gall", [H2, 2, POS, B], to=own)
        self.g12 = sb("g12", [H2, 2, 15, B], to=own)
        self.accT = sb("accT", [H2, 2, 2 * TT, B], to=own)
        self.st3 = sb("st3", [H2 + 1, 2, 2, P], to=own)
        own.close()
        self.stg_set, self.stg_used, self.qkv_mm, self.qkv_out, self.qkv_free = sem("stg_set"), sem("stg_used"), sem("qkv_mm"), sem("qkv_out"), sem("qkv_free")
        self.w_sc, self.w_ex, self.w_o, self.o_T, self.o_out = sem("w_sc"), sem("w_ex"), sem("w_o"), sem("o_T"), sem("o_out")
        self.so_mm, self.so_out, self.pooled, self.gelu_set, self.acc_set = sem("so_mm"), sem("so_out"), sem("pooled"), sem("gelu_set"), sem("acc_set")
        self.st3_set, self.st3_used, self.mix_mm, self.h2_set = sem("st3_set"), sem("st3_used"), sem("mix_mm"), sem("h2_set")

    def gpsimd(self, pool):
        nc, xnT, stg = self.nc, self.xnT, self.stg
        pool.wait_ge(self.s["xh_out"], 25)
        pool.wait_ge(self.pooled, 1)

        def slot(item):
            if (it := item(0)):
                i, u, _ = it
                pool.wait_ge(self.stg_used, i + 1)
                for h in range(2):
                    src = xnT[:, h, bass.ds(FRONT + 6 * i, 6), :].rearrange("p (w s) b -> p s w b", s=3)
                    last = nc.gpsimd.tensor_copy(stg[0:H2, u, h].rearrange("p s (w b) -> p s w b", w=2), src)
                last.then_inc(self.stg_set, 1)
        run_slots(pool, NWT, 1, slot)

        def mix(item):
            i, u, _ = item(0)
            pool.wait_ge(self.st3_used, i)
            nc.gpsimd.tensor_copy(self.st3[0:H2, u], self.accT[:, :, bass.ds(2 * i, 2), :].rearrange("p h t b -> p h (t b)")).then_inc(self.st3_set, 1)
        pool.wait_ge(self.acc_set, 1)
        run_slots(pool, TT, 1, mix)

    def tensor(self, pe):
        nc, mm = self.nc, self.nc.tensor.matmul
        pe1, pt1, pp, stg = self.pe1, self.pt1, self.pp, self.stg
        ident = self.const[:, C_ID:C_ID + P]
        pe.wait_ge(self.s["tok_free"], 28)
        pe.wait_ge(self.s["xh_out"], 25)

        def qkv(i, u, s):
            pe.wait_ge(self.qkv_out, 3 * i + s + 1)
            b = 2 * ((u + s) % 2)
            for n in range(2):
                mm(pe1[:, b + n, 0:288], stg[0:H2, u, 0, s], self.wqkv[0:H2, 0, n * 288:(n + 1) * 288], start=True, stop=False)
                last = mm(pe1[:, b + n, 0:288], stg[:, u, 1, s], self.wqkv[:, 1, n * 288:(n + 1) * 288], start=False, stop=True)
            last.then_inc(self.qkv_mm, 1)
            if s == 2:
                pe.drain().then_inc(self.stg_used, 1)

        def slot(item):
            a, c = item(0), item(2)
            if c:
                i, u, _ = c
                pe.wait_ge(self.w_o, i + 1)
                pe.wait_ge(self.o_out, i)
                for h in range(2):
                    for s in range(3):
                        last = nc.tensor.transpose(pt1[0:H2, h, s * P:(s + 1) * P], self.ob[:, s, h * H2:(h + 1) * H2], ident)
                last.then_inc(self.o_T, 1)
            if a:
                i, u, _ = a
                pe.wait_ge(self.stg_set, i + 1)
                qkv(i, u, 0)
            if c:
                i, u, _ = c
                pe.wait_ge(self.o_out, i + 1)
                pe.wait_ge(self.so_out, i)
                for m in range(2):
                    for h in range(2):
                        last = mm(pp[0:H2, m, 0:3 * P], self.mowT[:, h, m * H2:(m + 1) * H2], self.oT[:, h], start=(h == 0), stop=(h == 1))
                last.then_inc(self.so_mm, 1)
            if a:
                i, u, _ = a
                qkv(i, u, 1)
                qkv(i, u, 2)
        run_slots(pe, NWT, 3, slot)

        pe.wait_ge(self.so_out, NWT)

        def mix(item):
            i, u, _ = item(0)
            pe.wait_ge(self.st3_set, i + 1)
            pe.wait_ge(self.h2_set, i)
            mm(pp[:, u, 0:D], self.st3[0:H2, u, 0], self.owT[0:H2, 0], start=True, stop=False)
            mm(pp[:, u, 0:D], self.st3[:, u, 1], self.owT[:, 1], start=False, stop=True).then_inc(self.mix_mm, 1)
            pe.drain().then_inc(self.st3_used, 1)
        run_slots(pe, TT, 1, mix)

    def scalar(self, act):
        nc = self.nc
        pe1, pt1, pp, gall, colg = self.pe1, self.pt1, self.pp, self.gall, self.colg

        def qkv(i, u, s):
            if s == 0:
                act.wait_ge(self.qkv_free, i + 1)
            act.wait_ge(self.qkv_mm, 3 * i + s + 1)
            b = 2 * ((u + s) % 2)
            nc.scalar.activation(self.qkv[:, u, s].rearrange("p (n f) -> p n f", n=2), pe1[:, b:b + 2, 0:288], ACT.Copy).then_inc(self.qkv_out, 1)

        def slot(item):
            a, b, c = item(0), item(1), item(2)
            if c:
                i, u, _ = c
                act.wait_ge(self.o_T, i + 1)
                nc.scalar.activation(self.oT[:], pt1[0:H2, :, 0:3 * P], ACT.Copy).then_inc(self.o_out, 1)
            if a:
                qkv(*a[:2], 0)
            if c:
                i, u, _ = c
                act.wait_ge(self.so_mm, i + 1)
                for m in range(2):
                    dst = gall[:, m, bass.ds(6 * i, 6), :].rearrange("p (w s) b -> p s w b", s=3)
                    last = nc.scalar.activation(dst, pp[0:H2, m, 0:3 * P].rearrange("p (s w b) -> p s w b", s=3, w=2),
                                                ACT.Identity, bias=colg[:, m, 2:3])
                last.then_inc(self.so_out, 1)
            if a:
                qkv(*a[:2], 1)
            if b:
                i, u, _ = b
                act.wait_ge(self.w_sc, i + 1)
                nc.scalar.activation(self.ex[:], self.sc[:], ACT.Exp, scale=WHD ** -0.5).then_inc(self.w_ex, 1)
            if a:
                qkv(*a[:2], 2)
        run_slots(act, NWT, 3, slot)
        act.drain()
        for a, b in ((48, 66), (0, 16), (16, 32), (32, 48)):
            nc.scalar.activation(gall[:, :, a:b].rearrange("p h t b -> p h (t b)"), gall[:, :, a:b].rearrange("p h t b -> p h (t b)"), ACT.Gelu).then_inc(self.gelu_set, 1)

    def vector(self, dve):
        nc, v, xnT, qkv, prod = self.nc, self.nc.vector, self.xnT, self.qkv, self.prod
        dve.wait_ge(self.s["xh_out"], 25)
        for src, dst, n in ((FRONT, FRONT + 48, 15), (FRONT + 48, FRONT + 63, 3)):
            out = xnT[:, :, dst:dst + n, :]
            x = [xnT[:, :, src + q:src + q + 3 * n - 2:3, :] for q in range(3)]
            v.tensor_tensor(out, x[0], x[1], ALU.add)
            dve.drain()
            v.tensor_tensor(out, out, x[2], ALU.add)
            dve.drain()
            v.tensor_scalar(out, out, 1 / 3, None, ALU.mult)
            dve.drain()
        v.memset(self.stg[H2:H2 + 1].rearrange("p u h s n -> p (u h s n)"), 1.0).then_inc(self.stg_used, 2)
        v.memset(self.st3[H2:H2 + 1].rearrange("p u h n -> p (u h n)"), 1.0).then_inc(self.st3_used, 1)
        v.memset(self.mx[0:1, 0, 0:1], 0.0).then_inc(self.qkv_free, 2)
        v.memset(self.mx[0:1, 0, 1:2], 0.0).then_inc(self.qkv_out, 2)
        dve.drain().then_inc(self.pooled, 1)

        def slot(item):
            if not (it := item(1)):
                return
            i, u, _ = it
            dve.drain()
            dve.wait_ge(self.qkv_out, 3 * i + 5)
            for a in range(3):
                v.tensor_tensor(prod[:, a], qkv[:, u, a:a + 1, 0:D].to_broadcast([P, 3, D]), qkv[:, u, :, D:2 * D], ALU.mult)
            dve.drain()
            sc, ex, mx = self.sc, self.ex, self.mx
            v.tensor_reduce(sc[:].rearrange("p a b h -> p (a b h)"), prod[:].rearrange("p a b (h d) -> p (a b h) d", h=WH), X, ALU.add)
            dve.drain()
            v.tensor_reduce(mx[:], sc[:].rearrange("p a b h -> p a h b"), X, ALU.max)
            dve.drain()
            v.tensor_tensor(sc[:], sc[:], mx[:].unsqueeze(2).to_broadcast([P, 3, 3, WH]), ALU.subtract).then_inc(self.w_sc, 1)
            dve.wait_ge(self.w_ex, i + 1)
            v.tensor_reduce(mx[:], ex[:].rearrange("p a b h -> p a h b"), X, ALU.add)
            dve.drain()
            v.reciprocal(mx[:], mx[:])
            dve.drain()
            v.tensor_tensor(ex[:], ex[:], mx[:].unsqueeze(2).to_broadcast([P, 3, 3, WH]), ALU.mult)
            dve.drain()
            for a in range(3):
                v.tensor_tensor(prod[:, a].rearrange("p b (h d) -> p b h d", h=WH),
                                qkv[:, u, :, 2 * D:3 * D].rearrange("p b (h d) -> p b h d", h=WH),
                                ex[:, a].unsqueeze(3).to_broadcast([P, 3, WH, WHD]), ALU.mult)
            dve.drain().then_inc(self.qkv_free, 1)
            dve.wait_ge(self.o_T, i)
            v.tensor_tensor(self.ob[:], prod[:, :, 0], prod[:, :, 1], ALU.add)
            dve.drain()
            v.tensor_tensor(self.ob[:], self.ob[:], prod[:, :, 2], ALU.add).then_inc(self.w_o, 1)
        run_slots(dve, NWT, 3, slot)

        gall, g12, acc = self.gall, self.g12, self.accT
        dve.wait_ge(self.s["base_ld"], 16)
        dve.wait_ge(self.gelu_set, 1)
        for h in range(2):
            v.tensor_tensor(g12[:, h].rearrange("p (v u) b -> p v u b", u=5), gall[:, h, 48:63].rearrange("p (v u) b -> p v u b", u=5),
                            gall[:, h, 63:66].unsqueeze(2).to_broadcast([H2, 3, 5, B]), ALU.add)
        dve.drain()
        starts = [next(t for t in range(T) if t * 15 // T == u) for u in range(15)] + [2 * TT]
        for u in range(15):
            a, b = starts[u], starts[u + 1]
            dve.wait_ge(self.gelu_set, 2 + min((b - 2) // 16, 2))
            for lo, hi, src in (((0, 1, 0), (1, b, 0)) if u == 0 else ((a, b, a - 1),)):
                n = hi - lo
                v.tensor_tensor(acc[:, :, lo:hi], gall[:, :, src:src + n], g12[:, :, u:u + 1].to_broadcast([H2, 2, n, B]), ALU.add)
        dve.drain().then_inc(self.acc_set, 1)

        def mix(item):
            i, u, _ = item(0)
            dve.wait_ge(self.mix_mm, i + 1)
            row = self.hall[:, bass.ds(i, 1), :].rearrange("p o d -> p (o d)")
            v.tensor_tensor(row, row, self.pp[:, u, 0:D], ALU.add).then_inc(self.h2_set, 1)
        run_slots(dve, TT, 1, mix)

    def sync(self, sp, bs_st, last):
        for n in range(4):
            sp.wait_ge(bs_st[n], 112)
        sp.dma_start(self.hall[:, 0:TT], self.base_d.rearrange("(i t) b d -> (t b) i d", t=2)).then_inc(self.s["base_ld"], 16)
        for g in range(5):
            sp.wait_ge(self.h2_set, 5 * g + 5)
            for q in range(2):
                dst = self.h2_d.rearrange("b (i t) d -> t b i d", t=2)[q, :, 5 * g:5 * g + 5, :]
                sp.dma_start(dst, self.hall[q * B:(q + 1) * B, 5 * g:5 * g + 5]).then_inc(self.s["h2_st"], 16)
        sp.wait_ge(self.s["h2_st"], 160)


class Heads:

    def __init__(self, nc, ctx, sb, sem, A, const, ones, colg, x2, kbd, hall, h2_d, xs_d, yy_d, out, pe1, pt1, pp, s):
        self.nc, self.A, self.const, self.ones, self.colg, self.x2, self.kbd, self.hall = nc, A, const, ones, colg, x2, kbd, hall
        self.h2_d, self.xs_d, self.yy_d, self.out = h2_d, xs_d, yy_d, out
        self.pe1, self.pt1, self.pp, self.s = pe1, pt1, pp, s
        self.wqk = sb("wqk", [H2 + 1, 2, 3 * D])
        self.wproj = sb("wproj", [H2 + 1, 2, D])
        self.wgate = sb("wgate", [H2, 2, E])
        self.n2 = sb("n2", [P, 2, D])
        self.gates = sb("gates", [P, NP, 2])
        self.egs = sb("egs", [P, NP])
        self.meta = sb("meta", [1, 3, NT], I32)
        self.w1s = sb("w1s", [H2, E, 2 * HID])
        self.w2s = sb("w2s", [P, E, HC * D])
        self.b1s = sb("b1s", [P, E, HC])
        self.b2s = sb("b2s", [P, E, D])
        own = ExitStack()
        self.st = sb("st", [P, 32], to=own)
        self.bn = sb("bn", [P, 2, 6], to=own)
        self.xh2 = sb("xh2", [P, D], to=own)
        self.xT2 = sb("xT2", [H2 + 1, 2, P], to=own)
        self.qT = sb("qT", [H2, 2, P], to=own)
        self.vbd = sb("vbd", [P, 2, 6, 2 * (AHD + 1)], to=own)
        self.pm = sb("pm", [P, AH, B], to=own)
        self.mx2 = sb("mx2", [P, AH], to=own)
        self.pT = sb("pT", [P, 6, P], to=own)
        self.on = sb("on", [P, D], to=own)
        self.onT = sb("onT", [H2 + 1, 2, P], to=own)
        self.xn = sb("xn", [P, 2, D], to=own)
        self.xsrc = sb("xsrc", [P, 2, 2, DX], to=own)
        self.xnT2 = sb("xnT2", [H2, 2, P], to=own)
        self.lg = sb("lg", [P, E], to=own)
        self.m8 = sb("m8", [P, E], to=own)
        self.i8 = sb("i8", [P, E], U32, to=own)
        self.idx = sb("idx", [P, 2], to=own)
        self.oh = sb("oh", [P, 2, E], to=own)
        self.ohs = sb("ohs", [P, E], to=own)
        self.acc = sb("acc", [P, E], to=own)
        self.t8 = sb("t8", [P, 3, E], to=own)
        self.df = sb("df", [P, 2], to=own)
        self.dst = sb("dst", [P, 2, 2], I32, to=own)
        self.zero = sb("zero", [P, DX], to=own)
        self.mf = sb("mf", [P, 6, NT * E], to=own)
        self.nf = sb("nf", [P, 4, E], to=own)
        own.close()
        self.yl = x2[:].rearrange("p (a i k) d -> p a i k d", a=4, i=4)
        self.xdum = sb("xdum", [P, 2])
        self.yixs = sb("yixs", [P, NT], I32)
        self.yix = sb("yix", [P, 2], I32)
        self.w1 = sb("ew1", [H2, 2, 2, HID])
        self.b1 = sb("eb1", [P, 2, HC])
        self.xs = sb("xs", [P, 2, DX])
        self.xsT = sb("xsT", [H2, 2, ROWS])
        self.hT = sb("hT", [P, 2, HC, ROWS])
        self.ys = sb("ys", [P, 2, D])
        self.a_var, self.a_r, self.a_x, self.a_T, self.a_xT = sem("a_var"), sem("a_r"), sem("a_x"), sem("a_T"), sem("a_xT")
        self.a_qkv, self.a_q, self.a_v, self.a_k, self.b_s, self.b_sub = sem("a_qkv"), sem("a_q"), sem("a_v"), sem("a_k"), sem("b_s"), sem("b_sub")
        self.b_ex, self.b_pT, self.b_pTo, self.b_pv, self.b_on = sem("b_ex"), sem("b_pT"), sem("b_pTo"), sem("b_pv"), sem("b_on")
        self.c_T, self.c_out, self.c_proj, self.c_var, self.c_r = sem("c_T"), sem("c_out"), sem("c_proj"), sem("c_var"), sem("c_r")
        self.c_xn, self.c_nT, self.d_out, self.d_lg, self.d_oh = sem("c_xn"), sem("c_nT"), sem("d_out"), sem("d_lg"), sem("d_oh")
        self.d_rank, self.d_eg, self.d_dst, self.d_src = sem("d_rank"), sem("d_eg"), sem("d_dst"), sem("d_src")
        self.h_ld, self.hw_ld, self.init, self.tot, self.meta_set = sem("h_ld"), sem("hw_ld"), sem("init"), sem("tot"), sem("meta_set")
        self.zero_st, self.e_T, self.e_xT, self.e_h, self.e_g = sem("zero_st"), sem("e_T"), sem("e_xT"), sem("e_h"), sem("e_g")
        self.e_y, self.e_out, self.h_zero, self.y_free, self.dum_set = sem("e_y"), sem("e_out"), sem("h_zero"), sem("y_free"), sem("dum_set")
        self.o_st, self.res_set, self.d_lgo, self.xs_used, self.o_set = sem("o_st"), sem("res_set"), sem("d_lgo"), sem("xs_used"), sem("o_set")
        self.scat = [sem("scat0"), sem("scat1")]
        self.e_w = [sem("e_w0"), sem("e_w1")]
        self.ew_ld, self.e_wc = sem("ew_ld"), sem("e_wc")
        self.e_st = [sem("e_st0"), sem("e_st1")]
        self.y_ld = [sem(f"y_ld{n}") for n in range(4)]

    def gpsimd(self, pool):
        nc, st, g = self.nc, self.st, self.nc.gpsimd
        pool.wait_ge(self.init, 2)
        eps, mhalf = self.const[:, C_EPS:C_EPS + 1], self.const[:, C_NH:C_NH + 1]

        def slot(item):
            a, c, d = item(0), item(3), item(6)
            if a:
                i = a[0]
                pool.wait_ge(self.a_var, i + 1)
                g.tensor_tensor(st[:, 2:3], st[:, 1:2], eps, ALU.add)
                pool.drain()
                g.tensor_tensor(st[:, 2:3], st[:, 2:3], mhalf, ALU.pow)
                pool.drain()
                g.tensor_tensor(st[:, 3:4], st[:, 1:2], st[:, 2:3], ALU.mult)
                pool.drain()
                g.tensor_tensor(st[:, 3:4], st[:, 3:4], st[:, 2:3], ALU.mult)
                pool.drain()
                g.tensor_tensor(st[:, 3:4], st[:, 3:4], eps, ALU.add)
                pool.drain()
                g.tensor_tensor(st[:, 3:4], st[:, 3:4], mhalf, ALU.pow).then_inc(self.a_r, 1)
            if c:
                i = c[0]
                pool.wait_ge(self.c_var, i + 1)
                g.tensor_tensor(st[:, 8:9], st[:, 7:8], eps, ALU.add)
                pool.drain()
                g.tensor_tensor(st[:, 8:9], st[:, 8:9], mhalf, ALU.pow).then_inc(self.c_r, 1)
                rows = [t[:, bass.ds(i, 1), :].rearrange("p o d -> p (o d)") for t in (self.hall, self.x2)]
                g.tensor_tensor(rows[0], rows[0], rows[1], ALU.add).then_inc(self.res_set, 1)
            if d:
                i, u, _ = d
                pool.wait_ge(self.d_src, i + 2)
                pool.wait_ge(self.d_dst, i + 1)
                g.tensor_copy(self.xsrc[:, u, :, D:DX], self.const[:, C_ROW:C_ROW + 2 * NP].rearrange("p (i k) -> p i k", k=2)[:, bass.ds(i, 1), :].rearrange("p o k -> p k o"))
                pool.drain()
                for k in range(2):
                    g.indirect_dma_start(self.xs_d[:, :], bass.IndirectOffsetOnAxis(ap=self.dst[:, u, k:k + 1], axis=0),
                                         self.xsrc[:, u, k], None, bounds_check=E * R - 1, oob_is_err=False).then_inc(self.scat[u], 16)
        run_slots(pool, NP, 7, slot)

        held = self.xdum[:, 0:1], self.xdum[:, 1:2]

        def expert(item):
            if (a := item(4)):
                i, u, h = a
                pool.drain()
                pool.wait_ge(self.e_out, i + 1)
                pool.wait_ge(self.e_st[u], 16 * h)
                g.tensor_tensor(held[0], held[1], held[1], ALU.add)
                g.tensor_copy(self.yix[:, u:u + 1], self.yixs[:, bass.ds(i, 1)])
                pool.drain()
                g.indirect_dma_start(self.yy_d[:, :], bass.IndirectOffsetOnAxis(ap=self.yix[:, u:u + 1], axis=0),
                                     self.ys[:, u], None, bounds_check=2 * NP * P - 1, oob_is_err=False).then_inc(self.e_st[u], 16)
            if (b := item(1)):
                i, u, h = b
                pool.drain()
                pool.wait_ge(self.e_w[u], 16 * h + 16)
                g.tensor_tensor(held[0], held[1], held[1], ALU.add)
                g.tensor_copy(self.yixs[:, bass.ds(i, 1)], self.xs[:, u, D:DX]).then_inc(self.xs_used, 1)
        pool.wait_ge(self.dum_set, 1)
        run_slots(pool, NT, 5, expert)

    def vector(self, dve):
        nc, v, st, const, hall, x2 = self.nc, self.nc.vector, self.st, self.const, self.hall, self.x2
        pe1, pp = self.pe1, self.pp
        dve.wait_ge(self.s["h2_st"], 160)
        dve.drain()
        v.memset(self.pm[:], 0.0)
        v.memset(self.vbd[:], 0.0)
        dve.drain()
        v.memset(self.vbd[0:T, :, :, AHD:AHD + 1], 1.0)
        v.memset(self.vbd[B:B + T, :, :, 2 * AHD + 1:2 * AHD + 2], 1.0)
        v.memset(self.acc[:], 0.0)
        v.memset(self.xT2[H2:H2 + 1, 1], 1.0)
        v.memset(self.onT[H2:H2 + 1, 1], 1.0)
        v.memset(self.zero[:], 0.0)
        v.memset(hall[:], 0.0)
        dve.drain()
        v.memset(self.zero[:, D:DX], float(FAR))
        dve.drain().then_inc(self.init, 2)
        dve.drain().then_inc(self.e_T, 2)
        dve.drain().then_inc(self.y_free, 2)
        dve.drain().then_inc(self.e_g, 4)
        dve.drain().then_inc(self.xs_used, 2)
        dve.drain().then_inc(self.d_src, 1)
        dve.wait_ge(self.h_ld, 64)
        dve.wait_ge(self.hw_ld, 16 * 7)

        def row(t, i):
            return t[:, bass.ds(i, 1), :].rearrange("p o d -> p (o d)")

        def stats(src, k, bnk):
            v.bn_stats(self.bn[:, bnk], src)
            dve.drain()
            v.bn_aggr(st[:, k:k + 2], self.bn[:, bnk])

        def slot(item):
            n0, n1, n2, n3, n4, n6 = (item(lag) and item(lag)[0] for lag in (0, 1, 2, 3, 4, 6))
            if n4 is not None:
                xn = self.xn[:, item(4)[1]]
            lg = self.lg
            dve.drain()
            if n6 is not None:
                dve.wait_ge(self.d_lg, n6 + 1)
                v.tensor_copy(lg[:], pe1[:, 3, 256:256 + E]).then_inc(self.d_lgo, 1)
            if n4 is not None:
                dve.wait_ge(self.c_r, n4 + 1)
                dve.wait_ge(self.d_src, n4)
                v.tensor_scalar(xn, row(x2, n4), st[:, 6:7], st[:, 8:9], ALU.subtract, ALU.mult)
            dve.drain()
            if n6 is not None:
                v.max(self.m8[:], lg[:])
            if n4 is not None:
                v.tensor_tensor(xn, xn, self.n2[:, 0], ALU.mult)
            dve.drain()
            if n6 is not None:
                v.max_index(self.i8[:], self.m8[:], lg[:])
                dve.wait_ge(self.d_eg, n6)
                v.tensor_tensor(st[:, 12:13], self.m8[:, 1:2], self.m8[:, 0:1], ALU.subtract)
            if n4 is not None:
                v.tensor_tensor(xn, xn, self.n2[:, 1], ALU.add).then_inc(self.c_xn, 1)
            if n0 is not None:
                v.bn_stats(self.bn[:, 0], row(hall, n0))
            dve.drain()
            if n6 is not None:
                v.tensor_copy(self.idx[:], self.i8[:, 0:2])
            if n0 is not None:
                v.bn_aggr(st[:, 0:2], self.bn[:, 0]).then_inc(self.a_var, 1)
            if n2 is not None:
                dve.wait_ge(self.b_s, n2 + 1)
                sc = pe1[:, 0:2, 0:6 * T].rearrange("p n (h k) -> p n h k", h=6)
                v.tensor_reduce(self.mx2[:].rearrange("p (n h) -> p n h", n=2), sc, X, ALU.max)
            dve.drain()
            if n2 is not None:
                v.tensor_tensor(self.pm[:].rearrange("p (n h) k -> p n h k", n=2)[:, :, :, 0:T], sc,
                                self.mx2[:].rearrange("p (n h) -> p n h", n=2).unsqueeze(3).to_broadcast([P, 2, 6, T]),
                                ALU.subtract).then_inc(self.b_sub, 1)
            if n6 is not None:
                for k in range(2):
                    v.tensor_scalar(self.oh[:, k], const[:, C_EI:C_EI + E], self.idx[:, k:k + 1], const[:, C_VAL:C_VAL + 1],
                                    ALU.is_equal, ALU.mult)
                dve.drain()
                v.tensor_tensor(self.ohs[:], self.oh[:, 0], self.oh[:, 1], ALU.add).then_inc(self.d_oh, 1)
            if n1 is not None:
                dve.wait_ge(self.a_qkv, n1 + 1)
                for m in range(2):
                    for h in range(2):
                        k = pp[0:H2, 1, h * P + m * B:h * P + m * B + T].unsqueeze(1).to_broadcast([H2, 6, T])
                        last = v.tensor_tensor(self.kbd[:, m, h], k, const[0:H2, C_KM:C_KM + 6].unsqueeze(2).to_broadcast([H2, 6, T]), ALU.mult)
                last.then_inc(self.a_k, 1)
            if n0 is not None:
                dve.wait_ge(self.a_r, n0 + 1)
                v.tensor_scalar(row(x2, n0), row(hall, n0), st[:, 0:1], st[:, 2:3], ALU.subtract, ALU.mult)
            dve.drain()
            if n0 is not None:
                v.tensor_scalar(self.xh2[:], row(x2, n0), st[:, 3:4], None, ALU.mult).then_inc(self.a_x, 1)
            if n3 is not None:
                dve.wait_ge(self.c_proj, n3 + 1)
                v.tensor_tensor(row(x2, n3), row(x2, n3), pe1[:, 2, 256:256 + D], ALU.add)
                dve.drain()
                v.bn_stats(self.bn[:, 1], row(x2, n3))
            o = pe1[:, 1, 0:AH * (AHD + 1)].rearrange("p (h d) -> p h d", h=AH)
            if n2 is not None:
                dve.wait_ge(self.b_pv, n2 + 1)
                v.reciprocal(self.mx2[:], o[:, :, AHD:AHD + 1].rearrange("p h o -> p (h o)"))
            dve.drain()
            if n2 is not None:
                v.tensor_tensor(self.on[:].rearrange("p (h d) -> p h d", h=AH), o[:, :, 0:AHD],
                                self.mx2[:].unsqueeze(2).to_broadcast([P, AH, AHD]), ALU.mult).then_inc(self.b_on, 1)
            if n3 is not None:
                v.bn_aggr(st[:, 6:8], self.bn[:, 1]).then_inc(self.c_var, 1)
            if n6 is not None:
                dve.wait_ge(self.d_rank, n6 + 1)
                t = self.t8
                v.tensor_tensor(t[:, 0], self.pt1[:, 1, 0:E], const[:, C_ER:C_ER + E], ALU.add)
                v.tensor_tensor(self.acc[:], self.acc[:], self.ohs[:], ALU.add)
                dve.drain()
                v.tensor_tensor(t[:, 1:3], self.oh[:], t[:, 0:1].to_broadcast([P, 2, E]), ALU.mult)
                dve.drain()
                v.tensor_reduce(self.df[:], t[:, 1:3], X, ALU.add)
                dve.drain()
                v.tensor_scalar(self.dst[:, item(6)[1]], self.df[:], const[:, C_VAL + 1:C_VAL + 2], None, ALU.add).then_inc(self.d_dst, 1)
        run_slots(dve, NP, 7, slot)

        dve.drain().then_inc(self.tot, 1)
        dve.wait_ge(self.tot, 2)
        nf, mf = self.nf, self.mf
        cnt, cnt256, nt, cum = (nf[:, n] for n in range(4))
        ge = mf[:, 0].rearrange("p (j e) -> p j e", e=E)
        js, ers = const[:, C_J:C_J + NT], const[:, C_ER:C_ER + E]
        v.tensor_copy(cnt, pe1[:, 3, 0:E])
        dve.drain()
        v.tensor_scalar(cnt256, cnt, 1 / ROWS, None, ALU.mult)
        dve.drain()
        ng = NT // 2
        gt = mf[:, 1, 0:E * ng].rearrange("p (e m) -> p e m", e=E)
        v.tensor_tensor(gt, cnt256.unsqueeze(2).to_broadcast([P, E, ng]), js[:, 0:ng].unsqueeze(1).to_broadcast([P, E, ng]), ALU.is_gt)
        dve.drain()
        v.tensor_reduce(nt, gt, X, ALU.add)
        dve.drain()
        pr = mf[:, 2, 0:E * E].rearrange("p (e f) -> p e f", e=E)
        v.tensor_tensor(pr, const[:, C_L8:C_L8 + E * E].rearrange("p (e f) -> p e f", e=E), nt.unsqueeze(1).to_broadcast([P, E, E]), ALU.mult)
        dve.drain()
        v.tensor_reduce(cum, pr, X, ALU.add)
        dve.drain()
        v.tensor_tensor(ge, js.unsqueeze(2).to_broadcast([P, NT, E]), cum.unsqueeze(1).to_broadcast([P, NT, E]), ALU.is_ge)
        dve.drain()
        te, tl = mf[:, 3, 0:NT], mf[:, 4, 0:NT]
        v.tensor_reduce(te, ge, X, ALU.add)
        v.tensor_tensor(mf[:, 5].rearrange("p (j e) -> p j e", e=E), ge, nt.unsqueeze(1).to_broadcast([P, NT, E]), ALU.mult)
        dve.drain()
        v.tensor_reduce(tl, mf[:, 5].rearrange("p (j e) -> p j e", e=E), X, ALU.add)
        dve.drain()
        v.tensor_tensor(tl, js, tl, ALU.subtract)
        dve.drain()
        v.tensor_scalar(tl, tl, float(ROWS), None, ALU.mult)
        dve.drain()
        v.scalar_tensor_tensor(tl, te, float(R), tl, ALU.mult, ALU.add)
        dve.drain()
        v.tensor_scalar(self.meta[:, 0], te[0:1], float(E - 1), None, ALU.min)
        v.tensor_scalar(self.meta[:, 1], tl[0:1], float(E * R), None, ALU.min)
        v.tensor_tensor(self.meta[:, 2, 0:E], cnt[0:1], ers[0:1], ALU.add)
        dve.drain().then_inc(self.meta_set, 1)
        dve.wait_ge(self.d_eg, NP)
        g1, g2 = self.gates[:, :, 0], self.gates[:, :, 1]
        v.tensor_scalar(g1, self.egs[:], 1.0, None, ALU.add)
        dve.drain()
        v.reciprocal(g1, g1)
        dve.drain()
        v.tensor_tensor(g2, g1, self.egs[:], ALU.mult)
        for n in range(2):
            dve.wait_ge(self.scat[n], 16 * NP)
        v.memset(self.xdum[:], 0.0).then_inc(self.dum_set, 1)

        dve.wait_ge(self.ew_ld, 16 * 4)

        def expert(item):
            if (a := item(1)):
                i, u, h = a
                e = dve.value_load(self.meta[0:1, 0, bass.ds(i, 1)], min_val=0, max_val=E - 1)
                dve.wait_ge(self.e_g, 2 * i + 2)
                v.tensor_copy(self.b1[:, u], self.b1s[:, bass.ds(e, 1), :].rearrange("p o c -> p (o c)"))
                v.tensor_copy(self.w1[:, u].rearrange("p h f -> p (h f)"), self.w1s[:, bass.ds(e, 1), :].rearrange("p o f -> p (o f)"))
                dve.drain().then_inc(self.e_wc, 1)
            if (c := item(3)):
                i, u, h = c
                e = dve.value_load(self.meta[0:1, 0, bass.ds(i, 1)], min_val=0, max_val=E - 1)
                dve.wait_ge(self.e_y, i + 1)
                dve.wait_ge(self.e_st[u], 16 * h)
                v.tensor_tensor(self.ys[:, u], pp[:, u, 0:D], self.b2s[:, bass.ds(e, 1), :].rearrange("p o d -> p (o d)"), ALU.add).then_inc(self.e_out, 1)
                dve.drain().then_inc(self.y_free, 1)
        run_slots(dve, NT, 5, expert)

        dve.wait_ge(self.res_set, NP)
        for n in range(NP // 4):
            dve.wait_ge(self.y_ld[n % 4], 32 * (n // 4) + 32)
            for k in range(2):
                for i in range(4):
                    m = 4 * n + i
                    v.scalar_tensor_tensor(hall[:, m], self.yl[:, n % 4, i, k], self.gates[:, m, k:k + 1], hall[:, m], ALU.mult, ALU.add)
                dve.drain()
            dve.drain().then_inc(self.o_set, 1)

    def scalar(self, act):
        nc, f, pe1, pt1, pp, colg = self.nc, self.nc.scalar.activation, self.pe1, self.pt1, self.pp, self.colg
        act.wait_ge(self.init, 2)

        def slot(item):
            n0, n1, n2, n5, n6 = (item(lag) and item(lag)[0] for lag in (0, 1, 2, 5, 6))
            if n2 is not None:
                act.wait_ge(self.b_sub, n2 + 1)
                f(self.pm[:, :, 0:T], self.pm[:, :, 0:T], ACT.Exp, scale=AHD ** -0.5).then_inc(self.b_ex, 1)
            if n1 is not None:
                act.wait_ge(self.a_qkv, n1 + 1)
                f(self.qT[:], pp[0:H2, 0, 0:2 * P].rearrange("p (h n) -> p h n", h=2), ACT.Copy).then_inc(self.a_q, 1)
            if n5 is not None:
                u = item(5)[1]
                act.wait_ge(self.c_xn, n5 + 1)
                act.wait_ge(self.scat[u], 32 * item(5)[2])
                f(self.xsrc[:, u, :, 0:D], self.xn[:, u:u + 1].to_broadcast([P, 2, D]), ACT.Copy).then_inc(self.d_src, 1)
            if n5 is not None:
                act.wait_ge(self.c_nT, n5 + 1)
                f(self.xnT2[:], pe1[0:H2, 3, 0:2 * P].rearrange("p (h n) -> p h n", h=2), ACT.Copy).then_inc(self.d_out, 1)
            if n2 is not None:
                act.wait_ge(self.b_pT, n2 + 1)
                f(self.pT[:, 0:4].rearrange("p h n -> p (h n)"), pe1[:, 0], ACT.Copy)
                f(self.pT[:, 4:6].rearrange("p h n -> p (h n)"), pe1[:, 1, 0:2 * P], ACT.Copy).then_inc(self.b_pTo, 1)
            if n6 is not None:
                act.wait_ge(self.d_oh, n6 + 1)
                f(self.egs[:, bass.ds(n6, 1)], self.st[:, 12:13], ACT.Exp).then_inc(self.d_eg, 1)
            if n0 is not None:
                act.wait_ge(self.a_T, n0 + 1)
                for h in range(2):
                    last = f(self.xT2[0:H2, h], pt1[0:H2, 0, h * P:(h + 1) * P], ACT.Identity, bias=colg[:, h, 4:5], scale=colg[:, h, 3:4])
                last.then_inc(self.a_xT, 1)
            if n1 is not None:
                act.wait_ge(self.b_pv, n1)
                for m in range(2):
                    for e in range(2):
                        src = pp[m * B:m * B + T, 0, 256:256 + D].rearrange("p (h e d) -> p h e d", e=2, d=AHD)[:, :, e]
                        last = f(self.vbd[e * B:e * B + T, m, :, e * (AHD + 1):e * (AHD + 1) + AHD], src, ACT.Copy)
                last.then_inc(self.a_v, 1)
            if n2 is not None:
                act.wait_ge(self.c_T, n2 + 1)
                f(self.onT[0:H2], pe1[0:H2, 2, 0:2 * P].rearrange("p (h n) -> p h n", h=2), ACT.Copy).then_inc(self.c_out, 1)
        run_slots(act, NP, 7, slot)

        def expert(item):
            if not (b := item(1)):
                return
            i, u, h = b
            act.wait_ge(self.e_T, i + 3)
            f(self.xsT[:], pt1[0:H2, u, 0:2 * ROWS].rearrange("p (h n) -> p h n", h=2), ACT.Copy).then_inc(self.e_xT, 1)

        def hidden(item):
            if not (b := item(2)):
                return
            i, u, h = b
            act.wait_ge(self.e_wc, i + 1)
            act.wait_ge(self.y_free, i + 1)
            for c in range(HC):
                if c % 3 == 0:
                    act.wait_ge(self.e_h, 2 * i + c // 3 + 1)
                last = f(self.hT[:, u, c], pe1[:, 2 * u + c // 3, (c % 3) * ROWS:(c % 3 + 1) * ROWS], ACT.Gelu, bias=self.b1[:, u, c:c + 1])
                if c % 3 == 2:
                    last.then_inc(self.e_g, 1)

        def both(item):
            hidden(item)
            expert(item)
        run_slots(act, NT, 5, both)

    def tensor(self, pe):
        nc, mm, T_, pe1, pt1, pp = self.nc, self.nc.tensor.matmul, self.nc.tensor.transpose, self.pe1, self.pt1, self.pp
        ident, const = self.const[:, C_ID:C_ID + P], self.const
        pe.wait_ge(self.init, 2)
        pe.wait_ge(self.hw_ld, 16 * 7)

        def slot(item):
            n0, n1, n2, n3, n5, n6 = (item(lag) and item(lag)[0] for lag in (0, 1, 2, 3, 5, 6))
            if n2 is not None:
                pe.wait_ge(self.a_q, n2 + 1)
                pe.wait_ge(self.a_k, n2 + 1)
                pe.wait_ge(self.b_on, n2)
                for m in range(2):
                    for h in range(2):
                        last = mm(pe1[m * B:(m + 1) * B, h, 0:6 * T], self.qT[:, h, m * B:(m + 1) * B],
                                  self.kbd[:, m, h].rearrange("p h k -> p (h k)"), start=True, stop=True)
                last.then_inc(self.b_s, 1)
            if n1 is not None:
                pe.wait_ge(self.a_xT, n1 + 1)
                pe.wait_ge(self.a_v, n1)
                pe.wait_ge(self.a_k, n1)
                for g in range(2):
                    for m in range(2):
                        for h in range(2):
                            rows = H2 + h
                            mm(pp[0:H2, g, m * P:(m + 1) * P], self.wqk[0:rows, h, g * D + m * H2:g * D + (m + 1) * H2],
                               self.xT2[0:rows, h], start=(h == 0), stop=(h == 1))
                for h in range(2):
                    last = mm(pp[:, 0, 256:256 + D], self.xT2[0:H2 + h, h], self.wqk[0:H2 + h, h, 2 * D:3 * D], start=(h == 0), stop=(h == 1))
                last.then_inc(self.a_qkv, 1)
            if n5 is not None:
                pe.wait_ge(self.c_xn, n5 + 1)
                pe.wait_ge(self.d_lgo, n5)
                for h in range(2):
                    last = T_(pe1[0:H2, 3, h * P:(h + 1) * P], self.xn[:, item(5)[1], h * H2:(h + 1) * H2], ident)
                last.then_inc(self.c_nT, 1)
            if n2 is not None:
                pe.wait_ge(self.b_ex, n2 + 1)
                for n in range(6):
                    last = T_(pe1[:, n // 4, (n % 4) * P:(n % 4 + 1) * P], self.pm[:, 2 * n:2 * n + 2].rearrange("p h k -> p (h k)"), ident)
                last.then_inc(self.b_pT, 1)
            if n3 is not None:
                pe.wait_ge(self.c_out, n3 + 1)
                mm(pe1[:, 2, 256:256 + D], self.onT[0:H2, 0], self.wproj[0:H2, 0], start=True, stop=False)
                mm(pe1[:, 2, 256:256 + D], self.onT[:, 1], self.wproj[:, 1], start=False, stop=True).then_inc(self.c_proj, 1)
            if n5 is not None:
                pe.wait_ge(self.d_out, n5 + 1)
                for h in range(2):
                    last = mm(pe1[:, 3, 256:256 + E], self.xnT2[:, h], self.wgate[:, h], start=(h == 0), stop=(h == 1))
                last.then_inc(self.d_lg, 1)
            if n2 is not None:
                pe.wait_ge(self.b_pTo, n2 + 1)
                pe.wait_ge(self.a_v, n2 + 1)
                w = 2 * (AHD + 1)
                for m in range(2):
                    for n in range(6):
                        last = mm(pe1[m * B:(m + 1) * B, 1, n * w:(n + 1) * w], self.pT[:, n, m * B:(m + 1) * B], self.vbd[:, m, n], start=True, stop=True)
                last.then_inc(self.b_pv, 1)
            if n0 is not None:
                pe.wait_ge(self.a_x, n0 + 1)
                pe.wait_ge(self.a_xT, n0)
                for h in range(2):
                    last = T_(pt1[0:H2, 0, h * P:(h + 1) * P], self.xh2[:, h * H2:(h + 1) * H2], ident)
                last.then_inc(self.a_T, 1)
            if n6 is not None:
                pe.wait_ge(self.d_oh, n6 + 1)
                pe.wait_ge(self.d_dst, n6)
                mm(pt1[:, 1, 0:E], self.ones[:], self.acc[:], start=True, stop=False)
                mm(pt1[:, 1, 0:E], const[:, C_TRI:C_TRI + P], self.ohs[:], start=False, stop=True).then_inc(self.d_rank, 1)
            if n2 is not None:
                pe.wait_ge(self.b_on, n2 + 1)
                pe.wait_ge(self.c_var, n2)
                for h in range(2):
                    last = T_(pe1[0:H2, 2, h * P:(h + 1) * P], self.on[:, h * H2:(h + 1) * H2], ident)
                last.then_inc(self.c_T, 1)
        run_slots(pe, NP, 7, slot)
        pe.wait_ge(self.tot, 1)
        mm(pe1[:, 3, 0:E], self.ones[:], self.acc[:], start=True, stop=True).then_inc(self.tot, 1)
        pe.wait_ge(self.meta_set, 1)

        def expert(item):
            if (b := item(2)):
                i, u, h = b
                pe.wait_ge(self.e_xT, i + 1)
                pe.wait_ge(self.e_wc, i + 1)
                for n in range(HC):
                    for m in range(2):
                        last = mm(pe1[:, 2 * u + n // 3, (n % 3) * ROWS:(n % 3 + 1) * ROWS], self.w1[:, u, m, n * P:(n + 1) * P], self.xsT[:, m], start=(m == 0), stop=(m == 1))
                    if n % 3 == 2:
                        last.then_inc(self.e_h, 1)
            if (a := item(1)):
                i, u, h = a
                pe.wait_ge(self.e_w[u], 16 * h + 16)
                for n in range(2):
                    last = T_(pt1[0:H2, u, n * ROWS:(n + 1) * ROWS], self.xs[:, u, n * H2:(n + 1) * H2], ident)
                last.then_inc(self.e_T, 1)
            if (c := item(3)):
                i, u, h = c
                e = pe.value_load(self.meta[0:1, 0, bass.ds(i, 1)], min_val=0, max_val=E - 1)
                pe.wait_ge(self.e_g, 2 * i + 6)
                pe.wait_ge(self.y_free, i + 1)
                for n in range(HC):
                    last = mm(pp[:, u, 0:D], self.hT[:, u, n], self.w2s[:, bass.ds(e, 1), n * D:(n + 1) * D].rearrange("p o d -> p (o d)"), start=(n == 0), stop=(n == HC - 1))
                last.then_inc(self.e_y, 1)
        pe.wait_ge(self.ew_ld, 16 * 4)
        run_slots(pe, NT, 5, expert)

    def sync(self, sp):
        A, hall = self.A, self.hall
        sp.wait_ge(self.init, 2)
        for dst, src in ((self.wqk[0:H2], A["qkvT"]), (self.wqk[H2:H2 + 1, 1], A["qkvb"]), (self.wproj[0:H2], A["projT"]),
                         (self.wproj[H2:H2 + 1, 1], A["projb"]), (self.wgate[:], A["wgate"]), (self.n2[:, 0], A["n2"][0:1].to_broadcast([P, D])),
                         (self.n2[:, 1], A["n2"][1:2].to_broadcast([P, D]))):
            sp.dma_start(dst, src).then_inc(self.hw_ld, 16)
        for q in range(2):
            src = self.h2_d.rearrange("(i q) t d -> q t i d", q=2)[q, 0:T]
            for g in range(2):
                sp.dma_start(hall[q * B:q * B + T, 16 * g:16 * g + 16], src[:, 16 * g:16 * g + 16]).then_inc(self.h_ld, 16)
        sp.dma_start(self.xs_d[E * R:E * R + ROWS], self.zero[:]).then_inc(self.zero_st, 16)
        for dst, src in ((self.w1s[:], A["W1"].rearrange("e p h f -> p e (h f)")), (self.w2s[:], A["W2"].rearrange("e p c d -> p e (c d)")),
                         (self.b1s[:], A["b1"].rearrange("e p c -> p e c")),
                         (self.b2s[:].rearrange("p e d -> p (e d)"), A["b2"].rearrange("e d -> (e d)").unsqueeze(0).to_broadcast([P, E * D]))):
            sp.dma_start(dst, src).then_inc(self.ew_ld, 16)
        sp.wait_ge(self.meta_set, 1)
        for e in range(E):
            at = sp.value_load(self.meta[0:1, 2, e:e + 1], min_val=0, max_val=E * R - ROWS)
            sp.dma_start(self.xs_d[bass.ds(at, ROWS)], self.zero[:]).then_inc(self.zero_st, 16)
        for n in range(2):
            sp.wait_ge(self.scat[n], 16 * NP)
        sp.wait_ge(self.zero_st, 16 * (E + 1))
        sp.wait_ge(self.d_eg, NP)

        def slot(item):
            i, u, h = item(0)
            at = sp.value_load(self.meta[0:1, 1, bass.ds(i, 1)], min_val=0, max_val=E * R)
            sp.wait_ge(self.e_T, i + 1)
            sp.wait_ge(self.xs_used, i + 1)
            sp.dma_start(self.xs[:, u], self.xs_d[bass.ds(at, ROWS)]).then_inc(self.e_w[u], 16)
        run_slots(sp, NT, 1, slot)

        sp.wait_ge(self.dum_set, 1)
        for n in range(2):
            sp.wait_ge(self.e_st[n], (NT + 1 - n) // 2 * 16)

        def load(n):
            for q in range(2):
                src = self.yy_d.rearrange("(i q t k) d -> q t i k d", q=2, t=B, k=2)[q, 0:T, 4 * n:4 * n + 4]
                sp.dma_start(self.yl[q * B:q * B + T, n % 4], src).then_inc(self.y_ld[n % 4], 16)

        for n in range(4):
            load(n)
        for n in range(NP // 4):
            sp.wait_ge(self.o_set, n + 1)
            for q in range(2):
                dst = self.out.rearrange("(i q) t d -> q t i d", q=2)[q, :, 4 * n:4 * n + 4]
                sp.dma_start(dst, hall[q * B:q * B + T, 4 * n:4 * n + 4]).then_inc(self.o_st, 16)
            if n + 4 < NP // 4:
                load(n + 4)
        sp.wait_ge(self.o_st, 256)


def build(nc, A, out, stop=99):
    ctx = ExitStack()
    with ctx:
        def sem(name):
            return ctx.enter_context(nc.semaphore(name))

        def ps(name, shape):
            return ctx.enter_context(nc.psum_tensor(name, shape, F32))

        def sb(name, shape, dt=F32, to=None):
            return (to or ctx).enter_context(nc.sbuf_tensor(name, shape, dt))

        def dram(name, shape, dt=F32):
            return nc.dram_tensor(name, shape, dt, kind="Internal").ap()

        base_d = dram("base_d", [2 * TT, B, D])
        h2_d = dram("h2_d", [B, 2 * TT, D])
        xs_d = dram("xs_d", [NROW, DX])
        yy_d = dram("yy_d", [NP * P * 2, D])

        const = sb("const", [P, NCONST])
        ones = sb("ones", [P, P])
        ident = const[:, C_ID:C_ID + P]
        wqkv = sb("wqkv", [H2 + 1, 2, 3 * D])
        colg = sb("colg", [H2, 2, 5])
        mowT = sb("mowT", [H2, 2, D])
        owT = sb("owT", [H2 + 1, 2, D])

        e2 = ExitStack()
        x2 = sb("x2", [P, NP, D], to=e2)
        kbd = sb("kbd", [H2, 2, 2, 6, T], to=e2)
        e2.close()
        xnT = sb("xnT", [H2, 2, FRONT + POS, B])
        e1 = ExitStack()
        wm = sb("wm", [P, 4, KC, D + 1], to=e1)
        ww = sb("ww", [P, 6, D + 1], to=e1)
        s1b = sb("s1b", [P, D], to=e1)
        s2b = sb("s2b", [P, D], to=e1)
        cb = sb("cb", [P, D], to=e1)
        xm = sb("xm", [P, 2, 2, KC, NA], to=e1)
        x6 = sb("x6", [P, 4, KC, P], to=e1)
        raw = sb("raw", [P, 8 * NA + 8 * NB], to=e1)
        sqs = sb("sqs", [P, 2, 2, NA], to=e1)
        sq6 = sb("sq6", [P, 4, P], to=e1)
        xh = sb("xh", [P, 4, D], to=e1)
        bs = sb("bs", [P, 4, D], to=e1)
        hh = sb("hh", [P, D], to=e1)
        st1 = sb("st1", [P, 24], to=e1)
        bn1 = sb("bn1", [P, 6], to=e1)
        e0 = ExitStack()
        w1 = sb("w1", [P, 5, KC, D], to=e0)
        w2 = sb("w2", [P, 8, D], to=e0)
        gb = sb("gb", [P, 2, 38], to=e0)
        trow = sb("trow", [1, 2, D], to=e0)
        inw = sb("inw", [H2, 2, 3, D], to=e0)
        qkw = sb("qkw", [H2, 2, 3, D + 1], to=e0)
        inb = sb("inb", [H2 + 1, 3 * D], to=e0)
        e0.close()
        wv = sb("wv", [P, 2, 2 * NA + 2 * NB], to=e1)
        wsq = sb("wsq", [P, 2, 2 * NA + 2 * NB], to=e1)
        wv6 = sb("wv6", [P, 6 * P], to=e1)
        wsq6 = sb("wsq6", [P, 6 * P], to=e1)
        sqt = sb("sqt", [P, KC * NA], to=e1)
        e1.close()

        pe1 = ps("pe1", [P, 4, 512])
        pt1 = ps("pt1", [P, 2, 512])
        pp = ps("pp", [P, 2, 512])

        c_ld, w_ld, w_ld2 = sem("c_ld"), sem("w_ld"), sem("w_ld2")
        ones_set = sem("ones_set")
        bias_mm, bias_out = sem("bias_mm"), sem("bias_out")
        wm_set, sum_mm, sum_out = sem("wm_set"), sem("sum_mm"), sem("sum_out")
        fold_mm, fold_out = sem("fold_mm"), sem("fold_out")
        x_ld = [sem("x_ld0"), sem("x_ld1"), sem("x_ld6")]
        raw_ld = sem("raw_ld")
        wave_set, wsq_set, sq_half, sq_free, sqs_set = sem("wave_set"), sem("wsq_set"), sem("sq_half"), sem("sq_free"), sem("sqs_set")
        tok_mm, tok_free = sem("tok_mm"), sem("tok_free")
        xh_set, xh_T, xh_out = sem("xh_set"), sem("xh_T"), sem("xh_out")
        bs_set = sem("bs_set")
        var_set, var_r = sem("var_set"), sem("var_r")
        hvar_set, hvar_r = sem("hvar_set"), sem("hvar_r")
        bs_st = [sem(f"bs_st{n}") for n in range(4)]

        NTOK = 25
        s = {"xh_out": xh_out, "tok_free": tok_free, "base_ld": sem("base_ld"), "h2_st": sem("h2_st")}
        hall = sb("hall", [P, NP, D])
        wins = Windows(nc, ctx, sb, sem, A, const, ones, xnT, wqkv, colg, mowT, owT, hall, base_d, h2_d, pe1, pt1, pp, s) if stop >= 2 else None
        heads = Heads(nc, ctx, sb, sem, A, const, ones, colg, x2, kbd, hall, h2_d, xs_d, yy_d, out, pe1, pt1, pp, s) if stop >= 4 else None
        block = ctx.enter_context(nc.Block())

        def tile_of(r, pos):
            if pos == 3:
                return "last", 6, 14 * r + 6, 7
            i, j = (0, pos) if pos < 3 else (1, pos - 4)
            return i, 2 * j, 14 * r + 7 * i + 2 * j, 1

        eps_col = const[:, C_EPS:C_EPS + 1]

        def minus_half(n):
            return const[:, C_NH:C_NH + n]

        def before(pos):
            return (pos - 1) % 4 if pos else 2

        @block.sync
        def _(sp):
            sp.dma_start(const[:], A["consts"]).then_inc(c_ld, 16)
            for dst, src in ((gb[:], A["gb"]), (trow[:], A["tok_b"]), (w2[:], A["w2"])):
                sp.dma_start(dst, src).then_inc(w_ld, 16)
            for s in range(5):
                sp.dma_start(w1[:, s], A["w1"][:, s]).then_inc(w_ld, 16)
            for dst, src in ((inw[:], A["inw"]), (qkw[:], A["qkw"]), (inb[H2:H2 + 1, :], A["inb"]),
                             (colg[:], A["cols"]), (mowT[:], A["mowT"]), (owT[0:H2], A["owT"]), (owT[H2:H2 + 1, 1, :], A["ob"])):
                sp.dma_start(dst, src).then_inc(w_ld2, 16)

            def load_x(i, b):
                if b < 2:
                    sp.dma_start(xm[:, b].rearrange("p a c n -> p a (c n)"), A["xm"][bass.ds(i, 2)].rearrange("a p f -> p a f")).then_inc(x_ld[b], 16)
                else:
                    sp.dma_start(x6[:].rearrange("p a c n -> p (a c n)"), A["x6"][bass.ds(i, 1)].rearrange("a p f -> p (a f)")).then_inc(x_ld[2], 16)

            def load_raw(i, b):
                if b < 2:
                    for src, f0, f1 in (("xwa", 0, 8 * NA), ("xwb", 8 * NA, 8 * NA + 8 * NB)):
                        sp.dma_start(raw[:, f0:f1].rearrange("p (a f) -> p a f", a=2), A[src][bass.ds(i, 2)].rearrange("a p f -> p a f")).then_inc(raw_ld, 16)
                else:
                    for f0, f1 in ((0, 2048), (2048, 3072)):
                        sp.dma_start(raw[:, f0:f1], A["xw6"][bass.ds(i, 1), :, f0:f1].rearrange("a p f -> p (a f)")).then_inc(raw_ld, 16)

            load_x(0, 0)
            load_raw(0, 0)
            sp.wait_ge(wave_set, 1)
            load_raw(0, 2)
            load_x(0, 2)

            def pair(r):
                sp.wait_ge(wave_set, 3 * r + 2)
                load_raw(2 * r + 1, 1)
                sp.wait_ge(tok_mm, 7 * r)
                load_x(2 * r + 1, 1)
                sp.wait_ge(wave_set, 3 * r + 3)
                load_raw(2 * r + 2, 0)
                sp.wait_ge(tok_mm, 7 * r + 3)
                load_x(2 * r + 2, 0)
                sp.wait_ge(tok_mm, 7 * r + 4)
                load_x(r + 1, 2)
                sp.wait_ge(wave_set, 3 * r + 4)
                load_raw(r + 1, 2)

            with sp.Fori(0, 3) as r:
                pair(r)
            if wins:
                wins.sync(sp, bs_st, not heads)
            else:
                for n in range(4):
                    sp.wait_ge(bs_st[n], 112)
            if heads:
                heads.sync(sp)

        @block.scalar
        def _(act):
            def squares(u, b, loads, a):
                act.wait_ge(x_ld[b], loads)
                act.wait_ge(sq_free, 2 * u + a + 1)
                src = xm[:, b, a].rearrange("p c n -> p (c n)") if b < 2 else x6[:, 2 * a:2 * a + 2].rearrange("p q c n -> p (q c n)")
                nc.scalar.activation(sqt[:, 0:src.shape[1]], src, ACT.Square).then_inc(sq_half, 1)
                if a == 1:
                    act.wait_ge(wave_set, u + 1)
                    nc.scalar.activation(wsq[:, b] if b < 2 else wsq6[:], wv[:, b] if b < 2 else wv6[:], ACT.Square).then_inc(wsq_set, 1)

            def store(n, pos, r):
                _, _, t0, dt = tile_of(r, pos)
                k = pos % 4
                act.wait_ge(bs_set, n + 1)
                if dt == 1:
                    act.dma_start(base_d[bass.ds(t0, 2)].rearrange("t b d -> (t b) d"), bs[:, k]).then_inc(bs_st[k], 16)
                else:
                    for q in range(2):
                        act.dma_start(base_d[bass.ds(t0 + q * dt, 1)].rearrange("t b d -> (t b) d"),
                                      bs[q * B:(q + 1) * B, k]).then_inc(bs_st[k], 16)

            def put_T(n, pos, r):
                _, _, t0, dt = tile_of(r - 1, 6) if pos == 0 else tile_of(r, pos - 1)
                act.wait_ge(xh_T, n + 1)
                for h in range(2):
                    src = pt1[0:H2, pos % 2, h * P:(h + 1) * P].rearrange("p (t b) -> p t b", t=2)
                    for q in range(1 if dt == 1 else 2):
                        dst = xnT[:, h, bass.ds(FRONT + t0 + q * dt, 3 - dt if dt == 1 else 1), :]
                        last = nc.scalar.activation(dst, src if dt == 1 else src[:, q:q + 1, :], ACT.Identity,
                                                    bias=colg[:, h, 1:2], scale=colg[:, h, 0:1])
                last.then_inc(xh_out, 1)

            act.wait_ge(wm_set, 1)
            act.wait_ge(fold_out, 1)
            squares(0, 0, 16, 0)
            squares(0, 0, 16, 1)
            with act.Fori(0, 3) as r:
                for pos in range(7):
                    u, b, loads = UNIT_AT[pos // 2] if pos < 6 else (0, 0, 0)
                    if pos < 6:
                        squares(3 * r + u, b, 16 * r + loads, pos % 2)
                    put_T(7 * r + pos, pos, r)
                    store(7 * r + pos, pos, r)
            squares(10, 2, 64, 0)
            squares(10, 2, 64, 1)
            for pos in range(4):
                put_T(21 + pos, pos, 3)
                if pos < 3:
                    store(21 + pos, pos, 3)
            act.wait_ge(bs_set, 25)
            act.dma_start(base_d[T - 1:T + 1].rearrange("t b d -> (t b) d"), bs[:, 3]).then_inc(bs_st[3], 16)
            if wins:
                wins.scalar(act)
            if heads:
                heads.scalar(act)

        @block.gpsimd
        def _(pool):
            nc.gpsimd.memset(ones[:], 1.0).then_inc(ones_set, 1)
            nc.gpsimd.memset(xh[:, 2], 0.0).then_inc(ones_set, 1)

            def add_squares(u, b, a):
                pool.wait_ge(sq_half, 2 * u + a + 1)
                if b < 2:
                    dst = sqs[:, b, a]
                    src = [sqt[:, c * NA:(c + 1) * NA] for c in range(KC)]
                else:
                    dst = sq6[:, 2 * a:2 * a + 2]
                    halves = sqt[:, 0:2 * KC * P].rearrange("p (q c n) -> p q c n", q=2, c=KC)
                    src = [halves[:, :, c] for c in range(KC)]
                nc.gpsimd.tensor_tensor(dst, src[0], src[1], ALU.add)
                for c in range(2, KC):
                    pool.drain()
                    last = nc.gpsimd.tensor_tensor(dst, dst, src[c], ALU.add)
                last.then_inc(sq_free, 1)
                if a == 1:
                    pool.drain().then_inc(sqs_set, 1)

            def roots(n):
                pool.wait_ge(var_set, n + 1)
                nc.gpsimd.tensor_tensor(st1[:, 12:14], st1[:, 4:6], minus_half(2), ALU.pow).then_inc(var_r, 1)
                pool.wait_ge(hvar_set, n + 1)
                nc.gpsimd.tensor_tensor(st1[:, 10:11], st1[:, 9:10], eps_col, ALU.add)
                pool.drain()
                nc.gpsimd.tensor_tensor(st1[:, 10:11], st1[:, 10:11], minus_half(1), ALU.pow)
                pool.drain()
                nc.gpsimd.tensor_tensor(st1[:, 11:12], st1[:, 9:10], st1[:, 10:11], ALU.mult)
                pool.drain()
                nc.gpsimd.tensor_tensor(st1[:, 11:12], st1[:, 11:12], st1[:, 10:11], ALU.mult)
                pool.drain()
                nc.gpsimd.tensor_tensor(st1[:, 11:12], st1[:, 11:12], eps_col, ALU.add)
                pool.drain()
                nc.gpsimd.tensor_tensor(st1[:, 11:12], st1[:, 11:12], minus_half(1), ALU.pow).then_inc(hvar_r, 1)

            pool.wait_ge(c_ld, 16)
            nc.gpsimd.memset(st1[0:1, 20:21], 0.0).then_inc(sq_free, 1)
            add_squares(0, 0, 0)
            add_squares(0, 0, 1)
            with pool.Fori(0, 3) as r:
                for pos in range(7):
                    if pos < 6:
                        u, b, _ = UNIT_AT[pos // 2]
                        pool.wait_ge(tok_mm, 7 * r + (0, 0, 3)[pos // 2])
                        add_squares(3 * r + u, b, pos % 2)
                    roots(7 * r + pos)
            pool.wait_ge(tok_mm, 18)
            add_squares(10, 2, 0)
            add_squares(10, 2, 1)
            for pos in range(4):
                roots(21 + pos)
            if wins:
                wins.gpsimd(pool)
            if heads:
                heads.gpsimd(pool)

        @block.vector
        def _(dve):
            v = nc.vector
            v.memset(st1[0:1, 21:22], 0.0).then_inc(tok_free, 3)
            dve.wait_ge(c_ld, 16)
            dve.wait_ge(bias_mm, 1)
            v.tensor_copy(cb[:], pp[:, 0, 0:D]).then_inc(bias_out, 1)
            gm = gb[:, 0, 0:30].rearrange("p (s c) -> p s c", s=5)
            for s in range(5):
                v.tensor_tensor(w1[:, s], w1[:, s], gm[:, s].unsqueeze(2).to_broadcast([P, KC, D]), ALU.mult)
            v.tensor_tensor(w2[:], w2[:], gb[:, 0, 30:38].unsqueeze(2).to_broadcast([P, 8, D]), ALU.mult)
            dve.drain()
            for q in range(4):
                v.scalar_tensor_tensor(wm[:, q, :, 0:D], w1[:, 4], const[:, C_MK + q:C_MK + q + 1], w1[:, q], ALU.mult, ALU.add)
                v.tensor_scalar(wm[:, q, :, D:D + 1], const[:, C_MK + q:C_MK + q + 1].unsqueeze(1).to_broadcast([P, KC, 1]), 1.0, None, ALU.add)
            for q in range(6):
                v.scalar_tensor_tensor(ww[:, q, 0:D], w2[:, 6 + q // 4], const[:, C_MK + 4 + q:C_MK + 5 + q], w2[:, q], ALU.mult, ALU.add)
            v.tensor_scalar(ww[:, :, D:D + 1], const[:, C_MK + 4:C_MK + 10].unsqueeze(2), 1.0, None, ALU.add)
            dve.drain().then_inc(wm_set, 1)
            dve.wait_ge(sum_mm, 1)
            v.tensor_copy(s1b[:], pp[:, 0, 0:D])
            v.tensor_copy(s2b[:], pp[:, 1, 0:D]).then_inc(sum_out, 1)
            dve.wait_ge(fold_mm, 1)
            dve.wait_ge(w_ld2, 16 * 7)
            for h in range(2):
                v.tensor_copy(wqkv[0:H2, h, 0:2 * D], pe1[0:H2, 2 * h, 0:2 * D])
                v.tensor_copy(wqkv[0:H2, h, 2 * D:3 * D], pe1[0:H2, 2 * h + 1, 0:D])
            v.tensor_tensor(wqkv[H2:H2 + 1, 1, 0:2 * D], pt1[H2:H2 + 1, 0, 0:2 * D], inb[H2:H2 + 1, 0:2 * D], ALU.add)
            v.tensor_tensor(wqkv[H2:H2 + 1, 1, 2 * D:3 * D], pt1[H2:H2 + 1, 1, 0:D], inb[H2:H2 + 1, 2 * D:3 * D], ALU.add)
            dve.drain().then_inc(fold_out, 1)

            def waves(u, b):
                dve.wait_ge(raw_ld, 32 * u + 32)
                parts = ((2, NA), (2, NB)) if b < 2 else ((4, P), (2, P))
                f0 = w0 = 0
                for rows, n in parts:
                    src = raw[:, f0:f0 + 4 * rows * n].rearrange("p (a k n) -> p a k n", a=rows, k=4)
                    w = (wv[:, b] if b < 2 else wv6[:])[:, w0:w0 + rows * n].rearrange("p (a n) -> p a n", a=rows)
                    v.tensor_tensor(w, src[:, :, 1], src[:, :, 2], ALU.add)
                    dve.drain()
                    v.tensor_tensor(w, w, src[:, :, 3], ALU.add)
                    dve.drain()
                    v.scalar_tensor_tensor(w, src[:, :, 0], 3.0, w, ALU.mult, ALU.subtract)
                    f0, w0 = f0 + 4 * rows * n, w0 + rows * n
                dve.drain().then_inc(wave_set, 1)

            def post(n, k, stored):
                dve.wait_ge(tok_mm, n + 1)
                y = pe1[:, k]
                stat = y.rearrange("p (a c) -> p a c", a=2)[:, :, D:D + 2]
                m = st1[:, 0:4].rearrange("p (a c) -> p a c", a=2)
                mean, e2 = m[:, :, 0], m[:, :, 1]
                v.tensor_tensor(m, stat, const[:, C_INV:C_INV + 4].rearrange("p (a c) -> p a c", a=2), ALU.mult)
                dve.drain()
                v.tensor_tensor(st1[:, 4:6], mean, mean, ALU.mult)
                dve.drain()
                v.tensor_tensor(st1[:, 4:6], e2, st1[:, 4:6], ALU.subtract)
                dve.drain()
                v.tensor_scalar(st1[:, 4:6], st1[:, 4:6], 0.0, EPS, ALU.max, ALU.add).then_inc(var_set, 1)
                dve.wait_ge(var_r, n + 1)
                v.scalar_tensor_tensor(st1[:, 6:8], mean, -1.0, st1[:, 12:14], ALU.mult, ALU.mult)
                v.tensor_tensor(st1[:, 4:6], st1[:, 12:14], const[:, C_SIX:C_SIX + 2], ALU.mult)
                dve.drain()
                v.scalar_tensor_tensor(hh[:], s1b[:], st1[:, 6:7], cb[:], ALU.mult, ALU.add)
                dve.drain()
                v.scalar_tensor_tensor(hh[:], s2b[:], st1[:, 7:8], hh[:], ALU.mult, ALU.add)
                dve.drain()
                v.scalar_tensor_tensor(hh[:], y[:, 0:D], st1[:, 4:5], hh[:], ALU.mult, ALU.add)
                dve.drain()
                v.scalar_tensor_tensor(hh[:], y[:, 256:256 + D], st1[:, 5:6], hh[:], ALU.mult, ALU.add).then_inc(tok_free, 1)
                dve.drain()
                v.bn_stats(bn1[:], hh[:])
                dve.drain()
                v.bn_aggr(st1[:, 8:10], bn1[:]).then_inc(hvar_set, 1)
                dve.wait_ge(hvar_r, n + 1)
                dve.wait_ge(xh_T, n)
                dve.wait_ge(bs_st[k], stored)
                v.tensor_scalar(xh[:, k], hh[:], st1[:, 8:9], st1[:, 10:11], ALU.subtract, ALU.mult)
                dve.drain()
                v.tensor_tensor(bs[:, k], hh[:], xh[:, k], ALU.add).then_inc(bs_set, 1)
                v.tensor_scalar(xh[:, k], xh[:, k], st1[:, 11:12], None, ALU.mult).then_inc(xh_set, 1)
                dve.drain()

            waves(0, 0)
            with dve.Fori(0, 3) as r:
                for pos in range(7):
                    if pos in (0, 2, 4):
                        u, b, _ = UNIT_AT[pos // 2]
                        dve.wait_ge(tok_mm, 7 * r + (0, 0, 3)[pos // 2])
                        waves(3 * r + u, b)
                    post(7 * r + pos, pos % 4, 32 * r + (16 if pos >= 4 else 0))
            waves(10, 2)
            for pos in range(4):
                post(21 + pos, pos, 96)
            if wins:
                wins.vector(dve)
            if heads:
                heads.vector(dve)

        @block.tensor
        def _(pe):
            mm = nc.tensor.matmul
            pe.wait_ge(ones_set, 2)
            pe.wait_ge(w_ld, 16 * 8)
            def bcol(n, k=P):
                return gb[0:k, 1, n:n + 1].to_broadcast([k, P])

            for n in range(30):
                mm(pp[:, 0, 0:D], bcol(n), w1[:, n // KC, n % KC], start=(n == 0), stop=False)
            for n in range(8):
                k = 64 if n == 7 else P
                mm(pp[:, 0, 0:D], bcol(30 + n, k), w2[0:k, n], start=False, stop=False)
            for n in range(2):
                last = mm(pp[:, 0, 0:D], ones[0:1, :], trow[0:1, n], start=False, stop=(n == 1))
            last.then_inc(bias_mm, 1)
            pe.wait_ge(w_ld2, 16 * 7)
            for h in range(2):
                for g in range(3):
                    dst = pe1[0:H2, 2 * h + g // 2, (g % 2) * D:(g % 2) * D + D]
                    for m in range(2):
                        mm(dst, qkw[:, m, g, h * H2:(h + 1) * H2], inw[:, m, g], start=(m == 0), stop=(m == 1))
            for g in range(3):
                for m in range(2):
                    dst = pt1[H2:H2 + 1, g // 2, (g % 2) * D:(g % 2) * D + D]
                    last = mm(dst, qkw[:, m, g, D:D + 1], inw[:, m, g], start=(m == 0), stop=(m == 1))
            last.then_inc(fold_mm, 1)
            pe.wait_ge(wm_set, 1)
            pe.wait_ge(bias_out, 1)
            for n in range(24):
                mm(pp[:, 0, 0:D], ones[:], wm[:, n // KC, n % KC, 0:D], start=(n == 0), stop=(n == 23))
            for n in range(6):
                last = mm(pp[:, 1, 0:D], ones[:], ww[:, n, 0:D], start=(n == 0), stop=(n == 5))
            last.then_inc(sum_mm, 1)
            pe.wait_ge(fold_out, 1)

            def tokens(n, b, j0, k):
                pe.wait_ge(tok_free, n + 1)
                y = pe1[:, k]

                def cell(q, c):
                    if b == 2:
                        return x6[:, q, c]
                    n0 = (j0 + q % 2) * B
                    return xm[:, b, q // 2, c, n0:n0 + P]

                def cell_squares(q):
                    if b == 2:
                        return sq6[:, q]
                    n0 = (j0 + q % 2) * B
                    return sqs[:, b, q // 2, n0:n0 + P]

                def wave(rows, col, q):
                    if b == 2:
                        return col[:, q * P:(q + 1) * P]
                    n0 = (q // 2) * NA + (j0 + q % 2) * B if q < 4 else 2 * NA + (q - 4) * NB + j0 * B
                    return rows[:, b, n0:n0 + P]

                for q in range(4):
                    for c in range(KC):
                        mm(y[:, 0:D + 1], cell(q, c), wm[:, q, c], start=(q + c == 0), stop=(q == 3 and c == KC - 1))
                for q in range(4):
                    mm(y[:, D + 1:D + 2], cell_squares(q), wm[:, q, 0, D:D + 1], start=(q == 0), stop=(q == 3))
                for q in range(6):
                    mm(y[:, 256:256 + D + 1], wave(wv, wv6, q), ww[:, q], start=(q == 0), stop=(q == 5))
                for q in range(6):
                    last = mm(y[:, 256 + D + 1:256 + D + 2], wave(wsq, wsq6, q), ww[:, q, D:D + 1], start=(q == 0), stop=(q == 5))
                last.then_inc(tok_mm, 1)

            def transpose(n, pos):
                pe.wait_ge(xh_set, n)
                pe.wait_ge(xh_out, n)
                for h in range(2):
                    last = nc.tensor.transpose(pt1[0:H2, pos % 2, h * P:(h + 1) * P],
                                               xh[:, before(pos), h * H2:(h + 1) * H2], ident)
                last.then_inc(xh_T, 1)

            def unit_ready(u, b, loads):
                pe.wait_ge(x_ld[b], loads)
                pe.wait_ge(wave_set, u + 1)
                pe.wait_ge(wsq_set, u + 1)
                pe.wait_ge(sqs_set, u + 1)

            with pe.Fori(0, 3) as r:
                for pos in range(7):
                    if pos == 0:
                        unit_ready(3 * r, 0, 16 * r + 16)
                    if pos == 3:
                        unit_ready(3 * r + 1, 2, 16 * r + 16)
                    if pos == 4:
                        unit_ready(3 * r + 2, 1, 16 * r + 16)
                    tokens(7 * r + pos, 0 if pos < 3 else 2 if pos == 3 else 1, tile_of(0, pos)[1], pos % 4)
                    transpose(7 * r + pos, pos)
            for pos in range(4):
                if pos == 0:
                    unit_ready(9, 0, 64)
                if pos == 3:
                    unit_ready(10, 2, 64)
                tokens(21 + pos, 0 if pos < 3 else 2, tile_of(3, pos)[1], pos)
                transpose(21 + pos, pos)
            if wins:
                wins.tensor(pe)
            if heads:
                heads.tensor(pe)


def lay_out(inputs):
    import numpy as np

    f = {k: np.asarray(v) for k, v in inputs.items()}
    g = {}
    x = f["x"]
    pad = np.zeros((B, CH, NC * CELL, NC * CELL), x.dtype)
    pad[:, :, CELL // 2:CELL // 2 + 112, CELL // 2:CELL // 2 + 112] = x
    m = pad.reshape(B, CH, NC, 2, 8, NC, 2, 4, 2)
    m = m.transpose(2, 5, 3, 6, 4, 7, 8, 1, 0).reshape(NC, NC, P, KC, B)
    rows = np.ascontiguousarray(m.transpose(0, 2, 3, 1, 4))
    g["xm"] = np.ascontiguousarray(rows[:, :, :, :7]).reshape(NC, P, KC * NA)
    w = pad.reshape(B, CH, NC, 2, 4, 2, NC, 2, 4, 2)
    w = w.transpose(2, 6, 3, 7, 4, 8, 1, 5, 9, 0).reshape(NC, NC, D, 4, B)
    w = np.ascontiguousarray(w.transpose(0, 2, 3, 1, 4))
    low = w[:, P:]
    both = np.concatenate([low[:, :, :, 0:NC - 1], low[:, :, :, 1:NC]], 1)
    g["xwa"] = np.ascontiguousarray(w[:, :P, :, :7]).reshape(NC, P, 4 * NA)
    g["xwb"] = np.ascontiguousarray(both[:, :, :, :6]).reshape(NC, P, 4 * NB)
    x6, xw6 = [], []
    for r in range(4):
        i = [2 * r, min(2 * r + 1, G - 1)]
        x6.append(np.stack([np.stack([rows[k + a, :, :, 6 + b] for k in i], 2) for a in range(2) for b in range(2)], 1).reshape(P, -1))
        wa = np.stack([np.stack([w[k + a, :P, :, 6 + b] for k in i], 2) for a in range(2) for b in range(2)], 1).reshape(P, -1)
        wb = np.stack([np.stack([both[k + a, :, :, 6] for k in i], 2) for a in range(2)], 1).reshape(P, -1)
        xw6.append(np.concatenate([wa, wb], 1))
    g["x6"], g["xw6"] = np.stack(x6), np.stack(xw6)

    def main_rows(a):
        n = a.shape[1]
        a = a.reshape(16, 16, 5, CH, n)
        out = []
        for s in (1, 2, 3, 4, 0):
            t = a[:, :, s]
            if s == 0:
                t = np.roll(t, (8, 8), (0, 1))
            t = t.reshape(2, 8, 2, 4, 2, CH, n).transpose(0, 2, 1, 3, 4, 5, 6)
            out.append(t.reshape(P, KC, n))
        return np.ascontiguousarray(np.stack(out, 1))

    def wave_rows(a):
        n = a.shape[1]
        a = a.reshape(8, 8, 5, CH, n)
        r = []
        for s in (1, 2, 3, 4, 0):
            t = a[:, :, s]
            if s == 0:
                t = np.roll(t, (4, 4), (0, 1))
            r.append(t.reshape(2, 4, 2, 4, CH, n).transpose(0, 2, 1, 3, 4, 5).reshape(D, n))
        out = [r[q][:P] for q in range(4)]
        out += [np.concatenate([r[0][P:], r[1][P:]]), np.concatenate([r[2][P:], r[3][P:]])]
        out += [r[4][:P], np.concatenate([r[4][P:], r[4][P:]])]
        return np.ascontiguousarray(np.stack(out, 1))

    g["w1"] = main_rows(f["L0_tok_w1"])
    g["w2"] = wave_rows(f["L0_tok_w2"])
    gb = np.zeros((P, 2, 38), np.float32)
    for n, (a, b) in enumerate((("L0_tok_ln1_g", "L0_tok_ln2_g"), ("L0_tok_ln1_b", "L0_tok_ln2_b"))):
        gb[:, n, 0:30] = main_rows(f[a][:, None]).reshape(P, 30)
        gb[:, n, 30:] = wave_rows(f[b][:, None]).reshape(P, 8)
    g["gb"] = gb
    g["tok_b"] = np.stack([f["L0_tok_b1"], f["L0_tok_b2"]])[None]

    def halves(a):
        return np.ascontiguousarray(a.reshape(2, H2, -1).transpose(1, 0, 2))

    g["inw"] = halves(f["L0_attn_inw"].T).reshape(H2, 2, 3, D)
    qk = [halves(np.concatenate([f[f"L0_attn_{c}w"], f[f"L0_attn_{c}b"][:, None]], 1)) for c in "qkv"]
    g["qkw"] = np.ascontiguousarray(np.stack(qk, 2))
    g["inb"] = f["L0_attn_inb"][None]
    cols = [f[n][:, None] for n in ("L0_attn_ln_g", "L0_attn_ln_b", "L0_attn_mob", "L0_ffn_norm1_w", "L0_ffn_norm1_b")]
    g["cols"] = halves(np.concatenate(cols, 1))
    g["mowT"] = halves(f["L0_attn_mow"].T)
    g["owT"] = halves(f["L0_attn_ow"].T)
    g["ob"] = f["L0_attn_ob"][None]
    g["qkvT"] = halves(f["L0_ffn_qkv_w"].T)
    g["qkvb"] = f["L0_ffn_qkv_b"][None]
    g["projT"] = halves(f["L0_ffn_proj_w"].T)
    g["projb"] = f["L0_ffn_proj_b"][None]
    g["n2"] = np.stack([f["L0_ffn_norm2_w"], f["L0_ffn_norm2_b"]])
    g["wgate"] = halves(f["L0_ffn_w_gate"])
    g["W1"] = np.ascontiguousarray(f["L0_ffn_W1"].reshape(E, 2, H2, HID).transpose(0, 2, 1, 3))
    g["b1"] = np.ascontiguousarray(f["L0_ffn_b1"].reshape(E, HC, P).transpose(0, 2, 1))
    g["W2"] = np.ascontiguousarray(f["L0_ffn_W2"].reshape(E, HC, P, D).transpose(0, 2, 1, 3))
    g["b2"] = f["L0_ffn_b2"]

    c = np.zeros((P, NCONST), np.float32)
    c[:, C_ID:C_ID + P] = np.eye(P)
    p = np.arange(P)
    for q in range(4):
        c[:, C_MK + q] = p // 32 == 3 - q
        c[:, C_MK + 4 + q] = p // 48 == 3 - q
    for a in range(2):
        quad = (P + p % 64) // 48
        c[:, C_MK + 8 + a] = quad == 3 - 2 * a - p // 64
    c[:, C_INV:C_INV + 4] = [1 / PATCH, 1 / PATCH, 1 / (6 * WAVE), 1 / (36 * WAVE)]
    c[:, C_SIX:C_SIX + 2] = [1, 1 / 6]
    for h in range(6):
        c[:, C_KM + h] = p // AHD == h
    c[:, C_NH:C_NH + 2] = -0.5
    c[:, C_EPS:C_EPS + 2] = EPS
    c[:, C_EI:C_EI + E] = np.arange(E)
    real = (p % B) < T
    c[:, C_VAL] = real
    c[:, C_VAL + 1] = np.where(real, 0, FAR)
    c[:, C_ER:C_ER + E] = np.arange(E) * R
    c[:, C_J:C_J + NT] = np.arange(NT)
    c[:, C_L8:C_L8 + E * E] = (np.arange(E)[:, None] >= np.arange(E)[None]).reshape(-1)
    c[:, C_TRI:C_TRI + P] = p[:, None] < p[None]
    c[:, C_ROW:] = (2 * (P * np.arange(NP)[None, :, None] + p[:, None, None]) + np.arange(2)).reshape(P, -1)
    g["consts"] = c
    return g


def kernel(**inputs):
    import numpy as np
    import concourse.bacc as bacc
    from concourse.bass_utils import run_bass_kernel_spmd

    nc = bacc.Bacc("TRN2", target_bir_lowering=False, num_devices=1)
    arrays = lay_out(inputs)
    aps = {n: nc.dram_tensor(f"in_{n}", a.shape, mybir.dt.from_np(a.dtype), kind="ExternalInput").ap() for n, a in arrays.items()}
    out = nc.dram_tensor("out", (B, T, D), F32, kind="ExternalOutput").ap()
    build(nc, aps, out)
    r = run_bass_kernel_spmd(nc, [{f"in_{n}": a for n, a in arrays.items()}], core_ids=[0])
    return r.results[0]["out"]
```

```python
from contextlib import ExitStack

import concourse.bass as bass
from concourse import mybir

F32 = mybir.dt.float32
BF16 = mybir.dt.bfloat16
I32 = mybir.dt.int32
U32 = mybir.dt.uint32
ALU = mybir.AluOpType
ACT = mybir.ActivationFunctionType
X = mybir.AxisListType.X

P = 128
B = 64
G = 7
T = G * G
D = 192
H2 = D // 2
EPS = 1e-5
CELL = 16
NC = 8
CH = 3
KC = CELL * CELL * CH // P
PATCH = 5 * CELL * CELL * CH
WAVE = PATCH // 4
NA = 7 * B
NB = 6 * B
WH = 6
WHD = D // WH
NWT = 11
POS = 66
FRONT = 3
AH = 12
AHD = D // AH
NP = B // 2
E = 8
HID = 768
HC = HID // P
ROWS = 128
NT = (2 * B * T + E * (ROWS - 1)) // ROWS
R = B * T + ROWS
DX = D + 1
NROW = E * R + ROWS
FAR = 1 << 20
TT = (T + 1) // 2
UNIT_AT = [(1, 2, 16), (2, 1, 16), (3, 0, 32)]

C_ID = 0
C_MK = C_ID + P
C_INV = C_MK + 10
C_SIX = C_INV + 4
C_KM = C_SIX + 2
C_NH = C_KM + 6
C_EPS = C_NH + 2
C_EI = C_EPS + 2
C_VAL = C_EI + E
C_ER = C_VAL + 2
C_J = C_ER + E
C_L8 = C_J + NT
C_TRI = C_L8 + E * E
C_ROW = C_TRI + P
NCONST = C_ROW + 2 * NP


def run_slots(eng, n, depth, slot, unroll=2):
    def at(t, k, u, full):
        def item(lag):
            if not full and not 0 <= t - lag < n:
                return None
            return (t - lag, (u - lag) % unroll, k + (u - lag) // unroll)
        return item

    first = -(-(depth - 1) // unroll)
    last = n // unroll
    for t in range(first * unroll):
        slot(at(t, t // unroll, t % unroll, False))
    with eng.Fori(first, last) as k:
        for u in range(unroll):
            slot(at(unroll * k + u, k, u, True))
    for t in range(last * unroll, n + depth - 1):
        slot(at(t, t // unroll, t % unroll, False))


class Windows:

    def __init__(self, nc, ctx, sb, sem, A, const, ones, xnT, wqkv, colg, mowT, owT, hall, base_d, h2_d, pe1, pt1, pp, s):
        self.nc, self.const, self.xnT, self.wqkv, self.colg, self.mowT, self.owT = nc, const, xnT, wqkv, colg, mowT, owT
        self.hall, self.base_d, self.h2_d, self.pe1, self.pt1, self.pp, self.s = hall, base_d, h2_d, pe1, pt1, pp, s
        own = ExitStack()
        self.prod = sb("prod", [P, 3, 3, D], to=own)
        self.stg = sb("stg", [H2 + 1, 2, 2, 3, P], to=own)
        self.qkv = sb("qkv", [P, 2, 3, 3 * D], to=own)
        self.pv = sb("pv", [P, 3, 3, D], to=own)
        self.sc = sb("sc", [P, 3, 3, WH], to=own)
        self.ex = sb("ex", [P, 3, 3, WH], to=own)
        self.mx = sb("mx", [P, 3, WH], to=own)
        self.ob = sb("ob", [P, 3, D], to=own)
        self.oT = sb("oT", [H2, 2, 3 * P], to=own)
        self.gall = sb("gall", [H2, 2, POS, B], to=own)
        self.g12 = sb("g12", [H2, 2, 15, B], to=own)
        self.accT = sb("accT", [H2, 2, 2 * TT, B], to=own)
        self.st3 = sb("st3", [H2 + 1, 4, 2, P], to=own)
        own.close()
        self.stg0_set, self.ones_row = sem("stg0_set"), sem("ones_row")
        self.stg_set, self.stg_used, self.qkv_mm, self.qkv_out, self.qkv_free = sem("stg_set"), sem("stg_used"), sem("qkv_mm"), sem("qkv_out"), sem("qkv_free")
        self.w_sc, self.w_ex, self.w_pv, self.w_o, self.o_T, self.o_out = sem("w_sc"), sem("w_ex"), sem("w_pv"), sem("w_o"), sem("o_T"), sem("o_out")
        self.so_mm, self.so_out, self.pooled, self.gelu_set, self.acc_set = sem("so_mm"), sem("so_out"), sem("pooled"), sem("gelu_set"), sem("acc_set")
        self.st3_set, self.mix_mm, self.h2_set = [sem("st3_set0"), sem("st3_set1")], sem("mix_mm"), sem("h2_set")

    def gpsimd(self, pool):
        nc, xnT, stg = self.nc, self.xnT, self.stg
        pool.wait_ge(self.s["xh_out"], 25)

        def stage(i, u):
            if not (isinstance(i, int) and i < 2):
                pool.wait_ge(self.stg_used, i - 1)
            for h in range(2):
                src = xnT[:, h, bass.ds(FRONT + 6 * i, 6), :].rearrange("p (w s) b -> p s w b", s=3)
                last = nc.gpsimd.tensor_copy(stg[0:H2, u, h].rearrange("p s (w b) -> p s w b", w=2), src)
            last.then_inc(self.stg_set, 1)
        stage(1, 1)
        pool.wait_ge(self.pooled, 1)

        def add_up(i):
            pool.wait_ge(self.o_T, i)
            pool.wait_ge(self.w_pv, i + 1)
            nc.gpsimd.tensor_tensor(self.ob[:], self.pv[:, :, 0], self.pv[:, :, 1], ALU.add)
            pool.drain()
            nc.gpsimd.tensor_tensor(self.ob[:], self.ob[:], self.pv[:, :, 2], ALU.add).then_inc(self.w_o, 1)
        with pool.Fori(1, NWT // 2) as k:
            for u in range(2):
                stage(2 * k + u, u)
                add_up(2 * k + u - 2)
        for i in range(NWT // 2 * 2, NWT + 2):
            if i < NWT:
                stage(i, i % 2)
            add_up(i - 2)

        def mix(item):
            i, u, _ = item(0)
            if u % 2 == 0:
                pool.wait_ge(self.mix_mm, i + 1)
                pool.wait_ge(self.acc_set, i + 1)
                nc.gpsimd.tensor_copy(self.st3[0:H2, u], self.accT[:, :, bass.ds(2 * i, 2), :].rearrange("p h t b -> p h (t b)")).then_inc(self.st3_set[0], 1)
        run_slots(pool, TT, 1, mix, 4)

    def tensor(self, pe):
        nc, mm = self.nc, self.nc.tensor.matmul
        pe1, pt1, pp, stg = self.pe1, self.pt1, self.pp, self.stg
        ident = self.const[:, C_ID:C_ID + P]
        pe.wait_ge(self.ones_row, 1)
        pe.wait_ge(self.stg0_set, 1)

        def qkv(i, u, s):
            if isinstance(i, int) and i == 0 and s < 2:
                pe.wait_ge(self.s["tok_free"], 26 + 2 * s)
            else:
                pe.wait_ge(self.qkv_out, 3 * i + s - 1)
            b = 2 * ((u + s) % 2)
            for n in range(2):
                mm(pe1[:, b + n, 0:288], stg[0:H2, u, 0, s], self.wqkv[0:H2, 0, n * 288:(n + 1) * 288], start=True, stop=False)
                last = mm(pe1[:, b + n, 0:288], stg[:, u, 1, s], self.wqkv[:, 1, n * 288:(n + 1) * 288], start=False, stop=True)
            last.then_inc(self.qkv_mm, 1)
            if s == 2:
                pe.drain().then_inc(self.stg_used, 1)

        def slot(item):
            a, c = item(0), item(2)
            if a:
                i, u, _ = a
                if not (isinstance(i, int) and i == 0):
                    pe.wait_ge(self.stg_set, i)
                qkv(i, u, 0)
                qkv(i, u, 1)
            if c:
                i, u, _ = c
                pe.wait_ge(self.w_o, i + 1)
                pe.wait_ge(self.o_out, i)
                for h in range(2):
                    for s in range(3):
                        last = nc.tensor.transpose(pt1[0:H2, h, s * P:(s + 1) * P], self.ob[:, s, h * H2:(h + 1) * H2], ident)
                last.then_inc(self.o_T, 1)
            if a:
                qkv(*a[:2], 2)
            if c:
                i, u, _ = c
                pe.wait_ge(self.o_out, i + 1)
                pe.wait_ge(self.so_out, i)
                for m in range(2):
                    for h in range(2):
                        last = mm(pp[0:H2, m, 0:3 * P], self.mowT[:, h, m * H2:(m + 1) * H2], self.oT[:, h], start=(h == 0), stop=(h == 1))
                last.then_inc(self.so_mm, 1)
        run_slots(pe, NWT, 3, slot)

        pe.wait_ge(self.so_out, NWT)

        def mix(item):
            i, u, h = item(0)
            pe.wait_ge(self.st3_set[u % 2], 2 * h + u // 2 + 1)
            pe.wait_ge(self.h2_set, i + 1)
            mm(pe1[:, u, 0:D], self.st3[0:H2, u, 0], self.owT[0:H2, 0], start=True, stop=False)
            mm(pe1[:, u, 0:D], self.st3[:, u, 1], self.owT[:, 1], start=False, stop=True).then_inc(self.mix_mm, 1)
        run_slots(pe, TT, 1, mix, 4)

    def scalar(self, act):
        nc = self.nc
        pe1, pt1, pp, gall, colg = self.pe1, self.pt1, self.pp, self.gall, self.colg

        def gelus(parts):
            act.drain()
            for a, b in parts:
                part = gall[:, :, a:b].rearrange("p h t b -> p h (t b)")
                nc.scalar.activation(part, part, ACT.Gelu).then_inc(self.gelu_set, 1)

        act.wait_ge(self.s["tok_mm"], 25)
        for h in range(2):
            src = self.xnT[:, h, FRONT:FRONT + 6, :].rearrange("p (w s) b -> p s w b", s=3)
            last = nc.scalar.activation(self.stg[0:H2, 0, h].rearrange("p s (w b) -> p s w b", w=2), src, ACT.Copy)
        last.then_inc(self.stg0_set, 1)

        def qkv(i, u, s):
            if s == 0 and not (isinstance(i, int) and i < 2):
                act.wait_ge(self.qkv_free, i - 1)
            act.wait_ge(self.qkv_mm, 3 * i + s + 1)
            b = 2 * ((u + s) % 2)
            nc.scalar.activation(self.qkv[:, u, s].rearrange("p (n f) -> p n f", n=2), pe1[:, b:b + 2, 0:288], ACT.Copy).then_inc(self.qkv_out, 1)

        def slot(item):
            a, b, c = item(0), item(1), item(2)
            if a:
                qkv(*a[:2], 0)
            if a:
                qkv(*a[:2], 1)
            if b:
                i, u, _ = b
                act.wait_ge(self.w_sc, i + 1)
                nc.scalar.activation(self.ex[:], self.sc[:], ACT.Exp, scale=WHD ** -0.5).then_inc(self.w_ex, 1)
            if c:
                i, u, _ = c
                act.wait_ge(self.o_T, i + 1)
                nc.scalar.activation(self.oT[:], pt1[0:H2, :, 0:3 * P], ACT.Copy).then_inc(self.o_out, 1)
                if not a and not b:
                    gelus(((0, 16), (16, 32), (32, 48)))
            if a:
                qkv(*a[:2], 2)
            if c:
                i, u, _ = c
                act.wait_ge(self.so_mm, i + 1)
                for m in range(2):
                    dst = gall[:, m, bass.ds(6 * i, 6), :].rearrange("p (w s) b -> p s w b", s=3)
                    last = nc.scalar.activation(dst, pp[0:H2, m, 0:3 * P].rearrange("p (s w b) -> p s w b", s=3, w=2),
                                                ACT.Identity, bias=colg[:, m, 2:3])
                last.then_inc(self.so_out, 1)
        run_slots(act, NWT, 3, slot)
        gelus(((48, 66),))

        def mix(item):
            i, u, _ = item(0)
            if u % 2 == 1:
                act.wait_ge(self.mix_mm, i + 1)
                act.wait_ge(self.acc_set, i + 1)
                nc.scalar.activation(self.st3[0:H2, u], self.accT[:, :, bass.ds(2 * i, 2), :].rearrange("p h t b -> p h (t b)"), ACT.Copy).then_inc(self.st3_set[1], 1)
        run_slots(act, TT, 1, mix, 4)

    def set_ones_row(self, dve):
        self.nc.vector.memset(self.stg[H2:H2 + 1, :, 1].rearrange("p u s n -> p u (s n)"), 1.0).then_inc(self.ones_row, 1)

    def pool_tokens(self, dve, steps):
        v, xnT = self.nc.vector, self.xnT
        dve.wait_ge(self.s["xh_out"], 25)
        for step in steps:
            src, dst, n = ((FRONT, FRONT + 48, 15), (FRONT + 48, FRONT + 63, 3))[step // 3]
            out = xnT[:, :, dst:dst + n, :]
            x = [xnT[:, :, src + q:src + q + 3 * n - 2:3, :] for q in range(3)]
            if step % 3 == 0:
                v.tensor_tensor(out, x[0], x[1], ALU.add)
            elif step % 3 == 1:
                v.tensor_tensor(out, out, x[2], ALU.add)
            else:
                v.tensor_scalar(out, out, 1 / 3, None, ALU.mult)
            dve.drain()
        if 5 in steps:
            dve.drain().then_inc(self.pooled, 1)

    def vector(self, dve):
        nc, v, xnT, qkv, prod = self.nc, self.nc.vector, self.xnT, self.qkv, self.prod
        self.pool_tokens(dve, range(1, 6))

        def slot(item):
            if not (it := item(1)):
                return
            i, u, _ = it
            dve.drain()
            dve.wait_ge(self.qkv_out, 3 * i + 3)
            for a in range(3):
                v.tensor_tensor(prod[:, a], qkv[:, u, a:a + 1, 0:D].to_broadcast([P, 3, D]), qkv[:, u, :, D:2 * D], ALU.mult)
            dve.drain()
            sc, ex, mx = self.sc, self.ex, self.mx
            v.tensor_reduce(sc[:].rearrange("p a b h -> p (a b h)"), prod[:].rearrange("p a b (h d) -> p (a b h) d", h=WH), X, ALU.add)
            dve.drain()
            v.tensor_reduce(mx[:], sc[:].rearrange("p a b h -> p a h b"), X, ALU.max)
            dve.drain()
            v.tensor_tensor(sc[:], sc[:], mx[:].unsqueeze(2).to_broadcast([P, 3, 3, WH]), ALU.subtract).then_inc(self.w_sc, 1)
            dve.wait_ge(self.w_ex, i + 1)
            v.tensor_reduce(mx[:], ex[:].rearrange("p a b h -> p a h b"), X, ALU.add)
            dve.drain()
            v.reciprocal(mx[:], mx[:])
            dve.drain()
            v.tensor_tensor(ex[:], ex[:], mx[:].unsqueeze(2).to_broadcast([P, 3, 3, WH]), ALU.mult)
            dve.drain()
            dve.wait_ge(self.w_o, i)
            for a in range(3):
                last = v.tensor_tensor(self.pv[:, a].rearrange("p b (h d) -> p b h d", h=WH),
                                       qkv[:, u, :, 2 * D:3 * D].rearrange("p b (h d) -> p b h d", h=WH),
                                       ex[:, a].unsqueeze(3).to_broadcast([P, 3, WH, WHD]), ALU.mult)
            last.then_inc(self.w_pv, 1)
            dve.drain().then_inc(self.qkv_free, 1)
        run_slots(dve, NWT, 3, slot)

        v.memset(self.st3[H2:H2 + 1, :, 1], 1.0).then_inc(self.mix_mm, 4)
        v.memset(self.hall[:, TT:], 0.0).then_inc(self.h2_set, 4)
        gall, g12, acc = self.gall, self.g12, self.accT
        dve.wait_ge(self.s["base_ld"], 16)
        dve.wait_ge(self.gelu_set, 4)
        for h in range(2):
            v.tensor_tensor(g12[:, h].rearrange("p (v u) b -> p v u b", u=5), gall[:, h, 48:63].rearrange("p (v u) b -> p v u b", u=5),
                            gall[:, h, 63:66].unsqueeze(2).to_broadcast([H2, 3, 5, B]), ALU.add)
        dve.drain()
        starts = [next(t for t in range(T) if t * 15 // T == u) for u in range(15)] + [2 * TT]
        for u in range(15):
            a, b = starts[u], starts[u + 1]
            for lo, hi, src in (((0, 1, 0), (1, b, 0)) if u == 0 else ((a, b, a - 1),)):
                n = hi - lo
                last = v.tensor_tensor(acc[:, :, lo:hi], gall[:, :, src:src + n], g12[:, :, u:u + 1].to_broadcast([H2, 2, n, B]), ALU.add)
            last.then_inc(self.acc_set, b // 2 - a // 2)

        def mix(item):
            i, u, _ = item(0)
            dve.wait_ge(self.mix_mm, i + 5)
            row = self.hall[:, bass.ds(i, 1), :].rearrange("p o d -> p (o d)")
            v.tensor_tensor(row, row, self.pe1[:, u, 0:D], ALU.add).then_inc(self.h2_set, 1)
        run_slots(dve, TT, 1, mix, 4)

    def sync(self, sp, bs_st, heads):
        for n in range(4):
            sp.wait_ge(bs_st[n], 112)
        sp.dma_start(self.hall[:, 0:TT], self.base_d.rearrange("(i t) b d -> (t b) i d", t=2)).then_inc(self.s["base_ld"], 16)
        if heads:
            sp.wait_ge(self.qkv_free, NWT)
            heads.load_weights(sp)
        for g in range(5):
            sp.wait_ge(self.h2_set, 5 * g + 9)
            for q in range(2):
                dst = self.h2_d.rearrange("b (i t) d -> t b i d", t=2)[q, :, 5 * g:5 * g + 5, :]
                sp.dma_start(dst, self.hall[q * B:(q + 1) * B, 5 * g:5 * g + 5]).then_inc(self.s["h2_st"], 16)
        if not heads:
            sp.wait_ge(self.s["h2_st"], 160)


class Heads:

    def __init__(self, nc, ctx, sb, sem, A, const, ones, colg, x2, kbd, hall, h2_d, xs_d, yy_d, out, pe1, pt1, pp, s):
        self.nc, self.A, self.const, self.ones, self.colg, self.x2, self.kbd, self.hall = nc, A, const, ones, colg, x2, kbd, hall
        self.h2_d, self.xs_d, self.yy_d, self.out = h2_d, xs_d, yy_d, out
        self.pe1, self.pt1, self.pp, self.s = pe1, pt1, pp, s
        self.wqk = sb("wqk", [H2 + 1, 2, 3 * D])
        self.wproj = sb("wproj", [H2 + 1, 2, D])
        self.wgate = sb("wgate", [H2, 2, E])
        self.n2 = sb("n2", [P, 2, D])
        self.gates = sb("gates", [P, NP, 2])
        self.egs = sb("egs", [P, NP])
        self.meta = sb("meta", [1, 3, NT], I32)
        self.w1s = sb("w1s", [H2, E, 2 * HID])
        self.w2s = sb("w2s", [P, E, HC * D])
        self.b1s = sb("b1s", [P, E, HC])
        self.b2s = sb("b2s", [P, E, D])
        own = ExitStack()
        self.st = sb("st", [P, 32], to=own)
        self.bn = sb("bn", [P, 2, 6], to=own)
        self.xh2 = sb("xh2", [P, D], to=own)
        self.xT2 = sb("xT2", [H2 + 1, 2, P], to=own)
        self.qT = sb("qT", [H2, 2, P], to=own)
        self.vbd = sb("vbd", [P, 2, 6, 2 * (AHD + 1)], to=own)
        self.pm = sb("pm", [P, AH, B], to=own)
        self.mx2 = sb("mx2", [P, AH], to=own)
        self.pT = sb("pT", [P, 6, P], to=own)
        self.on = sb("on", [P, D], to=own)
        self.onT = sb("onT", [H2 + 1, 2, P], to=own)
        self.xn = sb("xn", [P, 2, D], to=own)
        self.xsrc = sb("xsrc", [P, 2, 2, DX], to=own)
        self.xnT2 = sb("xnT2", [H2, 2, P], to=own)
        self.lg = sb("lg", [P, E], to=own)
        self.m8 = sb("m8", [P, E], to=own)
        self.i8 = sb("i8", [P, E], U32, to=own)
        self.idx = sb("idx", [P, 2], to=own)
        self.oh = sb("oh", [P, 2, E], to=own)
        self.ohs = sb("ohs", [P, E], to=own)
        self.acc = sb("acc", [P, E], to=own)
        self.t8 = sb("t8", [P, 3, E], to=own)
        self.df = sb("df", [P, 2], to=own)
        self.dst = sb("dst", [P, 2, 2], I32, to=own)
        self.zero = sb("zero", [P, DX], to=own)
        self.mf = sb("mf", [P, 6, NT * E], to=own)
        self.nf = sb("nf", [P, 4, E], to=own)
        own.close()
        self.yl = x2[:].rearrange("p (a i k) d -> p a i k d", a=4, i=4)
        self.xdum = sb("xdum", [P, 2])
        self.yixs = sb("yixs", [P, NT], I32)
        self.yix = sb("yix", [P, 2], I32)
        self.w1 = sb("ew1", [H2, 2, 2, HID])
        self.b1 = sb("eb1", [P, 2, HC])
        self.xs = sb("xs", [P, 2, DX])
        self.xsT = sb("xsT", [H2, 2, ROWS])
        self.hT = sb("hT", [P, 2, HC, ROWS])
        self.ys = sb("ys", [P, 2, D])
        self.a_var, self.a_r, self.a_x, self.a_xh, self.a_T, self.a_xT = sem("a_var"), sem("a_r"), sem("a_x"), sem("a_xh"), sem("a_T"), sem("a_xT")
        self.a_qkv, self.a_q, self.a_v, self.a_k, self.b_s, self.b_sub = sem("a_qkv"), sem("a_q"), sem("a_v"), sem("a_k"), sem("b_s"), sem("b_sub")
        self.b_ex, self.b_pT, self.b_pTo, self.b_pv, self.b_on = sem("b_ex"), sem("b_pT"), sem("b_pTo"), sem("b_pv"), sem("b_on")
        self.c_T, self.c_out, self.c_proj, self.c_var, self.c_r = sem("c_T"), sem("c_out"), sem("c_proj"), sem("c_var"), sem("c_r")
        self.c_x, self.c_xn, self.c_nT, self.d_out, self.d_lg, self.d_oh = sem("c_x"), sem("c_xn"), sem("c_nT"), sem("d_out"), sem("d_lg"), sem("d_oh")
        self.d_rank, self.d_eg, self.d_dst, self.d_src = sem("d_rank"), sem("d_eg"), sem("d_dst"), sem("d_src")
        self.h_in, self.hw_ld, self.init, self.tot, self.meta_set = sem("h_in"), sem("hw_ld"), sem("init"), sem("tot"), sem("meta_set")
        self.zero_st, self.e_T, self.e_xT, self.e_h, self.e_g = sem("zero_st"), sem("e_T"), sem("e_xT"), sem("e_h"), sem("e_g")
        self.e_y, self.e_out, self.y_free, self.dum_set = sem("e_y"), sem("e_out"), sem("y_free"), sem("dum_set")
        self.o_st, self.res_set, self.d_lgo, self.xs_used, self.o_set = sem("o_st"), sem("res_set"), sem("d_lgo"), sem("xs_used"), sem("o_set")
        self.h_ld = [sem(f"h_ld{n}") for n in range(4)]
        self.scat = [sem("scat0"), sem("scat1")]
        self.e_w = [sem("e_w0"), sem("e_w1")]
        self.ew_ld, self.e_wc, self.y2_set = sem("ew_ld"), sem("e_wc"), sem("y2_set")
        self.e_st = [sem("e_st0"), sem("e_st1")]
        self.y_ld = [sem(f"y_ld{n}") for n in range(4)]

    def zero_tails(self, eng, experts):
        for e in experts:
            at = eng.value_load(self.meta[0:1, 2, e:e + 1], min_val=0, max_val=E * R - ROWS)
            eng.dma_start(self.xs_d[bass.ds(at, ROWS)], self.zero[:]).then_inc(self.zero_st, 16)

    def gpsimd(self, pool):
        nc, st, g = self.nc, self.st, self.nc.gpsimd
        pool.wait_ge(self.init, 2)
        eps, mhalf = self.const[:, C_EPS:C_EPS + 1], self.const[:, C_NH:C_NH + 1]

        def slot(item):
            a, b, c, d = item(0), item(4), item(3), item(7)
            if a:
                i = a[0]
                pool.wait_ge(self.a_T, i)
                pool.wait_ge(self.a_var, i + 1)
                g.tensor_tensor(st[:, 2:3], st[:, 1:2], eps, ALU.add)
                pool.drain()
                g.tensor_tensor(st[:, 2:3], st[:, 2:3], mhalf, ALU.pow)
                pool.drain()
                g.tensor_tensor(st[:, 3:4], st[:, 1:2], st[:, 2:3], ALU.mult)
                pool.drain()
                g.tensor_tensor(st[:, 3:4], st[:, 3:4], st[:, 2:3], ALU.mult)
                pool.drain()
                g.tensor_tensor(st[:, 3:4], st[:, 3:4], eps, ALU.add)
                pool.drain()
                g.tensor_tensor(st[:, 3:4], st[:, 3:4], mhalf, ALU.pow).then_inc(self.a_r, 1)
            if b:
                pool.wait_ge(self.c_x, b[0] + 1)
                g.tensor_tensor(self.xn[:, b[1]], self.xn[:, b[1]], self.n2[:, 0], ALU.mult)
            if d:
                i, u, _ = d
                pool.wait_ge(self.d_src, i + 2)
                pool.wait_ge(self.d_dst, i + 1)
                g.tensor_copy(self.xsrc[:, u, :, D:DX], self.const[:, C_ROW:C_ROW + 2 * NP].rearrange("p (i k) -> p i k", k=2)[:, bass.ds(i, 1), :].rearrange("p o k -> p k o"))
            pool.drain()
            if d:
                for k in range(2):
                    g.indirect_dma_start(self.xs_d[:, :], bass.IndirectOffsetOnAxis(ap=self.dst[:, u, k:k + 1], axis=0),
                                         self.xsrc[:, u, k], None, bounds_check=E * R - 1, oob_is_err=False).then_inc(self.scat[u], 16)
            if b:
                g.tensor_tensor(self.xn[:, b[1]], self.xn[:, b[1]], self.n2[:, 1], ALU.add).then_inc(self.c_xn, 1)
            if c:
                i = c[0]
                pool.wait_ge(self.c_var, i + 1)
                g.tensor_tensor(st[:, 8:9], st[:, 7:8], eps, ALU.add)
                pool.drain()
                g.tensor_tensor(st[:, 8:9], st[:, 8:9], mhalf, ALU.pow).then_inc(self.c_r, 1)
                rows = [t[:, bass.ds(i, 1), :].rearrange("p o d -> p (o d)") for t in (self.hall, self.x2)]
                g.tensor_tensor(rows[0], rows[0], rows[1], ALU.add).then_inc(self.res_set, 1)
        run_slots(pool, NP, 8, slot)

        held = self.xdum[:, 0:1], self.xdum[:, 1:2]

        def expert(item):
            if (a := item(4)):
                i, u, h = a
                pool.drain()
                pool.wait_ge(self.e_out, i + 1)
                pool.wait_ge(self.e_st[u], 16 * h)
                g.tensor_tensor(held[0], held[1], held[1], ALU.add)
                g.tensor_copy(self.yix[:, u:u + 1], self.yixs[:, bass.ds(i, 1)])
                pool.drain()
                g.indirect_dma_start(self.yy_d[:, :], bass.IndirectOffsetOnAxis(ap=self.yix[:, u:u + 1], axis=0),
                                     self.ys[:, u], None, bounds_check=2 * NP * P - 1, oob_is_err=False).then_inc(self.e_st[u], 16)
            if (b := item(1)):
                i, u, h = b
                pool.drain()
                pool.wait_ge(self.e_w[u], 16 * h + 16)
                g.tensor_tensor(held[0], held[1], held[1], ALU.add)
                g.tensor_copy(self.yixs[:, bass.ds(i, 1)], self.xs[:, u, D:DX]).then_inc(self.xs_used, 1)
        pool.wait_ge(self.dum_set, 1)
        run_slots(pool, NT, 5, expert)

    def vector(self, dve):
        nc, v, st, const, hall, x2 = self.nc, self.nc.vector, self.st, self.const, self.hall, self.x2
        pe1, pp = self.pe1, self.pp
        dve.drain()
        v.memset(self.pm[:], 0.0)
        v.memset(self.vbd[:], 0.0)
        dve.drain()
        v.memset(self.vbd[0:T, :, :, AHD:AHD + 1], 1.0)
        v.memset(self.vbd[B:B + T, :, :, 2 * AHD + 1:2 * AHD + 2], 1.0)
        v.memset(self.acc[:], 0.0)
        v.memset(self.xT2[H2:H2 + 1, 1], 1.0)
        v.memset(self.onT[H2:H2 + 1, 1], 1.0)
        v.memset(self.zero[:], 0.0)
        dve.drain()
        v.memset(self.zero[:, D:DX], float(FAR))
        dve.drain().then_inc(self.init, 2)
        dve.drain().then_inc(self.e_T, 2)
        dve.drain().then_inc(self.y_free, 2)
        dve.drain().then_inc(self.e_g, 4)
        dve.drain().then_inc(self.xs_used, 2)
        dve.drain().then_inc(self.d_src, 1)
        dve.wait_ge(self.hw_ld, 16 * 7)

        def row(t, i):
            return t[:, bass.ds(i, 1), :].rearrange("p o d -> p (o d)")

        def slot(item):
            n0, n1, n2, n3, n4, n6 = (item(lag) and item(lag)[0] for lag in (0, 1, 2, 3, 4, 6))
            if n4 is not None:
                xn = self.xn[:, item(4)[1]]
            lg = self.lg
            dve.drain()
            if n6 is not None:
                dve.wait_ge(self.d_lg, n6 + 1)
                v.tensor_copy(lg[:], pe1[:, 3, 256:256 + E]).then_inc(self.d_lgo, 1)
            dve.drain()
            if n6 is not None:
                v.max(self.m8[:], lg[:])
            if n0 is not None:
                dve.wait_ge(self.h_in, n0 + 1)
                v.bn_stats(self.bn[:, 0], row(hall, n0))
            if n2 is not None:
                dve.wait_ge(self.b_s, n2 + 1)
                sc = pe1[:, 0:2, 0:6 * T].rearrange("p n (h k) -> p n h k", h=6)
                v.tensor_reduce(self.mx2[:].rearrange("p (n h) -> p n h", n=2), sc, X, ALU.max)
            if n4 is not None:
                dve.wait_ge(self.c_r, n4 + 1)
                dve.wait_ge(self.d_src, n4)
                v.tensor_scalar(xn, row(x2, n4), st[:, 6:7], st[:, 8:9], ALU.subtract, ALU.mult).then_inc(self.c_x, 1)
            dve.drain()
            if n6 is not None:
                v.max_index(self.i8[:], self.m8[:], lg[:])
                dve.wait_ge(self.d_eg, n6)
                v.tensor_tensor(st[:, 12:13], self.m8[:, 1:2], self.m8[:, 0:1], ALU.subtract)
            if n0 is not None:
                v.bn_aggr(st[:, 0:2], self.bn[:, 0]).then_inc(self.a_var, 1)
            if n2 is not None:
                v.tensor_tensor(self.pm[:].rearrange("p (n h) k -> p n h k", n=2)[:, :, :, 0:T], sc,
                                self.mx2[:].rearrange("p (n h) -> p n h", n=2).unsqueeze(3).to_broadcast([P, 2, 6, T]),
                                ALU.subtract).then_inc(self.b_sub, 1)
            dve.drain()
            if n6 is not None:
                v.tensor_copy(self.idx[:], self.i8[:, 0:2])
            if n1 is not None:
                dve.wait_ge(self.a_qkv, n1 + 1)
                for m in range(2):
                    for h in range(2):
                        k = pp[0:H2, 1, h * P + m * B:h * P + m * B + T].unsqueeze(1).to_broadcast([H2, 6, T])
                        last = v.tensor_tensor(self.kbd[:, m, h], k, const[0:H2, C_KM:C_KM + 6].unsqueeze(2).to_broadcast([H2, 6, T]), ALU.mult)
                last.then_inc(self.a_k, 1)
            dve.drain()
            if n6 is not None:
                for k in range(2):
                    v.tensor_scalar(self.oh[:, k], const[:, C_EI:C_EI + E], self.idx[:, k:k + 1], const[:, C_VAL:C_VAL + 1],
                                    ALU.is_equal, ALU.mult)
                dve.drain()
                v.tensor_tensor(self.ohs[:], self.oh[:, 0], self.oh[:, 1], ALU.add).then_inc(self.d_oh, 1)
            if n0 is not None:
                dve.wait_ge(self.a_r, n0 + 1)
                v.tensor_scalar(row(x2, n0), row(hall, n0), st[:, 0:1], st[:, 2:3], ALU.subtract, ALU.mult).then_inc(self.a_x, 1)
            if n3 is not None:
                dve.wait_ge(self.c_proj, n3 + 1)
                v.tensor_tensor(row(x2, n3), row(x2, n3), pe1[:, 2, 256:256 + D], ALU.add)
                dve.drain()
                v.bn_stats(self.bn[:, 1], row(x2, n3))
            o = pe1[:, 1, 0:AH * (AHD + 1)].rearrange("p (h d) -> p h d", h=AH)
            if n2 is not None:
                dve.wait_ge(self.b_pv, n2 + 1)
                v.reciprocal(self.mx2[:], o[:, :, AHD:AHD + 1].rearrange("p h o -> p (h o)"))
            dve.drain()
            if n2 is not None:
                v.tensor_tensor(self.on[:].rearrange("p (h d) -> p h d", h=AH), o[:, :, 0:AHD],
                                self.mx2[:].unsqueeze(2).to_broadcast([P, AH, AHD]), ALU.mult).then_inc(self.b_on, 1)
            if n3 is not None:
                v.bn_aggr(st[:, 6:8], self.bn[:, 1]).then_inc(self.c_var, 1)
            if n6 is not None:
                dve.wait_ge(self.d_rank, n6 + 1)
                t = self.t8
                v.tensor_tensor(t[:, 0], self.pt1[:, 1, 0:E], const[:, C_ER:C_ER + E], ALU.add)
                v.tensor_tensor(self.acc[:], self.acc[:], self.ohs[:], ALU.add)
                dve.drain()
                v.tensor_tensor(t[:, 1:3], self.oh[:], t[:, 0:1].to_broadcast([P, 2, E]), ALU.mult)
                dve.drain()
                v.tensor_reduce(self.df[:], t[:, 1:3], X, ALU.add)
                dve.drain()
                dve.wait_ge(self.scat[item(6)[1]], 32 * item(6)[2])
                v.tensor_scalar(self.dst[:, item(6)[1]], self.df[:], const[:, C_VAL + 1:C_VAL + 2], None, ALU.add).then_inc(self.d_dst, 1)
        run_slots(dve, NP, 8, slot)

        dve.drain().then_inc(self.tot, 1)
        dve.wait_ge(self.tot, 2)
        nf, mf = self.nf, self.mf
        cnt, cnt256, nt, cum = (nf[:, n] for n in range(4))
        ge = mf[:, 0].rearrange("p (j e) -> p j e", e=E)
        js, ers = const[:, C_J:C_J + NT], const[:, C_ER:C_ER + E]
        v.tensor_copy(cnt, pe1[:, 3, 0:E])
        dve.drain()
        v.tensor_scalar(cnt256, cnt, 1 / ROWS, None, ALU.mult)
        dve.drain()
        ng = NT // 2
        gt = mf[:, 1, 0:E * ng].rearrange("p (e m) -> p e m", e=E)
        v.tensor_tensor(gt, cnt256.unsqueeze(2).to_broadcast([P, E, ng]), js[:, 0:ng].unsqueeze(1).to_broadcast([P, E, ng]), ALU.is_gt)
        dve.drain()
        v.tensor_reduce(nt, gt, X, ALU.add)
        dve.drain()
        pr = mf[:, 2, 0:E * E].rearrange("p (e f) -> p e f", e=E)
        v.tensor_tensor(pr, const[:, C_L8:C_L8 + E * E].rearrange("p (e f) -> p e f", e=E), nt.unsqueeze(1).to_broadcast([P, E, E]), ALU.mult)
        dve.drain()
        v.tensor_reduce(cum, pr, X, ALU.add)
        dve.drain()
        v.tensor_tensor(ge, js.unsqueeze(2).to_broadcast([P, NT, E]), cum.unsqueeze(1).to_broadcast([P, NT, E]), ALU.is_ge)
        dve.drain()
        te, tl = mf[:, 3, 0:NT], mf[:, 4, 0:NT]
        v.tensor_reduce(te, ge, X, ALU.add)
        v.tensor_tensor(mf[:, 5].rearrange("p (j e) -> p j e", e=E), ge, nt.unsqueeze(1).to_broadcast([P, NT, E]), ALU.mult)
        dve.drain()
        v.tensor_reduce(tl, mf[:, 5].rearrange("p (j e) -> p j e", e=E), X, ALU.add)
        dve.drain()
        v.tensor_tensor(tl, js, tl, ALU.subtract)
        dve.drain()
        v.tensor_scalar(tl, tl, float(ROWS), None, ALU.mult)
        dve.drain()
        v.scalar_tensor_tensor(tl, te, float(R), tl, ALU.mult, ALU.add)
        dve.drain()
        v.tensor_scalar(self.meta[:, 0], te[0:1], float(E - 1), None, ALU.min)
        v.tensor_scalar(self.meta[:, 1], tl[0:1], float(E * R), None, ALU.min)
        v.tensor_tensor(self.meta[:, 2, 0:E], cnt[0:1], ers[0:1], ALU.add)
        dve.drain().then_inc(self.meta_set, 1)
        dve.wait_ge(self.d_eg, NP)
        g1, g2 = self.gates[:, :, 0], self.gates[:, :, 1]
        v.tensor_scalar(g1, self.egs[:], 1.0, None, ALU.add)
        dve.drain()
        v.reciprocal(g1, g1)
        dve.drain()
        v.tensor_tensor(g2, g1, self.egs[:], ALU.mult)
        for n in range(2):
            dve.wait_ge(self.scat[n], 16 * NP)
        v.memset(self.xdum[:], 0.0).then_inc(self.dum_set, 1)

        dve.wait_ge(self.ew_ld, 16 * 4)

        def expert(item):
            if (a := item(1)):
                i, u, h = a
                e = dve.value_load(self.meta[0:1, 0, bass.ds(i, 1)], min_val=0, max_val=E - 1)
                dve.wait_ge(self.e_g, 2 * i + 2)
                v.tensor_copy(self.b1[:, u], self.b1s[:, bass.ds(e, 1), :].rearrange("p o c -> p (o c)"))
                v.tensor_copy(self.w1[:, u].rearrange("p h f -> p (h f)"), self.w1s[:, bass.ds(e, 1), :].rearrange("p o f -> p (o f)"))
                dve.drain().then_inc(self.e_wc, 1)
            if (c := item(3)):
                i, u, h = c
                e = dve.value_load(self.meta[0:1, 0, bass.ds(i, 1)], min_val=0, max_val=E - 1)
                dve.wait_ge(self.e_y, i + 1)
                dve.wait_ge(self.e_st[u], 16 * h)
                v.tensor_tensor(self.ys[:, u], pp[:, u, 0:D], self.b2s[:, bass.ds(e, 1), :].rearrange("p o d -> p (o d)"), ALU.add).then_inc(self.e_out, 1)
                dve.drain().then_inc(self.y_free, 1)
        run_slots(dve, NT, 5, expert)

        dve.wait_ge(self.res_set, NP)
        for n in range(NP // 4):
            dve.wait_ge(self.y_ld[n % 4], 32 * (n // 4) + 32)
            for i in range(4):
                m = 4 * n + i
                v.scalar_tensor_tensor(hall[:, m], self.yl[:, n % 4, i, 0], self.gates[:, m, 0:1], hall[:, m], ALU.mult, ALU.add)
            dve.drain()
            dve.wait_ge(self.y2_set, n + 1)
            v.tensor_tensor(hall[:, 4 * n:4 * n + 4], hall[:, 4 * n:4 * n + 4], self.yl[:, n % 4, :, 1], ALU.add).then_inc(self.o_set, 1)

    def scalar(self, act):
        nc, f, pe1, pt1, pp, colg = self.nc, self.nc.scalar.activation, self.pe1, self.pt1, self.pp, self.colg
        act.wait_ge(self.init, 2)

        def slot(item):
            n0, n1, n2, n5, n6 = (item(lag) and item(lag)[0] for lag in (0, 1, 2, 5, 6))
            if n2 is not None:
                act.wait_ge(self.b_sub, n2 + 1)
                f(self.pm[:, :, 0:T], self.pm[:, :, 0:T], ACT.Exp, scale=AHD ** -0.5).then_inc(self.b_ex, 1)
            if n1 is not None:
                act.wait_ge(self.a_qkv, n1 + 1)
                f(self.qT[:], pp[0:H2, 0, 0:2 * P].rearrange("p (h n) -> p h n", h=2), ACT.Copy).then_inc(self.a_q, 1)
            if n5 is not None:
                act.wait_ge(self.c_nT, n5 + 1)
                f(self.xnT2[:], pe1[0:H2, 3, 0:2 * P].rearrange("p (h n) -> p h n", h=2), ACT.Copy).then_inc(self.d_out, 1)
            if n2 is not None:
                act.wait_ge(self.b_pT, n2 + 1)
                f(self.pT[:, 0:4].rearrange("p h n -> p (h n)"), pe1[:, 0], ACT.Copy)
                f(self.pT[:, 4:6].rearrange("p h n -> p (h n)"), pe1[:, 1, 0:2 * P], ACT.Copy).then_inc(self.b_pTo, 1)
            if n6 is not None:
                act.wait_ge(self.d_oh, n6 + 1)
                f(self.egs[:, bass.ds(n6, 1)], self.st[:, 12:13], ACT.Exp).then_inc(self.d_eg, 1)
            if n0 is not None:
                act.wait_ge(self.a_x, n0 + 1)
                f(self.xh2[:], self.x2[:, bass.ds(n0, 1), :].rearrange("p o d -> p (o d)"), ACT.Copy, scale=self.st[:, 3:4]).then_inc(self.a_xh, 1)
                act.wait_ge(self.a_T, n0 + 1)
                for h in range(2):
                    last = f(self.xT2[0:H2, h], pt1[0:H2, 0, h * P:(h + 1) * P], ACT.Identity, bias=colg[:, h, 4:5], scale=colg[:, h, 3:4])
                last.then_inc(self.a_xT, 1)
            if n1 is not None:
                act.wait_ge(self.b_pv, n1)
                for m in range(2):
                    for e in range(2):
                        src = pp[m * B:m * B + T, 0, 256:256 + D].rearrange("p (h e d) -> p h e d", e=2, d=AHD)[:, :, e]
                        last = f(self.vbd[e * B:e * B + T, m, :, e * (AHD + 1):e * (AHD + 1) + AHD], src, ACT.Copy)
                last.then_inc(self.a_v, 1)
            if n2 is not None:
                act.wait_ge(self.c_T, n2 + 1)
                f(self.onT[0:H2], pe1[0:H2, 2, 0:2 * P].rearrange("p (h n) -> p h n", h=2), ACT.Copy).then_inc(self.c_out, 1)
            if n5 is not None:
                u = item(5)[1]
                act.wait_ge(self.c_xn, n5 + 1)
                act.wait_ge(self.scat[u], 32 * item(5)[2])
                f(self.xsrc[:, u, :, 0:D], self.xn[:, u:u + 1].to_broadcast([P, 2, D]), ACT.Copy).then_inc(self.d_src, 1)
        run_slots(act, NP, 8, slot)
        act.wait_ge(self.meta_set, 1)
        self.zero_tails(act, range(1, E, 2))

        def expert(item):
            if not (b := item(1)):
                return
            i, u, h = b
            act.wait_ge(self.e_T, i + 3)
            f(self.xsT[:], pt1[0:H2, u, 0:2 * ROWS].rearrange("p (h n) -> p h n", h=2), ACT.Copy).then_inc(self.e_xT, 1)

        def hidden(item):
            if not (b := item(2)):
                return
            i, u, h = b
            act.wait_ge(self.e_wc, i + 1)
            act.wait_ge(self.y_free, i + 1)
            for c in range(HC):
                if c % 3 == 0:
                    act.wait_ge(self.e_h, 2 * i + c // 3 + 1)
                last = f(self.hT[:, u, c], pe1[:, 2 * u + c // 3, (c % 3) * ROWS:(c % 3 + 1) * ROWS], ACT.Gelu, bias=self.b1[:, u, c:c + 1])
                if c % 3 == 2:
                    last.then_inc(self.e_g, 1)

        def both(item):
            hidden(item)
            expert(item)
        run_slots(act, NT, 5, both)

        for n in range(NP // 4):
            act.wait_ge(self.y_ld[n % 4], 32 * (n // 4) + 32)
            for i in range(4):
                y = self.yl[:, n % 4, i, 1]
                last = f(y, y, ACT.Copy, scale=self.gates[:, 4 * n + i, 1:2])
            last.then_inc(self.y2_set, 1)

    def tensor(self, pe):
        nc, mm, T_, pe1, pt1, pp = self.nc, self.nc.tensor.matmul, self.nc.tensor.transpose, self.pe1, self.pt1, self.pp
        ident, const = self.const[:, C_ID:C_ID + P], self.const
        pe.wait_ge(self.init, 2)
        pe.wait_ge(self.hw_ld, 16 * 7)

        def slot(item):
            n0, n1, n2, n3, n5, n6 = (item(lag) and item(lag)[0] for lag in (0, 1, 2, 3, 5, 6))
            if n2 is not None:
                pe.wait_ge(self.a_q, n2 + 1)
                pe.wait_ge(self.a_k, n2 + 1)
                pe.wait_ge(self.b_on, n2)
                for m in range(2):
                    for h in range(2):
                        last = mm(pe1[m * B:(m + 1) * B, h, 0:6 * T], self.qT[:, h, m * B:(m + 1) * B],
                                  self.kbd[:, m, h].rearrange("p h k -> p (h k)"), start=True, stop=True)
                last.then_inc(self.b_s, 1)
            if n1 is not None:
                pe.wait_ge(self.a_xT, n1 + 1)
                pe.wait_ge(self.a_v, n1)
                pe.wait_ge(self.a_k, n1)
                for g in range(2):
                    for m in range(2):
                        for h in range(2):
                            rows = H2 + h
                            mm(pp[0:H2, g, m * P:(m + 1) * P], self.wqk[0:rows, h, g * D + m * H2:g * D + (m + 1) * H2],
                               self.xT2[0:rows, h], start=(h == 0), stop=(h == 1))
                for h in range(2):
                    last = mm(pp[:, 0, 256:256 + D], self.xT2[0:H2 + h, h], self.wqk[0:H2 + h, h, 2 * D:3 * D], start=(h == 0), stop=(h == 1))
                last.then_inc(self.a_qkv, 1)
            if n5 is not None:
                pe.wait_ge(self.c_xn, n5 + 1)
                pe.wait_ge(self.d_lgo, n5)
                for h in range(2):
                    last = T_(pe1[0:H2, 3, h * P:(h + 1) * P], self.xn[:, item(5)[1], h * H2:(h + 1) * H2], ident)
                last.then_inc(self.c_nT, 1)
            if n2 is not None:
                pe.wait_ge(self.b_ex, n2 + 1)
                for n in range(6):
                    last = T_(pe1[:, n // 4, (n % 4) * P:(n % 4 + 1) * P], self.pm[:, 2 * n:2 * n + 2].rearrange("p h k -> p (h k)"), ident)
                last.then_inc(self.b_pT, 1)
            if n3 is not None:
                pe.wait_ge(self.c_out, n3 + 1)
                mm(pe1[:, 2, 256:256 + D], self.onT[0:H2, 0], self.wproj[0:H2, 0], start=True, stop=False)
                mm(pe1[:, 2, 256:256 + D], self.onT[:, 1], self.wproj[:, 1], start=False, stop=True).then_inc(self.c_proj, 1)
            if n5 is not None:
                pe.wait_ge(self.d_out, n5 + 1)
                for h in range(2):
                    last = mm(pe1[:, 3, 256:256 + E], self.xnT2[:, h], self.wgate[:, h], start=(h == 0), stop=(h == 1))
                last.then_inc(self.d_lg, 1)
            if n2 is not None:
                pe.wait_ge(self.b_pTo, n2 + 1)
                pe.wait_ge(self.a_v, n2 + 1)
                w = 2 * (AHD + 1)
                for m in range(2):
                    for n in range(6):
                        last = mm(pe1[m * B:(m + 1) * B, 1, n * w:(n + 1) * w], self.pT[:, n, m * B:(m + 1) * B], self.vbd[:, m, n], start=True, stop=True)
                last.then_inc(self.b_pv, 1)
            if n0 is not None:
                pe.wait_ge(self.a_xh, n0 + 1)
                pe.wait_ge(self.a_xT, n0)
                for h in range(2):
                    last = T_(pt1[0:H2, 0, h * P:(h + 1) * P], self.xh2[:, h * H2:(h + 1) * H2], ident)
                last.then_inc(self.a_T, 1)
            if n6 is not None:
                pe.wait_ge(self.d_oh, n6 + 1)
                pe.wait_ge(self.d_dst, n6)
                mm(pt1[:, 1, 0:E], self.ones[:], self.acc[:], start=True, stop=False)
                mm(pt1[:, 1, 0:E], const[:, C_TRI:C_TRI + P], self.ohs[:], start=False, stop=True).then_inc(self.d_rank, 1)
            if n2 is not None:
                pe.wait_ge(self.b_on, n2 + 1)
                pe.wait_ge(self.c_var, n2)
                for h in range(2):
                    last = T_(pe1[0:H2, 2, h * P:(h + 1) * P], self.on[:, h * H2:(h + 1) * H2], ident)
                last.then_inc(self.c_T, 1)
        run_slots(pe, NP, 8, slot)
        pe.wait_ge(self.tot, 1)
        mm(pe1[:, 3, 0:E], self.ones[:], self.acc[:], start=True, stop=True).then_inc(self.tot, 1)
        pe.wait_ge(self.meta_set, 1)

        def expert(item):
            if (b := item(2)):
                i, u, h = b
                pe.wait_ge(self.e_xT, i + 1)
                pe.wait_ge(self.e_wc, i + 1)
                for n in range(HC):
                    for m in range(2):
                        last = mm(pe1[:, 2 * u + n // 3, (n % 3) * ROWS:(n % 3 + 1) * ROWS], self.w1[:, u, m, n * P:(n + 1) * P], self.xsT[:, m], start=(m == 0), stop=(m == 1))
                    if n % 3 == 2:
                        last.then_inc(self.e_h, 1)
            if (a := item(1)):
                i, u, h = a
                pe.wait_ge(self.e_w[u], 16 * h + 16)
                for n in range(2):
                    last = T_(pt1[0:H2, u, n * ROWS:(n + 1) * ROWS], self.xs[:, u, n * H2:(n + 1) * H2], ident)
                last.then_inc(self.e_T, 1)
            if (c := item(3)):
                i, u, h = c
                e = pe.value_load(self.meta[0:1, 0, bass.ds(i, 1)], min_val=0, max_val=E - 1)
                pe.wait_ge(self.e_g, 2 * i + 6)
                pe.wait_ge(self.y_free, i + 1)
                for n in range(HC):
                    last = mm(pp[:, u, 0:D], self.hT[:, u, n], self.w2s[:, bass.ds(e, 1), n * D:(n + 1) * D].rearrange("p o d -> p (o d)"), start=(n == 0), stop=(n == HC - 1))
                last.then_inc(self.e_y, 1)
        pe.wait_ge(self.ew_ld, 16 * 4)
        run_slots(pe, NT, 5, expert)

    def load_weights(self, sp):
        A = self.A
        for dst, src in ((self.wqk[0:H2], A["qkvT"]), (self.wqk[H2:H2 + 1, 1], A["qkvb"]), (self.wproj[0:H2], A["projT"]),
                         (self.wproj[H2:H2 + 1, 1], A["projb"]), (self.wgate[:], A["wgate"]), (self.n2[:, 0], A["n2"][0:1].to_broadcast([P, D])),
                         (self.n2[:, 1], A["n2"][1:2].to_broadcast([P, D]))):
            sp.dma_start(dst, src).then_inc(self.hw_ld, 16)

    def sync(self, sp):
        A, hall = self.A, self.hall
        sp.wait_ge(self.s["h2_st"], 160)
        starts = (0, NP // 16, NP // 4, NP // 2, NP)
        for g in range(4):
            for q in range(2):
                src = self.h2_d.rearrange("(i q) t d -> q t i d", q=2)[q, 0:T]
                sp.dma_start(hall[q * B:q * B + T, starts[g]:starts[g + 1]], src[:, starts[g]:starts[g + 1]]).then_inc(self.h_ld[g], 16)
        for g in range(4):
            sp.wait_ge(self.h_ld[g], 32)
            sp.drain().then_inc(self.h_in, starts[g + 1] - starts[g])
        sp.wait_ge(self.init, 2)
        sp.dma_start(self.xs_d[E * R:E * R + ROWS], self.zero[:]).then_inc(self.zero_st, 16)
        for dst, src in ((self.w1s[:], A["W1"].rearrange("e p h f -> p e (h f)")), (self.w2s[:], A["W2"].rearrange("e p c d -> p e (c d)")),
                         (self.b1s[:], A["b1"].rearrange("e p c -> p e c")),
                         (self.b2s[:].rearrange("p e d -> p (e d)"), A["b2"].rearrange("e d -> (e d)").unsqueeze(0).to_broadcast([P, E * D]))):
            sp.dma_start(dst, src).then_inc(self.ew_ld, 16)
        sp.wait_ge(self.meta_set, 1)
        self.zero_tails(sp, range(0, E, 2))
        for n in range(2):
            sp.wait_ge(self.scat[n], 16 * NP)
        sp.wait_ge(self.zero_st, 16 * (E + 1))
        sp.wait_ge(self.d_eg, NP)

        def slot(item):
            i, u, h = item(0)
            at = sp.value_load(self.meta[0:1, 1, bass.ds(i, 1)], min_val=0, max_val=E * R)
            sp.wait_ge(self.e_T, i + 1)
            sp.wait_ge(self.xs_used, i + 1)
            sp.dma_start(self.xs[:, u], self.xs_d[bass.ds(at, ROWS)]).then_inc(self.e_w[u], 16)
        run_slots(sp, NT, 1, slot)

        sp.wait_ge(self.dum_set, 1)
        for n in range(2):
            sp.wait_ge(self.e_st[n], (NT + 1 - n) // 2 * 16)

        def load(n):
            for q in range(2):
                src = self.yy_d.rearrange("(i q t k) d -> q t i k d", q=2, t=B, k=2)[q, 0:T, 4 * n:4 * n + 4]
                sp.dma_start(self.yl[q * B:q * B + T, n % 4], src).then_inc(self.y_ld[n % 4], 16)

        for n in range(4):
            load(n)
        for n in range(NP // 4):
            sp.wait_ge(self.o_set, n + 1)
            for q in range(2):
                dst = self.out.rearrange("(i q) t d -> q t i d", q=2)[q, :, 4 * n:4 * n + 4]
                sp.dma_start(dst, hall[q * B:q * B + T, 4 * n:4 * n + 4]).then_inc(self.o_st, 16)
            if n + 4 < NP // 4:
                load(n + 4)
        sp.wait_ge(self.o_st, 256)


def build(nc, A, out, stop=99):
    ctx = ExitStack()
    with ctx:
        def sem(name):
            return ctx.enter_context(nc.semaphore(name))

        def ps(name, shape):
            return ctx.enter_context(nc.psum_tensor(name, shape, F32))

        def sb(name, shape, dt=F32, to=None):
            return (to or ctx).enter_context(nc.sbuf_tensor(name, shape, dt))

        def dram(name, shape, dt=F32):
            return nc.dram_tensor(name, shape, dt, kind="Internal").ap()

        base_d = dram("base_d", [2 * TT, B, D])
        h2_d = dram("h2_d", [B, 2 * TT, D])
        xs_d = dram("xs_d", [NROW, DX])
        yy_d = dram("yy_d", [NP * P * 2, D])

        const = sb("const", [P, NCONST])
        ones = sb("ones", [P, P])
        ident = const[:, C_ID:C_ID + P]
        wqkv = sb("wqkv", [H2 + 1, 2, 3 * D])
        colg = sb("colg", [H2, 2, 5])
        mowT = sb("mowT", [H2, 2, D])
        owT = sb("owT", [H2 + 1, 2, D])

        e2 = ExitStack()
        x2 = sb("x2", [P, NP, D], to=e2)
        kbd = sb("kbd", [H2, 2, 2, 6, T], to=e2)
        e2.close()
        xnT = sb("xnT", [H2, 2, FRONT + POS, B])
        e1 = ExitStack()
        wm = sb("wm", [P, 4, KC, D + 1], to=e1)
        ww = sb("ww", [P, 6, D + 1], to=e1)
        s1b = sb("s1b", [P, D], to=e1)
        s2b = sb("s2b", [P, D], to=e1)
        cb = sb("cb", [P, D], to=e1)
        xm = sb("xm", [P, 2, 2, KC, NA], to=e1)
        x6 = sb("x6", [P, 4, KC, P], to=e1)
        raw = sb("raw", [P, 8 * NA + 8 * NB], to=e1)
        sqs = sb("sqs", [P, 2, 2, NA], to=e1)
        sq6 = sb("sq6", [P, 4, P], to=e1)
        xh = sb("xh", [P, 4, D], to=e1)
        bs = sb("bs", [P, 4, D], to=e1)
        hh = sb("hh", [P, D], to=e1)
        st1 = sb("st1", [P, 24], to=e1)
        bn1 = sb("bn1", [P, 6], to=e1)
        e0 = ExitStack()
        w1 = sb("w1", [P, 5, KC, D], to=e0)
        w2 = sb("w2", [P, 8, D], to=e0)
        gb = sb("gb", [P, 2, 38], to=e0)
        trow = sb("trow", [1, 2, D], to=e0)
        inw = sb("inw", [H2, 2, 3, D], to=e0)
        qkw = sb("qkw", [H2, 2, 3, D + 1], to=e0)
        inb = sb("inb", [H2 + 1, 3 * D], to=e0)
        cw1 = xm[:, 1, 0, :, 0:D]
        cw2 = xm[:, 1, 1, 0:2, 0:D]
        sums = xm[0:2, 1, 1, 2:4, 0:D]
        e0.close()
        wv = sb("wv", [P, 2, 2 * NA + 2 * NB], to=e1)
        wsq = sb("wsq", [P, 2, 2 * NA + 2 * NB], to=e1)
        wv6 = sb("wv6", [P, 6 * P], to=e1)
        wsq6 = sb("wsq6", [P, 6 * P], to=e1)
        sqt = sb("sqt", [P, KC * NA], to=e1)
        e1.close()

        pe1 = ps("pe1", [P, 4, 512])
        pt1 = ps("pt1", [P, 2, 512])
        pp = ps("pp", [P, 2, 512])

        c_ld, gb_ld, w_ld, w_ld2 = sem("c_ld"), sem("gb_ld"), sem("w_ld"), sem("w_ld2")
        w1_ld = [sem(f"w1_ld{n}") for n in range(5)]
        ones_set = sem("ones_set")
        wm_set, sum_mm, sums_set, bias_mm = sem("wm_set"), sem("sum_mm"), sem("sums_set"), sem("bias_mm")
        fold_mm, fold_out = sem("fold_mm"), sem("fold_out")
        x_ld = [sem("x_ld0"), sem("x_ld1"), sem("x_ld6")]
        raw_ld = sem("raw_ld")
        wave_set, wsq_set, sq_half, sq_free, sqs_set = sem("wave_set"), sem("wsq_set"), sem("sq_half"), sem("sq_free"), sem("sqs_set")
        tok_mm, tok_free = sem("tok_mm"), sem("tok_free")
        xh_set, xh_T, xh_out = sem("xh_set"), sem("xh_T"), sem("xh_out")
        bs_set = sem("bs_set")
        var_set, var_r = sem("var_set"), sem("var_r")
        hvar_set, hvar_r = sem("hvar_set"), sem("hvar_r")
        bs_st = [sem(f"bs_st{n}") for n in range(4)]

        NTOK = 25
        s = {"xh_out": xh_out, "tok_mm": tok_mm, "tok_free": tok_free, "base_ld": sem("base_ld"), "h2_st": sem("h2_st")}
        hall = sb("hall", [P, NP, D])
        wins = Windows(nc, ctx, sb, sem, A, const, ones, xnT, wqkv, colg, mowT, owT, hall, base_d, h2_d, pe1, pt1, pp, s) if stop >= 2 else None
        heads = Heads(nc, ctx, sb, sem, A, const, ones, colg, x2, kbd, hall, h2_d, xs_d, yy_d, out, pe1, pt1, pp, s) if stop >= 4 else None
        block = ctx.enter_context(nc.Block())

        def tile_of(r, pos):
            if pos == 3:
                return "last", 6, 14 * r + 6, 7
            i, j = (0, pos) if pos < 3 else (1, pos - 4)
            return i, 2 * j, 14 * r + 7 * i + 2 * j, 1

        eps_col = const[:, C_EPS:C_EPS + 1]

        def minus_half(n):
            return const[:, C_NH:C_NH + n]

        def before(pos):
            return (pos - 1) % 4 if pos else 2

        @block.sync
        def _(sp):
            sp.dma_start(const[:], A["consts"]).then_inc(c_ld, 16)
            sp.dma_start(gb[:], A["gb"]).then_inc(gb_ld, 16)
            for s in (4, 0, 1, 2, 3):
                sp.dma_start(w1[:, s], A["w1"][:, s]).then_inc(w1_ld[s], 16)
            for dst, src in ((w2[:], A["w2"]), (trow[:], A["tok_b"])):
                sp.dma_start(dst, src).then_inc(w_ld, 16)
            for dst, src in ((inw[:], A["inw"]), (qkw[:], A["qkw"]), (inb[H2:H2 + 1, :], A["inb"]),
                             (colg[:], A["cols"]), (mowT[:], A["mowT"]), (owT[0:H2], A["owT"]), (owT[H2:H2 + 1, 1, :], A["ob"])):
                sp.dma_start(dst, src).then_inc(w_ld2, 16)

            def load_x(i, b):
                if b < 2:
                    sp.dma_start(xm[:, b].rearrange("p a c n -> p a (c n)"), A["xm"][bass.ds(i, 2)].rearrange("a p f -> p a f")).then_inc(x_ld[b], 16)
                else:
                    sp.dma_start(x6[:].rearrange("p a c n -> p (a c n)"), A["x6"][bass.ds(i, 1)].rearrange("a p f -> p (a f)")).then_inc(x_ld[2], 16)

            def load_raw(i, b):
                if b < 2:
                    for src, f0, f1 in (("xwa", 0, 8 * NA), ("xwb", 8 * NA, 8 * NA + 8 * NB)):
                        sp.dma_start(raw[:, f0:f1].rearrange("p (a f) -> p a f", a=2), A[src][bass.ds(i, 2)].rearrange("a p f -> p a f")).then_inc(raw_ld, 16)
                else:
                    for f0, f1 in ((0, 2048), (2048, 3072)):
                        sp.dma_start(raw[:, f0:f1], A["xw6"][bass.ds(i, 1), :, f0:f1].rearrange("a p f -> p (a f)")).then_inc(raw_ld, 16)

            load_x(0, 0)
            load_raw(0, 0)
            sp.wait_ge(wave_set, 1)
            load_raw(0, 2)
            load_x(0, 2)

            def pair(r):
                sp.wait_ge(wave_set, 3 * r + 2)
                load_raw(2 * r + 1, 1)
                sp.wait_ge(tok_mm, 7 * r)
                load_x(2 * r + 1, 1)
                sp.wait_ge(wave_set, 3 * r + 3)
                load_raw(2 * r + 2, 0)
                sp.wait_ge(tok_mm, 7 * r + 3)
                load_x(2 * r + 2, 0)
                sp.wait_ge(tok_mm, 7 * r + 4)
                load_x(r + 1, 2)
                sp.wait_ge(wave_set, 3 * r + 4)
                load_raw(r + 1, 2)

            with sp.Fori(0, 3) as r:
                pair(r)
            sp.wait_ge(bs_set, 25)
            sp.dma_start(base_d[T - 1:T + 1].rearrange("t b d -> (t b) d"), bs[:, 3]).then_inc(bs_st[3], 16)
            if wins:
                wins.sync(sp, bs_st, heads)
            else:
                for n in range(4):
                    sp.wait_ge(bs_st[n], 112)
            if heads:
                heads.sync(sp)

        @block.scalar
        def _(act):
            def squares(u, b, loads, a):
                act.wait_ge(x_ld[b], loads)
                act.wait_ge(sq_free, 2 * u + a + 1)
                src = xm[:, b, a].rearrange("p c n -> p (c n)") if b < 2 else x6[:, 2 * a:2 * a + 2].rearrange("p q c n -> p (q c n)")
                nc.scalar.activation(sqt[:, 0:src.shape[1]], src, ACT.Square).then_inc(sq_half, 1)
                if a == 1:
                    act.wait_ge(wave_set, u + 1)
                    nc.scalar.activation(wsq[:, b] if b < 2 else wsq6[:], wv[:, b] if b < 2 else wv6[:], ACT.Square).then_inc(wsq_set, 1)

            def store(n, pos, r):
                _, _, t0, dt = tile_of(r, pos)
                k = pos % 4
                act.wait_ge(bs_set, n + 1)
                if dt == 1:
                    act.dma_start(base_d[bass.ds(t0, 2)].rearrange("t b d -> (t b) d"), bs[:, k]).then_inc(bs_st[k], 16)
                else:
                    for q in range(2):
                        act.dma_start(base_d[bass.ds(t0 + q * dt, 1)].rearrange("t b d -> (t b) d"),
                                      bs[q * B:(q + 1) * B, k]).then_inc(bs_st[k], 16)

            def put_T(n, pos, r):
                _, _, t0, dt = tile_of(r - 1, 6) if pos == 0 else tile_of(r, pos - 1)
                act.wait_ge(xh_T, n + 1)
                for h in range(2):
                    src = pt1[0:H2, pos % 2, h * P:(h + 1) * P].rearrange("p (t b) -> p t b", t=2)
                    for q in range(1 if dt == 1 else 2):
                        dst = xnT[:, h, bass.ds(FRONT + t0 + q * dt, 3 - dt if dt == 1 else 1), :]
                        last = nc.scalar.activation(dst, src if dt == 1 else src[:, q:q + 1, :], ACT.Identity,
                                                    bias=colg[:, h, 1:2], scale=colg[:, h, 0:1])
                last.then_inc(xh_out, 1)

            act.wait_ge(wm_set, 1)
            act.wait_ge(fold_out, 1)
            squares(0, 0, 16, 0)
            squares(0, 0, 16, 1)
            squares(1, 2, 16, 0)
            with act.Fori(0, 3) as r:
                for pos in range(7):
                    if pos < 3:
                        u, b, loads = UNIT_AT[(pos + 1) // 2]
                        squares(3 * r + u, b, 16 * r + loads, (pos + 1) % 2)
                    if pos in (4, 5):
                        u, b, loads = UNIT_AT[2]
                        squares(3 * r + u, b, 16 * r + loads, pos % 2)
                    if pos == 6:
                        squares(3 * r + 4, 2, 16 * r + 32, 0)
                    put_T(7 * r + pos, pos, r)
                    store(7 * r + pos, pos, r)
            squares(10, 2, 64, 1)
            for pos in range(4):
                put_T(21 + pos, pos, 3)
                if pos < 3:
                    store(21 + pos, pos, 3)
            if wins:
                wins.scalar(act)
            if heads:
                heads.scalar(act)

        @block.gpsimd
        def _(pool):
            nc.gpsimd.memset(ones[:], 1.0).then_inc(ones_set, 1)
            nc.gpsimd.memset(xh[:, 2], 0.0).then_inc(ones_set, 1)

            def add_squares(u, b, a):
                pool.wait_ge(sq_half, 2 * u + a + 1)
                if b < 2:
                    dst = sqs[:, b, a]
                    src = [sqt[:, c * NA:(c + 1) * NA] for c in range(KC)]
                else:
                    dst = sq6[:, 2 * a:2 * a + 2]
                    halves = sqt[:, 0:2 * KC * P].rearrange("p (q c n) -> p q c n", q=2, c=KC)
                    src = [halves[:, :, c] for c in range(KC)]
                nc.gpsimd.tensor_tensor(dst, src[0], src[1], ALU.add)
                for c in range(2, KC):
                    pool.drain()
                    last = nc.gpsimd.tensor_tensor(dst, dst, src[c], ALU.add)
                last.then_inc(sq_free, 1)
                if a == 1:
                    pool.drain().then_inc(sqs_set, 1)

            def roots(n):
                pool.wait_ge(var_set, n + 1)
                nc.gpsimd.tensor_tensor(st1[:, 12:14], st1[:, 4:6], minus_half(2), ALU.pow).then_inc(var_r, 1)
                pool.wait_ge(hvar_set, n + 1)
                nc.gpsimd.tensor_tensor(st1[:, 10:11], st1[:, 9:10], eps_col, ALU.add)
                pool.drain()
                nc.gpsimd.tensor_tensor(st1[:, 10:11], st1[:, 10:11], minus_half(1), ALU.pow)
                pool.drain()
                nc.gpsimd.tensor_tensor(st1[:, 11:12], st1[:, 9:10], st1[:, 10:11], ALU.mult)
                pool.drain()
                nc.gpsimd.tensor_tensor(st1[:, 11:12], st1[:, 11:12], st1[:, 10:11], ALU.mult)
                pool.drain()
                nc.gpsimd.tensor_tensor(st1[:, 11:12], st1[:, 11:12], eps_col, ALU.add)
                pool.drain()
                nc.gpsimd.tensor_tensor(st1[:, 11:12], st1[:, 11:12], minus_half(1), ALU.pow).then_inc(hvar_r, 1)

            pool.wait_ge(c_ld, 16)
            nc.gpsimd.memset(st1[0:1, 20:21], 0.0).then_inc(sq_free, 1)
            add_squares(0, 0, 0)
            add_squares(0, 0, 1)
            with pool.Fori(0, 3) as r:
                for pos in range(7):
                    if pos < 6:
                        u, b, _ = UNIT_AT[pos // 2]
                        pool.wait_ge(tok_mm, 7 * r + (0, 0, 3)[pos // 2])
                        add_squares(3 * r + u, b, pos % 2)
                    roots(7 * r + pos)
            pool.wait_ge(tok_mm, 18)
            add_squares(10, 2, 0)
            add_squares(10, 2, 1)
            for pos in range(4):
                roots(21 + pos)
            if wins:
                wins.gpsimd(pool)
            if heads:
                heads.gpsimd(pool)

        @block.vector
        def _(dve):
            v = nc.vector
            v.memset(st1[0:1, 21:22], 0.0).then_inc(tok_free, 3)
            dve.wait_ge(c_ld, 16)
            dve.wait_ge(gb_ld, 16)
            g5 = gb[:, 0, 0:30].rearrange("p (s c) -> p s c", s=5).unsqueeze(3)
            dve.wait_ge(w1_ld[4], 16)
            v.tensor_tensor(cw1, w1[:, 4], g5[:, 4].to_broadcast([P, KC, D]), ALU.mult)
            for q in range(4):
                dve.wait_ge(w1_ld[q], 16)
                v.tensor_tensor(wm[:, q, :, 0:D], w1[:, q], g5[:, q].to_broadcast([P, KC, D]), ALU.mult)
                dve.drain()
                v.scalar_tensor_tensor(wm[:, q, :, 0:D], cw1, const[:, C_MK + q:C_MK + q + 1], wm[:, q, :, 0:D], ALU.mult, ALU.add)
                v.tensor_scalar(wm[:, q, :, D:D + 1], const[:, C_MK + q:C_MK + q + 1].unsqueeze(1).to_broadcast([P, KC, 1]), 1.0, None, ALU.add)
            dve.wait_ge(w_ld, 16 * 2)
            v.tensor_tensor(cw2, w2[:, 6:8], gb[:, 0, 36:38].unsqueeze(2).to_broadcast([P, 2, D]), ALU.mult)
            v.tensor_tensor(ww[:, :, 0:D], w2[:, 0:6], gb[:, 0, 30:36].unsqueeze(2).to_broadcast([P, 6, D]), ALU.mult)
            dve.drain()
            for q in range(6):
                v.scalar_tensor_tensor(ww[:, q, 0:D], cw2[:, q // 4], const[:, C_MK + 4 + q:C_MK + 5 + q], ww[:, q, 0:D], ALU.mult, ALU.add)
            v.tensor_scalar(ww[:, :, D:D + 1], const[:, C_MK + 4:C_MK + 10].unsqueeze(2), 1.0, None, ALU.add)
            dve.drain().then_inc(wm_set, 1)
            dve.wait_ge(sum_mm, 1)
            v.tensor_copy(sums[:, 0], pp[0:2, 0, 0:D])
            v.tensor_copy(sums[:, 1], pp[0:2, 1, 0:D])
            dve.drain().then_inc(sums_set, 1)
            dve.wait_ge(fold_mm, 1)
            dve.wait_ge(w_ld2, 16 * 7)
            for h in range(2):
                v.tensor_copy(wqkv[0:H2, h, 0:2 * D], pe1[0:H2, 2 * h, 0:2 * D])
                v.tensor_copy(wqkv[0:H2, h, 2 * D:3 * D], pe1[0:H2, 2 * h + 1, 0:D])
            v.tensor_tensor(wqkv[H2:H2 + 1, 1, 0:2 * D], pt1[H2:H2 + 1, 0, 0:2 * D], inb[H2:H2 + 1, 0:2 * D], ALU.add)
            v.tensor_tensor(wqkv[H2:H2 + 1, 1, 2 * D:3 * D], pt1[H2:H2 + 1, 1, 0:D], inb[H2:H2 + 1, 2 * D:3 * D], ALU.add)
            dve.wait_ge(bias_mm, 1)
            v.tensor_copy(cb[:], pp[:, 0, 256:256 + D])
            v.tensor_copy(s1b[:], pp[:, 1, 0:D])
            v.tensor_copy(s2b[:], pp[:, 1, 256:256 + D])
            dve.drain().then_inc(fold_out, 1)

            def waves(u, b):
                dve.wait_ge(raw_ld, 32 * u + 32)
                parts = ((2, NA), (2, NB)) if b < 2 else ((4, P), (2, P))
                f0 = w0 = 0
                for rows, n in parts:
                    src = raw[:, f0:f0 + 4 * rows * n].rearrange("p (a k n) -> p a k n", a=rows, k=4)
                    w = (wv[:, b] if b < 2 else wv6[:])[:, w0:w0 + rows * n].rearrange("p (a n) -> p a n", a=rows)
                    v.tensor_tensor(w, src[:, :, 1], src[:, :, 2], ALU.add)
                    dve.drain()
                    v.tensor_tensor(w, w, src[:, :, 3], ALU.add)
                    dve.drain()
                    v.scalar_tensor_tensor(w, src[:, :, 0], 3.0, w, ALU.mult, ALU.subtract)
                    f0, w0 = f0 + 4 * rows * n, w0 + rows * n
                dve.drain().then_inc(wave_set, 1)

            def post(n, k, stored, on_var=None, on_hvar=None):
                dve.wait_ge(tok_mm, n + 1)
                y = pe1[:, k]
                stat = y.rearrange("p (a c) -> p a c", a=2)[:, :, D:D + 2]
                m = st1[:, 0:4].rearrange("p (a c) -> p a c", a=2)
                mean, e2 = m[:, :, 0], m[:, :, 1]
                v.tensor_tensor(m, stat, const[:, C_INV:C_INV + 4].rearrange("p (a c) -> p a c", a=2), ALU.mult)
                dve.drain()
                v.tensor_tensor(st1[:, 4:6], mean, mean, ALU.mult)
                dve.drain()
                v.tensor_tensor(st1[:, 4:6], e2, st1[:, 4:6], ALU.subtract)
                dve.drain()
                v.tensor_scalar(st1[:, 4:6], st1[:, 4:6], 0.0, EPS, ALU.max, ALU.add).then_inc(var_set, 1)
                if on_var:
                    on_var(dve)
                dve.wait_ge(var_r, n + 1)
                v.scalar_tensor_tensor(st1[:, 6:8], mean, -1.0, st1[:, 12:14], ALU.mult, ALU.mult)
                v.tensor_tensor(st1[:, 4:6], st1[:, 12:14], const[:, C_SIX:C_SIX + 2], ALU.mult)
                dve.drain()
                v.scalar_tensor_tensor(hh[:], s1b[:], st1[:, 6:7], cb[:], ALU.mult, ALU.add)
                dve.drain()
                v.scalar_tensor_tensor(hh[:], s2b[:], st1[:, 7:8], hh[:], ALU.mult, ALU.add)
                dve.drain()
                v.scalar_tensor_tensor(hh[:], y[:, 0:D], st1[:, 4:5], hh[:], ALU.mult, ALU.add)
                dve.drain()
                v.scalar_tensor_tensor(hh[:], y[:, 256:256 + D], st1[:, 5:6], hh[:], ALU.mult, ALU.add).then_inc(tok_free, 1)
                dve.drain()
                v.bn_stats(bn1[:], hh[:])
                dve.drain()
                v.bn_aggr(st1[:, 8:10], bn1[:]).then_inc(hvar_set, 1)
                if on_hvar:
                    on_hvar(dve, range(1))
                dve.wait_ge(hvar_r, n + 1)
                dve.wait_ge(xh_T, n)
                dve.wait_ge(bs_st[k], stored)
                v.tensor_scalar(xh[:, k], hh[:], st1[:, 8:9], st1[:, 10:11], ALU.subtract, ALU.mult)
                dve.drain()
                v.tensor_tensor(bs[:, k], hh[:], xh[:, k], ALU.add).then_inc(bs_set, 1)
                v.tensor_scalar(xh[:, k], xh[:, k], st1[:, 11:12], None, ALU.mult).then_inc(xh_set, 1)
                dve.drain()

            waves(0, 0)
            with dve.Fori(0, 3) as r:
                for pos in range(7):
                    if pos in (0, 2, 4):
                        u, b, _ = UNIT_AT[pos // 2]
                        dve.wait_ge(tok_mm, 7 * r + (0, 0, 3)[pos // 2])
                        waves(3 * r + u, b)
                    post(7 * r + pos, pos % 4, 32 * r + (16 if pos >= 4 else 0))
            waves(10, 2)
            for pos in range(4):
                early = wins and pos == 3
                post(21 + pos, pos, 96, early and wins.set_ones_row, early and wins.pool_tokens)
            if wins:
                wins.vector(dve)
            if heads:
                heads.vector(dve)

        @block.tensor
        def _(pe):
            mm = nc.tensor.matmul
            pe.wait_ge(ones_set, 2)
            pe.wait_ge(gb_ld, 16)
            for s in (4, 0, 1, 2, 3):
                pe.wait_ge(w1_ld[s], 16)
                for c in range(KC):
                    mm(pp[0:2, 0, 0:D], gb[:, :, s * KC + c], w1[:, s, c], start=(s == 4 and c == 0), stop=(s == 3 and c == KC - 1))
            pe.wait_ge(w_ld, 16 * 2)
            for n in range(8):
                k = 64 if n == 7 else P
                last = mm(pp[0:2, 1, 0:D], gb[0:k, :, 30 + n], w2[0:k, n], start=(n == 0), stop=(n == 7))
            last.then_inc(sum_mm, 1)
            pe.wait_ge(w_ld2, 16 * 7)
            for h in range(2):
                for g in range(3):
                    dst = pe1[0:H2, 2 * h + g // 2, (g % 2) * D:(g % 2) * D + D]
                    for m in range(2):
                        mm(dst, qkw[:, m, g, h * H2:(h + 1) * H2], inw[:, m, g], start=(m == 0), stop=(m == 1))
            for g in range(3):
                for m in range(2):
                    dst = pt1[H2:H2 + 1, g // 2, (g % 2) * D:(g % 2) * D + D]
                    last = mm(dst, qkw[:, m, g, D:D + 1], inw[:, m, g], start=(m == 0), stop=(m == 1))
            last.then_inc(fold_mm, 1)
            pe.wait_ge(sums_set, 1)
            row = [ident[0:2, n:n + 1].to_broadcast([2, P]) for n in range(2)]
            mm(pp[:, 0, 256:256 + D], row[1], sums[:, 0], start=True, stop=False)
            mm(pp[:, 0, 256:256 + D], row[1], sums[:, 1], start=False, stop=False)
            for n in range(2):
                mm(pp[:, 0, 256:256 + D], ones[0:1, :], trow[0:1, n], start=False, stop=(n == 1))
            mm(pp[:, 1, 0:D], row[0], sums[:, 0], start=True, stop=True)
            mm(pp[:, 1, 256:256 + D], row[0], sums[:, 1], start=True, stop=True).then_inc(bias_mm, 1)
            pe.wait_ge(fold_out, 1)

            def tokens(n, b, j0, k, unit):
                pe.wait_ge(tok_free, n + 1)
                y = pe1[:, k]

                def cell(q, c):
                    if b == 2:
                        return x6[:, q, c]
                    n0 = (j0 + q % 2) * B
                    return xm[:, b, q // 2, c, n0:n0 + P]

                def cell_squares(q):
                    if b == 2:
                        return sq6[:, q]
                    n0 = (j0 + q % 2) * B
                    return sqs[:, b, q // 2, n0:n0 + P]

                def wave(rows, col, q):
                    if b == 2:
                        return col[:, q * P:(q + 1) * P]
                    n0 = (q // 2) * NA + (j0 + q % 2) * B if q < 4 else 2 * NA + (q - 4) * NB + j0 * B
                    return rows[:, b, n0:n0 + P]

                if unit:
                    pe.wait_ge(x_ld[b], unit[1])
                for q in range(4):
                    for c in range(KC):
                        mm(y[:, 0:D + 1], cell(q, c), wm[:, q, c], start=(q + c == 0), stop=(q == 3 and c == KC - 1))
                if unit:
                    pe.wait_ge(wave_set, unit[0] + 1)
                for q in range(6):
                    mm(y[:, 256:256 + D + 1], wave(wv, wv6, q), ww[:, q], start=(q == 0), stop=(q == 5))
                if unit:
                    pe.wait_ge(wsq_set, unit[0] + 1)
                for q in range(6):
                    mm(y[:, 256 + D + 1:256 + D + 2], wave(wsq, wsq6, q), ww[:, q, D:D + 1], start=(q == 0), stop=(q == 5))
                if unit:
                    pe.wait_ge(sqs_set, unit[0] + 1)
                for q in range(4):
                    last = mm(y[:, D + 1:D + 2], cell_squares(q), wm[:, q, 0, D:D + 1], start=(q == 0), stop=(q == 3))
                last.then_inc(tok_mm, 1)

            def transpose(n, pos):
                pe.wait_ge(xh_set, n)
                pe.wait_ge(xh_out, n)
                for h in range(2):
                    last = nc.tensor.transpose(pt1[0:H2, pos % 2, h * P:(h + 1) * P],
                                               xh[:, before(pos), h * H2:(h + 1) * H2], ident)
                last.then_inc(xh_T, 1)

            with pe.Fori(0, 3) as r:
                for pos in range(7):
                    unit = {0: (3 * r, 16 * r + 16), 3: (3 * r + 1, 16 * r + 16), 4: (3 * r + 2, 16 * r + 16)}.get(pos)
                    tokens(7 * r + pos, 0 if pos < 3 else 2 if pos == 3 else 1, tile_of(0, pos)[1], pos % 4, unit)
                    transpose(7 * r + pos, pos)
            for pos in range(4):
                tokens(21 + pos, 0 if pos < 3 else 2, tile_of(3, pos)[1], pos, {0: (9, 64), 3: (10, 64)}.get(pos))
                transpose(21 + pos, pos)
            if wins:
                wins.tensor(pe)
            if heads:
                heads.tensor(pe)


def lay_out(inputs):
    import numpy as np

    f = {k: np.asarray(v) for k, v in inputs.items()}
    g = {}
    x = f["x"]
    pad = np.zeros((B, CH, NC * CELL, NC * CELL), x.dtype)
    pad[:, :, CELL // 2:CELL // 2 + 112, CELL // 2:CELL // 2 + 112] = x
    m = pad.reshape(B, CH, NC, 2, 8, NC, 2, 4, 2)
    m = m.transpose(2, 5, 3, 6, 4, 7, 8, 1, 0).reshape(NC, NC, P, KC, B)
    rows = np.ascontiguousarray(m.transpose(0, 2, 3, 1, 4))
    g["xm"] = np.ascontiguousarray(rows[:, :, :, :7]).reshape(NC, P, KC * NA)
    w = pad.reshape(B, CH, NC, 2, 4, 2, NC, 2, 4, 2)
    w = w.transpose(2, 6, 3, 7, 4, 8, 1, 5, 9, 0).reshape(NC, NC, D, 4, B)
    w = np.ascontiguousarray(w.transpose(0, 2, 3, 1, 4))
    low = w[:, P:]
    both = np.concatenate([low[:, :, :, 0:NC - 1], low[:, :, :, 1:NC]], 1)
    g["xwa"] = np.ascontiguousarray(w[:, :P, :, :7]).reshape(NC, P, 4 * NA)
    g["xwb"] = np.ascontiguousarray(both[:, :, :, :6]).reshape(NC, P, 4 * NB)
    x6, xw6 = [], []
    for r in range(4):
        i = [2 * r, min(2 * r + 1, G - 1)]
        x6.append(np.stack([np.stack([rows[k + a, :, :, 6 + b] for k in i], 2) for a in range(2) for b in range(2)], 1).reshape(P, -1))
        wa = np.stack([np.stack([w[k + a, :P, :, 6 + b] for k in i], 2) for a in range(2) for b in range(2)], 1).reshape(P, -1)
        wb = np.stack([np.stack([both[k + a, :, :, 6] for k in i], 2) for a in range(2)], 1).reshape(P, -1)
        xw6.append(np.concatenate([wa, wb], 1))
    g["x6"], g["xw6"] = np.stack(x6), np.stack(xw6)

    def main_rows(a):
        n = a.shape[1]
        a = a.reshape(16, 16, 5, CH, n)
        out = []
        for s in (1, 2, 3, 4, 0):
            t = a[:, :, s]
            if s == 0:
                t = np.roll(t, (8, 8), (0, 1))
            t = t.reshape(2, 8, 2, 4, 2, CH, n).transpose(0, 2, 1, 3, 4, 5, 6)
            out.append(t.reshape(P, KC, n))
        return np.ascontiguousarray(np.stack(out, 1))

    def wave_rows(a):
        n = a.shape[1]
        a = a.reshape(8, 8, 5, CH, n)
        r = []
        for s in (1, 2, 3, 4, 0):
            t = a[:, :, s]
            if s == 0:
                t = np.roll(t, (4, 4), (0, 1))
            r.append(t.reshape(2, 4, 2, 4, CH, n).transpose(0, 2, 1, 3, 4, 5).reshape(D, n))
        out = [r[q][:P] for q in range(4)]
        out += [np.concatenate([r[0][P:], r[1][P:]]), np.concatenate([r[2][P:], r[3][P:]])]
        out += [r[4][:P], np.concatenate([r[4][P:], r[4][P:]])]
        return np.ascontiguousarray(np.stack(out, 1))

    g["w1"] = main_rows(f["L0_tok_w1"])
    g["w2"] = wave_rows(f["L0_tok_w2"])
    gb = np.zeros((P, 2, 38), np.float32)
    for n, (a, b) in enumerate((("L0_tok_ln1_g", "L0_tok_ln2_g"), ("L0_tok_ln1_b", "L0_tok_ln2_b"))):
        gb[:, n, 0:30] = main_rows(f[a][:, None]).reshape(P, 30)
        gb[:, n, 30:] = wave_rows(f[b][:, None]).reshape(P, 8)
    g["gb"] = gb
    g["tok_b"] = np.stack([f["L0_tok_b1"], f["L0_tok_b2"]])[None]

    def halves(a):
        return np.ascontiguousarray(a.reshape(2, H2, -1).transpose(1, 0, 2))

    g["inw"] = halves(f["L0_attn_inw"].T).reshape(H2, 2, 3, D)
    qk = [halves(np.concatenate([f[f"L0_attn_{c}w"], f[f"L0_attn_{c}b"][:, None]], 1)) for c in "qkv"]
    g["qkw"] = np.ascontiguousarray(np.stack(qk, 2))
    g["inb"] = f["L0_attn_inb"][None]
    cols = [f[n][:, None] for n in ("L0_attn_ln_g", "L0_attn_ln_b", "L0_attn_mob", "L0_ffn_norm1_w", "L0_ffn_norm1_b")]
    g["cols"] = halves(np.concatenate(cols, 1))
    g["mowT"] = halves(f["L0_attn_mow"].T)
    g["owT"] = halves(f["L0_attn_ow"].T)
    g["ob"] = f["L0_attn_ob"][None]
    g["qkvT"] = halves(f["L0_ffn_qkv_w"].T)
    g["qkvb"] = f["L0_ffn_qkv_b"][None]
    g["projT"] = halves(f["L0_ffn_proj_w"].T)
    g["projb"] = f["L0_ffn_proj_b"][None]
    g["n2"] = np.stack([f["L0_ffn_norm2_w"], f["L0_ffn_norm2_b"]])
    g["wgate"] = halves(f["L0_ffn_w_gate"])
    g["W1"] = np.ascontiguousarray(f["L0_ffn_W1"].reshape(E, 2, H2, HID).transpose(0, 2, 1, 3))
    g["b1"] = np.ascontiguousarray(f["L0_ffn_b1"].reshape(E, HC, P).transpose(0, 2, 1))
    g["W2"] = np.ascontiguousarray(f["L0_ffn_W2"].reshape(E, HC, P, D).transpose(0, 2, 1, 3))
    g["b2"] = f["L0_ffn_b2"]

    c = np.zeros((P, NCONST), np.float32)
    c[:, C_ID:C_ID + P] = np.eye(P)
    p = np.arange(P)
    for q in range(4):
        c[:, C_MK + q] = p // 32 == 3 - q
        c[:, C_MK + 4 + q] = p // 48 == 3 - q
    for a in range(2):
        quad = (P + p % 64) // 48
        c[:, C_MK + 8 + a] = quad == 3 - 2 * a - p // 64
    c[:, C_INV:C_INV + 4] = [1 / PATCH, 1 / PATCH, 1 / (6 * WAVE), 1 / (36 * WAVE)]
    c[:, C_SIX:C_SIX + 2] = [1, 1 / 6]
    for h in range(6):
        c[:, C_KM + h] = p // AHD == h
    c[:, C_NH:C_NH + 2] = -0.5
    c[:, C_EPS:C_EPS + 2] = EPS
    c[:, C_EI:C_EI + E] = np.arange(E)
    real = (p % B) < T
    c[:, C_VAL] = real
    c[:, C_VAL + 1] = np.where(real, 0, FAR)
    c[:, C_ER:C_ER + E] = np.arange(E) * R
    c[:, C_J:C_J + NT] = np.arange(NT)
    c[:, C_L8:C_L8 + E * E] = (np.arange(E)[:, None] >= np.arange(E)[None]).reshape(-1)
    c[:, C_TRI:C_TRI + P] = p[:, None] < p[None]
    c[:, C_ROW:] = (2 * (P * np.arange(NP)[None, :, None] + p[:, None, None]) + np.arange(2)).reshape(P, -1)
    g["consts"] = c
    return g


def kernel(**inputs):
    import numpy as np
    import concourse.bacc as bacc
    from concourse.bass_utils import run_bass_kernel_spmd

    nc = bacc.Bacc("TRN2", target_bir_lowering=False, num_devices=1)
    arrays = lay_out(inputs)
    aps = {n: nc.dram_tensor(f"in_{n}", a.shape, mybir.dt.from_np(a.dtype), kind="ExternalInput").ap() for n, a in arrays.items()}
    out = nc.dram_tensor("out", (B, T, D), F32, kind="ExternalOutput").ap()
    build(nc, aps, out)
    r = run_bass_kernel_spmd(nc, [{f"in_{n}": a for n, a in arrays.items()}], core_ids=[0])
    return r.results[0]["out"]
```
